# Optimizing a Trainium2 kernel written in Bass

```python
import numpy as np
import jax
import jax.numpy as jnp

def _softmax(x, axis=-1):
    return jax.nn.softmax(x, axis=axis)

def _gelu(x):
    return jax.nn.gelu(x, approximate=True)

def _silu(x):
    return jax.nn.silu(x)

def _sigmoid(x):
    return jax.nn.sigmoid(x)

def _layernorm(x, axis=-1, eps=1e-05):
    m = jnp.mean(x, axis=axis, keepdims=True)
    v = jnp.var(x, axis=axis, keepdims=True)
    return (x - m) / jnp.sqrt(v + eps)

def _scatter_add(tgt, idx, src, axis=0):
    return tgt.at[idx].add(src)

def _segment_sum(src, seg, n):
    return jax.ops.segment_sum(src, seg, n)
kernel_name = 'mk_xattn_ffn_d4_seqx_r4_199704'

def setup_inputs(seed: int=0):
    np.random.seed(seed)
    _w = jnp.asarray

    def _rec_inputs():
        import jax
        import jax.numpy as jnp
        _rk = jax.random.key(seed)
        x = -0.0002928 + 1 * jax.random.normal(jax.random.fold_in(_rk, 1), (8, 112, 512), jnp.float32)
        _lenS = 112 - jax.random.randint(jax.random.fold_in(_rk, 7), (8,), 0, max(1, 112 // 4) + 1, jnp.int32)
        _lenS2 = 375 - jax.random.randint(jax.random.fold_in(_rk, 8), (8,), 0, max(1, 375 // 4) + 1, jnp.int32)
        _ctx_512P = jax.random.normal(jax.random.fold_in(_rk, 11), (8, 16, 128), jnp.float32)
        _ctx_512c = jax.random.dirichlet(jax.random.fold_in(_rk, 511), 0.3 * jnp.ones((16,), jnp.float32), (8, 375))
        _ctx_512t = jnp.einsum('bsk,bkd->bsd', _ctx_512c, _ctx_512P)
        _ctx_512t = _ctx_512t * jax.lax.rsqrt(jnp.mean(jnp.square(_ctx_512t)) + 1e-12) * 0.953939
        ctx_512 = 0.000227908 + 0.99994 * (_ctx_512t + 0.3 * jax.random.normal(jax.random.fold_in(_rk, 611), (8, 375, 128), jnp.float32))
        return (x, ctx_512)
    x, ctx_512 = _rec_inputs()

    def _L0_xattn_setup():
        import jax, jax.numpy as jnp
        import numpy as np
        B, S, L = (2, 256, 256)
        DIM_Q, H, K, D_C, D_CQ, R = (512, 16, 128, 128, 384, 64)

        def _rope_tables(length, dim):
            inv = 1.0 / 10000.0 ** (jnp.arange(0, dim, 2, dtype=jnp.float32) / dim)
            f = jnp.arange(length, dtype=jnp.float32)[:, None] * inv[None, :]
            sin = jnp.repeat(jnp.sin(f), 2, axis=-1)
            cos = jnp.repeat(jnp.cos(f), 2, axis=-1)
            return (sin, cos)

        def _rotate_half(x):
            half = x.shape[-1] // 2
            return jnp.concatenate([-x[..., half:], x[..., :half]], axis=-1)

        def _apply_rope(x, sin, cos):
            return x * cos + _rotate_half(x) * sin
        key = jax.random.key(seed)
        ks = jax.random.split(key, 8)
        return {'hidden_q': jax.random.normal(ks[0], (B, S, DIM_Q), jnp.float32), 'kv_c': jax.random.normal(ks[1], (B, L, D_C), jnp.float32), 'Wq': jax.random.normal(ks[2], (H * K, DIM_Q), jnp.float32) / np.sqrt(DIM_Q).astype(np.float32), 'w_kc_q': jax.random.normal(ks[3], (H, K, D_CQ), jnp.float32) / np.sqrt(K).astype(np.float32), 'w_kc_kv': jax.random.normal(ks[4], (H, K, D_C), jnp.float32) / np.sqrt(K).astype(np.float32), 'W_qr': jax.random.normal(ks[5], (H, D_CQ, R), jnp.float32) / np.float32(np.sqrt(D_CQ) * np.sqrt(R)), 'W_kr': jax.random.normal(ks[6], (H, D_C, R), jnp.float32) / np.sqrt(D_C).astype(np.float32), 'Wo': jax.random.normal(ks[7], (DIM_Q, H * K), jnp.float32) / np.sqrt(H * K).astype(np.float32)}
    _L0_xattn_all = _L0_xattn_setup()
    _L0_xattn_in = {k: v for k, v in _L0_xattn_all.items() if k in ('Wq', 'w_kc_q', 'w_kc_kv', 'W_qr', 'W_kr', 'Wo')}
    del _L0_xattn_all

    def _L0_ffn_setup():
        import jax, jax.numpy as jnp
        import numpy as np
        B, S, H = (2, 256, 512)
        E, K, F = (8, 2, 352)
        N_SHARED = 2
        FS = F * N_SHARED
        ROUTED_SCALE = 1.0

        def _swiglu_mlp(x, wg, wu, wd):
            return jax.nn.silu(x @ wg.T) * (x @ wu.T) @ wd.T
        key = jax.random.key(seed)
        ks = jax.random.split(key, 8)

        def w(k, shape, fan_in):
            return jax.random.normal(k, shape, jnp.float32) * (1.0 / np.sqrt(fan_in))
        return {'hidden_states': jax.random.normal(ks[0], (B, S, H), jnp.float32), 'gate_weight': w(ks[1], (E, H), H), 'w_gate': w(ks[2], (E, F, H), H), 'w_up': w(ks[3], (E, F, H), H), 'w_down': w(ks[4], (E, H, F), F), 'sw_gate': w(ks[5], (FS, H), H), 'sw_up': w(ks[6], (FS, H), H), 'sw_down': w(ks[7], (H, FS), FS)}
    _L0_ffn_all = _L0_ffn_setup()
    _L0_ffn_in = {k: v for k, v in _L0_ffn_all.items() if k in ('gate_weight', 'w_gate', 'w_up', 'w_down', 'sw_gate', 'sw_up', 'sw_down')}
    del _L0_ffn_all

    def _L1_xattn_setup():
        import jax, jax.numpy as jnp
        import numpy as np
        B, S, H, NH, L = (2, 512, 512, 16, 128)
        HD = H // NH
        key = jax.random.key(seed)
        k1, k2, k3, k4, k5 = jax.random.split(key, 5)
        scale = 0.02
        return {'q': jax.random.normal(k1, (B, S, H), dtype=jnp.float32), 'latent_kv': jax.random.normal(k2, (B, S, L), dtype=jnp.float32), 'Wq': jax.random.normal(k3, (H, H), dtype=jnp.float32) * scale, 'Wkv_expand': jax.random.normal(k4, (2 * H, L), dtype=jnp.float32) * scale, 'Wout': jax.random.normal(k5, (H, H), dtype=jnp.float32) * scale}
    _L1_xattn_all = _L1_xattn_setup()
    _L1_xattn_in = {k: v for k, v in _L1_xattn_all.items() if k in ('Wq', 'Wkv_expand', 'Wout')}
    del _L1_xattn_all

    def _L1_ffn_setup():
        import jax, jax.numpy as jnp
        import numpy as np

        @jax.custom_vjp
        def ste_sign(x):
            return jnp.sign(x)

        def _ste_fwd(x):
            return (jnp.sign(x), None)

        def _ste_bwd(_, g):
            return (g,)
        ste_sign.defvjp(_ste_fwd, _ste_bwd)
        D_MODEL = 512
        D_HIDDEN = 2048
        key = jax.random.key(seed)
        k_x, k_up, k_dn = jax.random.split(key, 3)
        x = jax.random.normal(k_x, (2, 512, D_MODEL), dtype=jnp.float32)
        up_weight = jax.random.normal(k_up, (D_HIDDEN, D_MODEL), dtype=jnp.float32) * 0.02
        down_weight = jax.random.normal(k_dn, (D_MODEL, D_HIDDEN), dtype=jnp.float32) * 0.02
        up_scale = jnp.ones((D_HIDDEN,), dtype=jnp.float32)
        down_scale = jnp.ones((D_MODEL,), dtype=jnp.float32)
        output_scale = jnp.ones((1,), dtype=jnp.float32)
        return {'x': x, 'up_weight': up_weight, 'down_weight': down_weight, 'up_scale': up_scale, 'down_scale': down_scale, 'output_scale': output_scale}
    _L1_ffn_all = _L1_ffn_setup()
    _L1_ffn_in = {k: v for k, v in _L1_ffn_all.items() if k in ('up_weight', 'down_weight', 'up_scale', 'down_scale', 'output_scale')}
    del _L1_ffn_all

    def _L2_xattn_setup():
        import jax, jax.numpy as jnp
        import numpy as np
        B, S, L = (2, 256, 256)
        DIM_Q, H, K, D_C, D_CQ, R = (512, 16, 128, 128, 384, 64)

        def _rope_tables(seq_len, dim, dtype):
            inv_freq = 1.0 / 10000.0 ** (jnp.arange(0, dim, 2, dtype=dtype) / dim)
            t = jnp.arange(seq_len, dtype=dtype)
            freqs = t[:, None] * inv_freq[None, :]
            sin = jnp.repeat(jnp.sin(freqs), 2, axis=-1)
            cos = jnp.repeat(jnp.cos(freqs), 2, axis=-1)
            return (sin, cos)

        def _rotate_half(x):
            h = x.shape[-1] // 2
            return jnp.concatenate([-x[..., h:], x[..., :h]], axis=-1)
        key = jax.random.key(seed)
        ks = jax.random.split(key, 8)
        s_in = 1.0 / np.sqrt(DIM_Q)
        s_k = 1.0 / np.sqrt(K)
        s_cq = 1.0 / np.sqrt(D_CQ)
        s_c = 1.0 / np.sqrt(D_C)
        return {'hidden_q': jax.random.normal(ks[0], (B, S, DIM_Q), jnp.float32), 'kv_c': jax.random.normal(ks[1], (B, L, D_C), jnp.float32), 'Wq': jax.random.normal(ks[2], (H * K, DIM_Q), jnp.float32) * s_in, 'w_kc_q': jax.random.normal(ks[3], (H, K, D_CQ), jnp.float32) * s_k, 'w_kc_kv': jax.random.normal(ks[4], (H, K, D_C), jnp.float32) * s_k, 'W_qr': jax.random.normal(ks[5], (H, D_CQ, R), jnp.float32) * s_cq / np.sqrt(R), 'W_kr': jax.random.normal(ks[6], (H, D_C, R), jnp.float32) * s_c, 'Wo': jax.random.normal(ks[7], (DIM_Q, H * K), jnp.float32) * s_k}
    _L2_xattn_all = _L2_xattn_setup()
    _L2_xattn_in = {k: v for k, v in _L2_xattn_all.items() if k in ('Wq', 'w_kc_q', 'w_kc_kv', 'W_qr', 'W_kr', 'Wo')}
    del _L2_xattn_all

    def _L2_ffn_setup():
        import jax, jax.numpy as jnp
        import numpy as np
        B, S, D_IN, D_OUT = (4, 512, 512, 512)
        EPS = 1e-10
        key = jax.random.key(seed)
        kx, kw, kb = jax.random.split(key, 3)
        x = jax.random.normal(kx, (B, S, D_IN), dtype=jnp.float32)
        weight = jax.random.normal(kw, (D_OUT, D_IN), dtype=jnp.float32) * 0.02
        bias = jax.random.normal(kb, (D_OUT,), dtype=jnp.float32) * 0.02
        return {'x': x, 'weight': weight, 'bias': bias}
    _L2_ffn_all = _L2_ffn_setup()
    _L2_ffn_in = {k: v for k, v in _L2_ffn_all.items() if k in ('weight', 'bias')}
    del _L2_ffn_all

    def _L3_xattn_setup():
        import jax, jax.numpy as jnp
        import numpy as np
        B, S, L = (2, 256, 256)
        DIM_Q, H, K, D_C, D_CQ, R = (512, 16, 128, 128, 384, 64)

        def _rope_tables(length, dim):
            inv = 1.0 / 10000.0 ** (jnp.arange(0, dim, 2, dtype=jnp.float32) / dim)
            f = jnp.arange(length, dtype=jnp.float32)[:, None] * inv[None, :]
            sin = jnp.repeat(jnp.sin(f), 2, axis=-1)
            cos = jnp.repeat(jnp.cos(f), 2, axis=-1)
            return (sin, cos)

        def _rotate_half(x):
            half = x.shape[-1] // 2
            return jnp.concatenate([-x[..., half:], x[..., :half]], axis=-1)

        def _apply_rope(x, sin, cos):
            return x * cos + _rotate_half(x) * sin
        key = jax.random.key(seed)
        ks = jax.random.split(key, 8)
        return {'hidden_q': jax.random.normal(ks[0], (B, S, DIM_Q), jnp.float32), 'kv_c': jax.random.normal(ks[1], (B, L, D_C), jnp.float32), 'Wq': jax.random.normal(ks[2], (H * K, DIM_Q), jnp.float32) / np.sqrt(DIM_Q).astype(np.float32), 'w_kc_q': jax.random.normal(ks[3], (H, K, D_CQ), jnp.float32) / np.sqrt(K).astype(np.float32), 'w_kc_kv': jax.random.normal(ks[4], (H, K, D_C), jnp.float32) / np.sqrt(K).astype(np.float32), 'W_qr': jax.random.normal(ks[5], (H, D_CQ, R), jnp.float32) / np.float32(np.sqrt(D_CQ) * np.sqrt(R)), 'W_kr': jax.random.normal(ks[6], (H, D_C, R), jnp.float32) / np.sqrt(D_C).astype(np.float32), 'Wo': jax.random.normal(ks[7], (DIM_Q, H * K), jnp.float32) / np.sqrt(H * K).astype(np.float32)}
    _L3_xattn_all = _L3_xattn_setup()
    _L3_xattn_in = {k: v for k, v in _L3_xattn_all.items() if k in ('Wq', 'w_kc_q', 'w_kc_kv', 'W_qr', 'W_kr', 'Wo')}
    del _L3_xattn_all

    def _L3_ffn_setup():
        import jax, jax.numpy as jnp
        import numpy as np
        B, S, H = (1, 256, 512)
        F = 256
        E = 16
        K = 2
        NS = 1
        ROUTE_SCALE = 1.0
        key = jax.random.key(seed)
        ks = jax.random.split(key, 8)

        def w(k, shape, fan_in):
            return jax.random.normal(k, shape, jnp.float32) * fan_in ** (-0.5)
        return {'hidden_states': jax.random.normal(ks[0], (B, S, H), jnp.float32), 'gate_w': w(ks[1], (H, E), H), 'expert_bias': jnp.zeros((E,), jnp.float32), 'shared_gate_w': w(ks[2], (H, F * NS), H), 'shared_up_w': w(ks[3], (H, F * NS), H), 'shared_down_w': w(ks[4], (F * NS, H), F * NS), 'experts_gate_up': w(ks[5], (E, H, 2 * F), H), 'experts_down': w(ks[6], (E, F, H), F)}
    _L3_ffn_all = _L3_ffn_setup()
    _L3_ffn_in = {k: v for k, v in _L3_ffn_all.items() if k in ('gate_w', 'expert_bias', 'shared_gate_w', 'shared_up_w', 'shared_down_w', 'experts_gate_up', 'experts_down')}
    del _L3_ffn_all
    return {'x': x, 'ctx_512': ctx_512, 'L0_xattn_Wq': _L0_xattn_in['Wq'], 'L0_xattn_w_kc_q': _L0_xattn_in['w_kc_q'], 'L0_xattn_w_kc_kv': _L0_xattn_in['w_kc_kv'], 'L0_xattn_W_qr': _L0_xattn_in['W_qr'], 'L0_xattn_W_kr': _L0_xattn_in['W_kr'], 'L0_xattn_Wo': _L0_xattn_in['Wo'], 'L0_ffn_gate_weight': _L0_ffn_in['gate_weight'], 'L0_ffn_w_gate': _L0_ffn_in['w_gate'], 'L0_ffn_w_up': _L0_ffn_in['w_up'], 'L0_ffn_w_down': _L0_ffn_in['w_down'], 'L0_ffn_sw_gate': _L0_ffn_in['sw_gate'], 'L0_ffn_sw_up': _L0_ffn_in['sw_up'], 'L0_ffn_sw_down': _L0_ffn_in['sw_down'], 'L1_xattn_Wq': _L1_xattn_in['Wq'], 'L1_xattn_Wkv_expand': _L1_xattn_in['Wkv_expand'], 'L1_xattn_Wout': _L1_xattn_in['Wout'], 'L1_ffn_up_weight': _L1_ffn_in['up_weight'], 'L1_ffn_down_weight': _L1_ffn_in['down_weight'], 'L1_ffn_up_scale': _L1_ffn_in['up_scale'], 'L1_ffn_down_scale': _L1_ffn_in['down_scale'], 'L1_ffn_output_scale': _L1_ffn_in['output_scale'], 'L2_xattn_Wq': _L2_xattn_in['Wq'], 'L2_xattn_w_kc_q': _L2_xattn_in['w_kc_q'], 'L2_xattn_w_kc_kv': _L2_xattn_in['w_kc_kv'], 'L2_xattn_W_qr': _L2_xattn_in['W_qr'], 'L2_xattn_W_kr': _L2_xattn_in['W_kr'], 'L2_xattn_Wo': _L2_xattn_in['Wo'], 'L2_ffn_weight': _L2_ffn_in['weight'], 'L2_ffn_bias': _L2_ffn_in['bias'], 'L3_xattn_Wq': _L3_xattn_in['Wq'], 'L3_xattn_w_kc_q': _L3_xattn_in['w_kc_q'], 'L3_xattn_w_kc_kv': _L3_xattn_in['w_kc_kv'], 'L3_xattn_W_qr': _L3_xattn_in['W_qr'], 'L3_xattn_W_kr': _L3_xattn_in['W_kr'], 'L3_xattn_Wo': _L3_xattn_in['Wo'], 'L3_ffn_gate_w': _L3_ffn_in['gate_w'], 'L3_ffn_expert_bias': _L3_ffn_in['expert_bias'], 'L3_ffn_shared_gate_w': _L3_ffn_in['shared_gate_w'], 'L3_ffn_shared_up_w': _L3_ffn_in['shared_up_w'], 'L3_ffn_shared_down_w': _L3_ffn_in['shared_down_w'], 'L3_ffn_experts_gate_up': _L3_ffn_in['experts_gate_up'], 'L3_ffn_experts_down': _L3_ffn_in['experts_down']}

def reference(x, ctx_512, L0_xattn_Wq, L0_xattn_w_kc_q, L0_xattn_w_kc_kv, L0_xattn_W_qr, L0_xattn_W_kr, L0_xattn_Wo, L0_ffn_gate_weight, L0_ffn_w_gate, L0_ffn_w_up, L0_ffn_w_down, L0_ffn_sw_gate, L0_ffn_sw_up, L0_ffn_sw_down, L1_xattn_Wq, L1_xattn_Wkv_expand, L1_xattn_Wout, L1_ffn_up_weight, L1_ffn_down_weight, L1_ffn_up_scale, L1_ffn_down_scale, L1_ffn_output_scale, L2_xattn_Wq, L2_xattn_w_kc_q, L2_xattn_w_kc_kv, L2_xattn_W_qr, L2_xattn_W_kr, L2_xattn_Wo, L2_ffn_weight, L2_ffn_bias, L3_xattn_Wq, L3_xattn_w_kc_q, L3_xattn_w_kc_kv, L3_xattn_W_qr, L3_xattn_W_kr, L3_xattn_Wo, L3_ffn_gate_w, L3_ffn_expert_bias, L3_ffn_shared_gate_w, L3_ffn_shared_up_w, L3_ffn_shared_down_w, L3_ffn_experts_gate_up, L3_ffn_experts_down):
    import jax
    import jax.numpy as jnp

    def _L0_xattn_ref(hidden_q, kv_c, Wq, w_kc_q, w_kc_kv, W_qr, W_kr, Wo):
        import jax, jax.numpy as jnp
        import numpy as np
        B, S, L = (2, 256, 256)
        DIM_Q, H, K, D_C, D_CQ, R = (512, 16, 128, 128, 384, 64)

        def _rope_tables(length, dim):
            inv = 1.0 / 10000.0 ** (jnp.arange(0, dim, 2, dtype=jnp.float32) / dim)
            f = jnp.arange(length, dtype=jnp.float32)[:, None] * inv[None, :]
            sin = jnp.repeat(jnp.sin(f), 2, axis=-1)
            cos = jnp.repeat(jnp.cos(f), 2, axis=-1)
            return (sin, cos)

        def _rotate_half(x):
            half = x.shape[-1] // 2
            return jnp.concatenate([-x[..., half:], x[..., :half]], axis=-1)

        def _apply_rope(x, sin, cos):
            return x * cos + _rotate_half(x) * sin
        Bv, Sv, _ = hidden_q.shape
        _, Lv, _ = kv_c.shape
        q_hk = (hidden_q @ Wq.T).reshape(Bv, Sv, H, K)
        q_big = jnp.einsum('bshk,hkq->bshq', q_hk, w_kc_q)
        sin_q, cos_q = _rope_tables(Sv, D_CQ)
        q_big = _apply_rope(q_big, sin_q[None, :, None, :], cos_q[None, :, None, :])
        sin_k, cos_k = _rope_tables(Lv, D_C)
        kv_r = _apply_rope(kv_c, sin_k[None], cos_k[None])
        q_r = jnp.einsum('bshq,hqr->bhsr', q_big, W_qr)
        k_r = jnp.einsum('bld,hdr->bhlr', kv_r, W_kr)
        scores = jnp.einsum('bhsr,bhlr->bhsl', q_r, k_r)
        attn = jax.nn.softmax(scores, axis=-1)
        ctx_c = jnp.einsum('bhsl,bld->bhsd', attn, kv_r)
        ctx_lat = jnp.einsum('bhsd,hkd->bhsk', ctx_c, w_kc_kv)
        ctx = ctx_lat.transpose(0, 2, 1, 3).reshape(Bv, Sv, H * K)
        return ctx @ Wo.T

    def _L0_ffn_ref(hidden_states, gate_weight, w_gate, w_up, w_down, sw_gate, sw_up, sw_down):
        import jax, jax.numpy as jnp
        import numpy as np
        B, S, H = (2, 256, 512)
        E, K, F = (8, 2, 352)
        N_SHARED = 2
        FS = F * N_SHARED
        ROUTED_SCALE = 1.0

        def _swiglu_mlp(x, wg, wu, wd):
            return jax.nn.silu(x @ wg.T) * (x @ wu.T) @ wd.T
        b, s, h = hidden_states.shape
        x = hidden_states.reshape(-1, h)
        T = x.shape[0]
        logits = x.astype(jnp.float32) @ gate_weight.astype(jnp.float32).T
        scores = jax.nn.softmax(logits, axis=-1)
        topk_w, topk_idx = jax.lax.top_k(scores, K)
        topk_w = topk_w / (jnp.sum(topk_w, axis=-1, keepdims=True) + 1e-20)
        topk_w = topk_w * ROUTED_SCALE
        cw = jnp.zeros((T, E), jnp.float32).at[jnp.arange(T)[:, None], topk_idx].add(topk_w)
        g = jax.nn.silu(jnp.einsum('th,efh->tef', x, w_gate)) * jnp.einsum('th,efh->tef', x, w_up)
        expert_out = jnp.einsum('tef,ehf->teh', g, w_down)
        y = jnp.einsum('te,teh->th', cw, expert_out).reshape(b, s, h)
        y = y + _swiglu_mlp(x, sw_gate, sw_up, sw_down).reshape(b, s, h)
        return y

    def _L1_xattn_ref(q, latent_kv, Wq, Wkv_expand, Wout):
        import jax, jax.numpy as jnp
        import numpy as np
        B, S, H, NH, L = (2, 512, 512, 16, 128)
        HD = H // NH
        b, sq, _ = q.shape
        sk = latent_kv.shape[1]
        qp = q @ Wq.T
        kv = latent_kv @ Wkv_expand.T
        k, v = jnp.split(kv, 2, axis=-1)
        qh = qp.reshape(b, sq, NH, HD).transpose(0, 2, 1, 3)
        kh = k.reshape(b, sk, NH, HD).transpose(0, 2, 1, 3)
        vh = v.reshape(b, sk, NH, HD).transpose(0, 2, 1, 3)
        inv_sqrt_d = 1.0 / jnp.sqrt(jnp.float32(HD))
        scores = jnp.einsum('bhqd,bhkd->bhqk', qh, kh) * inv_sqrt_d
        causal = jnp.tril(jnp.ones((sq, sk), dtype=bool))
        scores = jnp.where(causal, scores, jnp.finfo(scores.dtype).min)
        attn = jax.nn.softmax(scores, axis=-1)
        out = jnp.einsum('bhqk,bhkd->bhqd', attn, vh)
        out = out.transpose(0, 2, 1, 3).reshape(b, sq, H)
        return out @ Wout.T

    def _L1_ffn_ref(x, up_weight, down_weight, up_scale, down_scale, output_scale):
        import jax, jax.numpy as jnp
        import numpy as np

        @jax.custom_vjp
        def ste_sign(x):
            return jnp.sign(x)

        def _ste_fwd(x):
            return (jnp.sign(x), None)

        def _ste_bwd(_, g):
            return (g,)
        ste_sign.defvjp(_ste_fwd, _ste_bwd)
        D_MODEL = 512
        D_HIDDEN = 2048
        up_w = ste_sign(up_weight)
        down_w = ste_sign(down_weight)
        hidden = jnp.einsum('bsd,hd->bsh', x, up_w) * up_scale
        hidden = jax.nn.relu(hidden)
        out = jnp.einsum('bsh,dh->bsd', hidden, down_w) * down_scale
        return out * output_scale

    def _L2_xattn_ref(hidden_q, kv_c, Wq, w_kc_q, w_kc_kv, W_qr, W_kr, Wo):
        import jax, jax.numpy as jnp
        import numpy as np
        B, S, L = (2, 256, 256)
        DIM_Q, H, K, D_C, D_CQ, R = (512, 16, 128, 128, 384, 64)

        def _rope_tables(seq_len, dim, dtype):
            inv_freq = 1.0 / 10000.0 ** (jnp.arange(0, dim, 2, dtype=dtype) / dim)
            t = jnp.arange(seq_len, dtype=dtype)
            freqs = t[:, None] * inv_freq[None, :]
            sin = jnp.repeat(jnp.sin(freqs), 2, axis=-1)
            cos = jnp.repeat(jnp.cos(freqs), 2, axis=-1)
            return (sin, cos)

        def _rotate_half(x):
            h = x.shape[-1] // 2
            return jnp.concatenate([-x[..., h:], x[..., :h]], axis=-1)
        b, s, _ = hidden_q.shape
        l = kv_c.shape[1]
        q_hk = (hidden_q @ Wq.T).reshape(b, s, H, K)
        q_big = jnp.einsum('bshk,hkq->bshq', q_hk, w_kc_q)
        sin, cos = _rope_tables(l, D_C, kv_c.dtype)
        kv_rope = kv_c * cos[None] + _rotate_half(kv_c) * sin[None]
        q_r = jnp.einsum('bshq,hqr->bhsr', q_big, W_qr)
        k_r = jnp.einsum('bld,hdr->bhlr', kv_rope, W_kr)
        scores = jnp.einsum('bhsr,bhlr->bhsl', q_r, k_r)
        attn = jax.nn.softmax(scores, axis=-1)
        ctx_c = jnp.einsum('bhsl,bld->bhsd', attn, kv_rope)
        ctx_lat = jnp.einsum('bhsd,hkd->bshk', ctx_c, w_kc_kv)
        out = ctx_lat.reshape(b, s, H * K) @ Wo.T
        return out

    def _L2_ffn_ref(x, weight, bias):
        import jax, jax.numpy as jnp
        import numpy as np
        B, S, D_IN, D_OUT = (4, 512, 512, 512)
        EPS = 1e-10
        scale = jnp.mean(jnp.abs(weight))
        w_t = jnp.clip(jnp.round(weight / (scale + EPS)), -1.0, 1.0)
        w_ste = weight + jax.lax.stop_gradient(w_t * scale - weight)
        return jnp.einsum('bsi,oi->bso', x, w_ste) + bias

    def _L3_xattn_ref(hidden_q, kv_c, Wq, w_kc_q, w_kc_kv, W_qr, W_kr, Wo):
        import jax, jax.numpy as jnp
        import numpy as np
        B, S, L = (2, 256, 256)
        DIM_Q, H, K, D_C, D_CQ, R = (512, 16, 128, 128, 384, 64)

        def _rope_tables(length, dim):
            inv = 1.0 / 10000.0 ** (jnp.arange(0, dim, 2, dtype=jnp.float32) / dim)
            f = jnp.arange(length, dtype=jnp.float32)[:, None] * inv[None, :]
            sin = jnp.repeat(jnp.sin(f), 2, axis=-1)
            cos = jnp.repeat(jnp.cos(f), 2, axis=-1)
            return (sin, cos)

        def _rotate_half(x):
            half = x.shape[-1] // 2
            return jnp.concatenate([-x[..., half:], x[..., :half]], axis=-1)

        def _apply_rope(x, sin, cos):
            return x * cos + _rotate_half(x) * sin
        Bv, Sv, _ = hidden_q.shape
        _, Lv, _ = kv_c.shape
        q_hk = (hidden_q @ Wq.T).reshape(Bv, Sv, H, K)
        q_big = jnp.einsum('bshk,hkq->bshq', q_hk, w_kc_q)
        sin_q, cos_q = _rope_tables(Sv, D_CQ)
        q_big = _apply_rope(q_big, sin_q[None, :, None, :], cos_q[None, :, None, :])
        sin_k, cos_k = _rope_tables(Lv, D_C)
        kv_r = _apply_rope(kv_c, sin_k[None], cos_k[None])
        q_r = jnp.einsum('bshq,hqr->bhsr', q_big, W_qr)
        k_r = jnp.einsum('bld,hdr->bhlr', kv_r, W_kr)
        scores = jnp.einsum('bhsr,bhlr->bhsl', q_r, k_r)
        attn = jax.nn.softmax(scores, axis=-1)
        ctx_c = jnp.einsum('bhsl,bld->bhsd', attn, kv_r)
        ctx_lat = jnp.einsum('bhsd,hkd->bhsk', ctx_c, w_kc_kv)
        ctx = ctx_lat.transpose(0, 2, 1, 3).reshape(Bv, Sv, H * K)
        return ctx @ Wo.T

    def _L3_ffn_ref(hidden_states, gate_w, expert_bias, shared_gate_w, shared_up_w, shared_down_w, experts_gate_up, experts_down):
        import jax, jax.numpy as jnp
        import numpy as np
        B, S, H = (1, 256, 512)
        F = 256
        E = 16
        K = 2
        NS = 1
        ROUTE_SCALE = 1.0
        b, s, h = hidden_states.shape
        x = hidden_states.reshape(-1, h)
        T = x.shape[0]
        router_logits = (x @ gate_w).astype(jnp.float32)
        scores = jax.nn.sigmoid(router_logits)
        _, selected = jax.lax.top_k(scores + expert_bias[None, :], K)
        top_scores = jnp.take_along_axis(scores, selected, axis=1)
        top_scores = top_scores / (top_scores.sum(-1, keepdims=True) + 1e-20)
        top_scores = top_scores * ROUTE_SCALE
        shared = jax.nn.silu(x @ shared_gate_w) * (x @ shared_up_w) @ shared_down_w
        comb = jnp.zeros((T, E), jnp.float32).at[jnp.arange(T)[:, None], selected].add(top_scores)
        routed = jnp.zeros_like(x)
        for e in range(E):
            gu = x @ experts_gate_up[e]
            g, u = jnp.split(gu, 2, axis=-1)
            routed = routed + comb[:, e:e + 1] * (jax.nn.silu(g) * u @ experts_down[e])
        return (shared + routed).reshape(b, s, h)
    x = x + _L0_xattn_ref(_layernorm(x, axis=-1), ctx_512, L0_xattn_Wq, L0_xattn_w_kc_q, L0_xattn_w_kc_kv, L0_xattn_W_qr, L0_xattn_W_kr, L0_xattn_Wo)
    x = x + _L0_ffn_ref(_layernorm(x, axis=-1), L0_ffn_gate_weight, L0_ffn_w_gate, L0_ffn_w_up, L0_ffn_w_down, L0_ffn_sw_gate, L0_ffn_sw_up, L0_ffn_sw_down)
    x = x + _L1_xattn_ref(_layernorm(x, axis=-1), ctx_512, L1_xattn_Wq, L1_xattn_Wkv_expand, L1_xattn_Wout)
    x = x + _L1_ffn_ref(_layernorm(x, axis=-1), L1_ffn_up_weight, L1_ffn_down_weight, L1_ffn_up_scale, L1_ffn_down_scale, L1_ffn_output_scale)
    x = x + _L2_xattn_ref(_layernorm(x, axis=-1), ctx_512, L2_xattn_Wq, L2_xattn_w_kc_q, L2_xattn_w_kc_kv, L2_xattn_W_qr, L2_xattn_W_kr, L2_xattn_Wo)
    x = x + _L2_ffn_ref(_layernorm(x, axis=-1), L2_ffn_weight, L2_ffn_bias)
    x = x + _L3_xattn_ref(_layernorm(x, axis=-1), ctx_512, L3_xattn_Wq, L3_xattn_w_kc_q, L3_xattn_w_kc_kv, L3_xattn_W_qr, L3_xattn_W_kr, L3_xattn_Wo)
    x = x + _L3_ffn_ref(_layernorm(x, axis=-1), L3_ffn_gate_w, L3_ffn_expert_bias, L3_ffn_shared_gate_w, L3_ffn_shared_up_w, L3_ffn_shared_down_w, L3_ffn_experts_gate_up, L3_ffn_experts_down)
    return x

_drawn_inputs = setup_inputs


def setup_inputs(seed=0):
    import zlib

    import numpy as np

    out = dict(_drawn_inputs(seed))
    spreads = {'L1_ffn_up_scale': (1.0, 0.2),
     'L1_ffn_down_scale': (1.0, 0.2),
     'L3_ffn_expert_bias': (0.0, 0.8)}
    factors = {'L1_xattn_Wq': 8.0,
     'L2_xattn_Wq': 8.0,
     'L2_xattn_w_kc_q': 8.0,
     'L2_xattn_w_kc_kv': 8.0,
     'L2_xattn_W_qr': 8.0,
     'L2_xattn_W_kr': 8.0,
     'L2_xattn_Wo': 8.0,
     'L2_ffn_weight': 40.671,
     'L2_ffn_bias': 64.0,
     'L3_xattn_Wq': 8.0,
     'L3_xattn_w_kc_q': 8.0,
     'L3_xattn_w_kc_kv': 8.0,
     'L3_xattn_W_qr': 8.0,
     'L3_xattn_W_kr': 8.0,
     'L3_xattn_Wo': 8.0,
     'L3_ffn_gate_w': 8.0,
     'L3_ffn_shared_gate_w': 8.0,
     'L3_ffn_shared_up_w': 8.0,
     'L3_ffn_shared_down_w': 8.0,
     'L3_ffn_experts_gate_up': 8.0,
     'L3_ffn_experts_down': 8.0}
    for name, (base, spread) in spreads.items():
        noise = np.random.default_rng([zlib.crc32(name.encode()), seed]).standard_normal(out[name].shape)
        drawn = base * np.exp(spread * noise) if base else spread * noise
        out[name] = jnp.asarray(drawn.astype(out[name].dtype))
    for name, factor in factors.items():
        out[name] = (out[name] * factor).astype(out[name].dtype)
    return out
```

```python
from contextlib import ExitStack

import concourse.bass as bass
from concourse import mybir

ALU = mybir.AluOpType
ACT = mybir.ActivationFunctionType
F32 = mybir.dt.float32
AX_X = mybir.AxisListType.X

STAGES = 8

B, S, D = 8, 112, 512
L, DC = 375, 128
T = B * S
P = 128
C = D // P
HALVES = 2
HT = T // HALVES
BH = B // HALVES
KC, KP = 3, L // 3
HEADS = 16
QC = 3
R = 64
H1, HD1 = 16, 32
EPS = 1e-5
HUGE = 3.0e38
MASKED = -3.0e38
MAGIC = 12582912.0

ROPE_FIRST = ["ww", "q0", "q1", "a0", "b0", "c0", "a1", "b1", "c1", "p0", "p1"]
ROPE_FULL = ["ww", "q0", "q1", "v0", "a0", "b0", "c0", "a1", "b1", "c1", "p0",
             "o0", "o1", "o2", "o3", "p1", "o4", "o5", "o6", "o7"]
ROPE_LAST = ["v0", "o0", "o1", "o2", "o3", "o4", "o5", "o6", "o7"]
FOLD_FIRST = ["ww", "q0", "q1", "wb", "p0", "p1"]
FOLD_FULL = ["ww", "q0", "q1", "v0", "v1", "wb", "p0", "o0", "o1", "o2", "o3", "p1",
             "o4", "o5", "o6", "o7"]
FOLD_LAST = ["v0", "v1", "o0", "o1", "o2", "o3", "o4", "o5", "o6", "o7"]
GLU_HALF = ["g0", "u0", "g1", "u1", "s0", "s1"]
SIGN_ROUND = ["00", "01", "10", "11"]
NBANK = 4
SCALE1 = HD1 ** -0.5
W2_STEPS = 5
N_W1 = 8


class Ring:

    def __init__(self, names, at, per=0, i=0):
        self.at, self.per, self.i = at, per, i
        self.n = {name: k for k, name in enumerate(names)}

    def bank(self, name):
        return (self.at + self.n[name]) % NBANK

    def uses_before(self, name):
        return self.per // NBANK * self.i + (self.at + self.n[name]) // NBANK

    def count(self, name):
        return self.per * self.i + self.at + self.n[name] + 1


def build(nc, x_in, ctx_t, ctx_r, tabs_q, tabs_k, tabs_r, mask_in, ident_in,
          latent, gates, bias3, glu_gu, glu_dn, glu_sel, w1q, w1kv, w1o,
          up1, dn1, dn1s, out1s, w2, b2, out):
    GLU_E = [g.shape[2] for g in gates]
    GLU_N = [w.shape[0] for w in glu_gu]
    SGN_N = up1.shape[0]

    ctx = ExitStack()
    with ctx:
        def sb(name, shape, dt=F32):
            return ctx.enter_context(nc.sbuf_tensor(name, shape, dt))

        def sem(name):
            return ctx.enter_context(nc.semaphore(name))

        x = sb("x", [P, C, T])
        xn = sb("xn", [P, C, T])
        sq = sb("sq", [P, C, T])
        var = sb("var", [S, B])
        nwt = sb("nwt", [S, 3, B])
        rstd = sb("rstd", [S, B])
        half_pow = sb("half_pow", [S, B])
        diag = sb("diag", [S, B, S])
        ident = sb("ident", [P, P])
        ones = sb("ones", [P, P])
        one = sb("one", [P, P])
        mask = sb("mask", [S, S])
        raw_s = sb("raw_s", [P, B, S])
        kv_t = sb("kv_t", [P, B, L])
        kv_r = sb("kv_r", [KP, B, KC, DC])
        rope_t = sb("rope_t", [P, 2, L])
        rope_r = sb("rope_r", [KP, 2, KC, DC])
        rope_q = sb("rope_q", [P, 2, QC, S])
        rot_t = sq[:, :, :].rearrange("p c t -> p (c t)")[:, 0:B * L].rearrange("p (b l) -> p b l", b=B)
        rot_r = xn[0:KP, :, :].rearrange("p c t -> p (c t)")[:, 0:B * KC * DC].rearrange(
            "p (b c d) -> p b c d", b=B, c=KC)
        w_qk = sb("w_qk", [R, QC * P + DC])
        w_q = sb("w_q", [P, C, P])
        w_kc = sb("w_kc", [P, QC, P])
        w_vo = sb("w_vo", [P, DC + D])
        ww = sb("ww", [P, QC, DC])
        wb = sb("wb", [P, DC])
        vo = sb("vo", [DC, D])
        q_t = sb("q_t", [P, T])
        qb = sb("qb", [P, QC, T])
        turned = sb("turned", [P, QC, HT])
        qp = sb("qp", [P, T])
        nmax = sb("nmax", [S, B])
        psum_e = sb("psum_e", [S, B])
        prec = sb("prec", [S, B])
        probs = sb("probs", [S, 2, L])
        probs_t = sb("probs_t", [KP, KC, S])
        ctx_sb = sb("ctx_sb", [P, T])
        w_gu = sb("w_gu", [P, 2, 2 * C, P])
        w_dn = sb("w_dn", [P, 2, D])
        w_sel = sb("w_sel", [max(GLU_E) + 1, 2, P])
        gate_w = [sb(f"gate_w{n}", [P, C, e]) for n, e in enumerate(GLU_E)]
        silu = sb("silu", [P, 2, HT])
        share = sb("share", [P, 2, HT])
        hid = sb("hid", [P, HALVES, 2, HT])
        comb_t = sb("comb_t", [max(GLU_E) + 1, T])
        ebias = sb("ebias", [S, GLU_E[1]])
        rt = [[sb(f"rt{n}_{k}", [S, B, e]) for k in range(6)] for n, e in enumerate(GLU_E)]
        rs = [[sb(f"rs{n}_{k}", [S, B]) for k in range(5)] for n in range(2)]
        comb = [sb(f"comb{n}", [S, B, e + 1]) for n, e in enumerate(GLU_E)]
        revio_i = [sb(f"revio_i{n}", [S, e], mybir.dt.int32) for n, e in enumerate(GLU_E)]
        revio = [sb(f"revio{n}", [S, e]) for n, e in enumerate(GLU_E)]
        w1q_s = sb("w1q_s", [P, C, D])
        w1kv_s = sb("w1kv_s", [P, 2 * D])
        w1o_s = sb("w1o_s", [P, C, D])
        qb_flat = qb[:, :, :].rearrange("p c t -> p (c t)")
        q1 = q_t[:, 0:C * S].rearrange("p (c s) -> p c s", c=C)
        k1 = q_t[:, C * S:2 * C * S].rearrange("p (c s) -> p c s", c=C)
        v1 = qp[0:S, 0:D]
        s1 = qb_flat[0:S, 0:16 * S].rearrange("s (r t) -> s r t", r=4)
        m1 = sb("m1", [S, 4, 4])
        z1 = sb("z1", [S, 4, 4])
        pt1 = qb_flat[0:S, 16 * S:24 * S].rearrange("s (r t) -> s r t", r=2)
        c1 = turned[:, 0, :]
        raw_up = sb("raw_up", [P, 2, C, P])
        raw_dn = sb("raw_dn", [P, 2, D + 1])
        sup = sb("sup", [P, 2])
        sdn = sb("sdn", [P, C])
        s_out = sb("s_out", [P, 1])
        sdo = sb("sdo", [P, C])
        w2s = sb("w2s", [P, C, D])
        w2b = sb("w2b", [P, C])
        w2m = sb("w2m", [P, 4])
        w2t = sq[:, :, :].rearrange("p c t -> p (c t)")[:, 0:C * D].rearrange("p (c d) -> p c d", c=C)
        w2p = sb("w2p", [P, C * 8])
        raw_b = sb("raw_b", [P, S])

        bank = [ctx.enter_context(nc.psum_tensor(f"bank{n}", [P, 512], F32)) for n in range(8)]

        x_loaded = sem("x_loaded")
        consts_loaded = sem("consts_loaded")
        ctx_loaded = sem("ctx_loaded")
        w1_loaded = sem("w1_loaded")
        w2_loaded = sem("w2_loaded")
        scales_loaded = sem("scales_loaded")
        consts_set = sem("consts_set")
        gp_set = sem("gp_set")
        rope_r_step = sem("rope_r_step")
        rope_t_step = sem("rope_t_step")
        w2_step = sem("w2_step")
        w2_sum = sem("w2_sum")
        ln_mean = sem("ln_mean")
        ln_centred = sem("ln_centred")
        ln_squared = sem("ln_squared")
        ln_var = sem("ln_var")
        ln_step = sem("ln_step")
        ln_pow = sem("ln_pow")
        ln_spread = sem("ln_spread")
        ln_done = sem("ln_done")
        ring_ready = sem("ring_ready")
        bank_free = [sem(f"bank_free{n}") for n in range(NBANK)]
        w_in = {k: sem(f"{k}_in") for k in ("w_qk", "w_q", "w_kc", "w_vo")}
        w_used = {k: sem(f"{k}_used") for k in ("w_qk", "w_q", "w_kc", "w_vo")}
        rope_added = sem("rope_added")
        scores_ready = sem("scores_ready")
        max_ready = sem("max_ready")
        exp_ready = sem("exp_ready")
        rec_ready = sem("rec_ready")
        probs_ready = sem("probs_ready")
        turned_ready = sem("turned_ready")
        probs_t_ready = sem("probs_t_ready")
        ctx_ready = sem("ctx_ready")
        ctx_kept = sem("ctx_kept")
        gu_in = [sem(f"gu_in{j}") for j in range(2)]
        sel_in, sel_used = sem("sel_in"), sem("sel_used")
        raw_b_ready = sem("raw_b_ready")
        w2_tern = sem("w2_tern")
        gu_used = [sem(f"gu_used{j}") for j in range(2)]
        dn_in = sem("dn_in")
        dn_used = sem("dn_used")
        hid_ready = sem("hid_ready")
        down_ready = sem("down_ready")
        down_added = sem("down_added")
        logits_ready = sem("logits_ready")
        route_act = sem("route_act")
        route_step = sem("route_step")
        comb_turned = sem("comb_turned")
        comb_kept = sem("comb_kept")
        q1_ready, q1_kept = sem("q1_ready"), sem("q1_kept")
        s1_ready, s1_masked, s1_max, s1_shift = sem("s1_ready"), sem("s1_masked"), sem("s1_max"), sem("s1_shift")
        s1_exp, s1_sum, s1_rec, s1_norm = sem("s1_exp"), sem("s1_sum"), sem("s1_rec"), sem("s1_norm")
        p1_turned, p1_kept = sem("p1_turned"), sem("p1_kept")
        c1_ready, c1_kept = sem("c1_ready"), sem("c1_kept")
        o1_ready, o1_added = sem("o1_ready"), sem("o1_added")
        up_in = [sem(f"up_in{j}") for j in range(2)]
        dn1_in = sem("dn1_in")
        sgn_up = [sem(f"sgn_up{j}") for j in range(2)]
        sgn_dn = sem("sgn_dn")
        sdo_ready = sem("sdo_ready")
        sup_kept = sem("sup_kept")
        t2_ready, t2_added = sem("t2_ready"), sem("t2_added")
        out_done = sem("out_done")

        block = ctx.enter_context(nc.Block())

        ring_at = {}
        at = 0
        ring_at["lat0"] = at
        at += len(ROPE_FIRST) + (HEADS - 1) * len(ROPE_FULL) + len(ROPE_LAST)
        ring_at["glu0"] = at
        at += GLU_N[0] // 2 * 2 * len(GLU_HALF)
        ring_at["sgn"] = at
        at += SGN_N // 2 * 4
        ring_at["lat1"] = at
        at += len(FOLD_FIRST) + (HEADS - 1) * len(FOLD_FULL) + len(FOLD_LAST)
        ring_at["lat2"] = at
        at += len(ROPE_FIRST) + (HEADS - 1) * len(ROPE_FULL) + len(ROPE_LAST)
        ring_at["glu1"] = at
        at += GLU_N[1] // 2 * 2 * len(GLU_HALF)
        ring_at["end"] = at
        assert all(v % NBANK == 0 for v in ring_at.values())
        ring_after = {"lat0": "glu0", "glu0": "sgn", "sgn": "lat1", "lat1": "lat2", "lat2": "glu1", "glu1": "end"}
        rounds_at = {"glu0": 0, "sgn": GLU_N[0] // 2, "glu1": GLU_N[0] // 2 + SGN_N // 2}
        rounds_all = rounds_at["glu1"] + GLU_N[1] // 2
        ropes_at = {0: 0, 2: HEADS}
        route_end = [22, 22 + 18]

        def half(h):
            return slice(h * HT, (h + 1) * HT)

        def queries(b):
            return slice(b * S, (b + 1) * S)

        def layer_input_ready(eng, stage):
            if stage == 0:
                eng.wait_ge(x_loaded, 16)
            elif stage in (1, 5, 7):
                layer = {1: "lat0", 5: "lat1", 7: "lat2"}[stage]
                for n in range(NBANK):
                    eng.wait_ge(bank_free[n], ring_at[ring_after[layer]] // NBANK)
            elif stage in (2, 4, 8):
                rounds = {2: rounds_at["sgn"], 4: rounds_at["glu1"], 8: rounds_all}[stage]
                eng.wait_ge(down_added, rounds * 2 * C)
            elif stage == 3:
                eng.wait_ge(o1_added, B)
            elif stage == 6:
                eng.wait_ge(t2_added, HALVES * C)

        @block.sync
        def _(sp):
            sp.dma_start(x[:, :, :], x_in).then_inc(x_loaded, 16)
            sp.dma_start(ident[:, :], ident_in).then_inc(consts_loaded, 16)
            sp.dma_start(rope_q[:, :, :, :], tabs_q).then_inc(consts_loaded, 16)
            sp.dma_start(kv_r[:, :, :, :], ctx_r).then_inc(ctx_loaded, 16)
            sp.dma_start(rope_r[:, :, :, :], tabs_r).then_inc(ctx_loaded, 16)
            sp.dma_start(kv_t[:, :, :], ctx_t).then_inc(ctx_loaded, 16)
            sp.dma_start(rot_t[0:DC // 2, :, :], ctx_t[DC // 2:DC]).then_inc(ctx_loaded, 16)
            sp.dma_start(rot_t[DC // 2:DC, :, :], ctx_t[0:DC // 2]).then_inc(ctx_loaded, 16)
            sp.dma_start(rope_t[:, :, :], tabs_k).then_inc(ctx_loaded, 16)

            def latent_loads(n):
                w = latent[n]

                def load(h, g):
                    if n or not isinstance(g, int):
                        sp.wait_ge(w_used["w_qk"], g)
                    sp.dma_start(w_qk[:, :], w["qk"][h]).then_inc(w_in["w_qk"], 16)
                    if n or not isinstance(g, int):
                        sp.wait_ge(w_used["w_q"], g)
                    sp.dma_start(w_q[:, :, :], w["q"][h]).then_inc(w_in["w_q"], 16)
                    sp.wait_ge(w_used["w_kc"], g + 1)
                    sp.dma_start(w_kc[:, :, :], w["kc"][h]).then_inc(w_in["w_kc"], 16)
                    if n or not isinstance(g, int):
                        sp.wait_ge(w_used["w_vo"], g)
                    sp.dma_start(w_vo[:, :], w["vo"][h]).then_inc(w_in["w_vo"], 16)

                load(0, n * HEADS)
                with sp.Fori(1, HEADS) as h:
                    load(h, h + n * HEADS)

            def glu_loads(n, name):
                r0 = rounds_at[name]
                g0 = 0 if n == 0 else GLU_N[0] // 2
                e1 = GLU_E[n] + 1

                def load(i, first):
                    for j in range(2):
                        if not first:
                            sp.wait_ge(gu_used[j], i + r0)
                        sp.dma_start(w_gu[:, j, :, :], glu_gu[n][2 * i + j]).then_inc(gu_in[j], 16)
                    if not first:
                        sp.wait_ge(sel_used, i + r0)
                    sp.dma_start(w_sel[0:e1, :, :], glu_sel[n][i]).then_inc(sel_in, 16)
                    if not first:
                        sp.wait_ge(dn_used, i + r0)
                    sp.dma_start(w_dn[:, :, :], glu_dn[n][i]).then_inc(dn_in, 16)

                load(0, r0 == 0)
                with sp.Fori(1, GLU_N[n] // 2) as i:
                    load(i, False)

            def sign_loads():
                def load(i, first):
                    for j in range(2):
                        if not first:
                            sp.wait_ge(sgn_up[j], i)
                        sp.dma_start(raw_up[:, j, :, :], up1[2 * i + j]).then_inc(up_in[j], 16)
                    if not first:
                        sp.wait_ge(sgn_dn, i)
                    sp.dma_start(raw_dn[:, :, :], dn1[i]).then_inc(dn1_in, 16)

                load(0, True)
                with sp.Fori(1, SGN_N // 2) as i:
                    load(i, False)

            sp.dma_start(w2s[:, :, :], w2).then_inc(w2_loaded, 16)
            sp.dma_start(w2b[:, :], b2).then_inc(w1_loaded, 16)
            sp.dma_start(mask[:, :], mask_in).then_inc(consts_loaded, 16)
            for n in range(2):
                sp.dma_start(gate_w[n][:, :, :], gates[n]).then_inc(w1_loaded, 16)
            sp.dma_start(ebias[:, :], bias3.partition_broadcast(S)).then_inc(w1_loaded, 16)
            sp.dma_start(raw_s[:, :, :], ctx_t[:, :, 0:S]).then_inc(w1_loaded, 16)
            sp.dma_start(w1q_s[:, :, :], w1q).then_inc(w1_loaded, 16)
            sp.dma_start(w1kv_s[:, :], w1kv).then_inc(w1_loaded, 16)
            sp.dma_start(w1o_s[:, :, :], w1o).then_inc(w1_loaded, 16)
            sp.dma_start(sdn[:, :], dn1s).then_inc(scales_loaded, 16)
            sp.dma_start(s_out[:, :], out1s.partition_broadcast(P)).then_inc(scales_loaded, 16)
            latent_loads(0)
            if STAGES > 1:
                glu_loads(0, "glu0")
            if STAGES > 3:
                sign_loads()
            if STAGES > 4:
                latent_loads(1)
            if STAGES > 6:
                latent_loads(2)
            if STAGES > 7:
                glu_loads(1, "glu1")
            layer_input_ready(sp, STAGES)
            sp.dma_start(out, x[:, :, :]).then_inc(out_done, 16)
            sp.wait_ge(out_done, 16)

        @block.tensor
        def _(pe):
            def layer_norm(s):
                layer_input_ready(pe, s)
                if s == 0:
                    pe.wait_ge(consts_set, 2)
                for h in range(HALVES):
                    for c in range(C):
                        mm = pe.matmul(bank[h][:, 0:HT], ones[:, :], x[:, c, half(h)], start=(c == 0), stop=(c == C - 1))
                        if s in (2, 4) and h == 0 and c == 0:
                            mm.then_inc(dn_used, 1)
                    mm.then_inc(ln_mean, 1)
                for b in range(B):
                    if b % BH == 0:
                        pe.wait_ge(ln_squared, HALVES * C * s + C * (b // BH + 1))
                    for c in range(C):
                        mm = pe.matmul(bank[2][0:S, b:b + 1], sq[:, c, queries(b)], ones[:, 0:1],
                                       start=(c == 0), stop=(c == C - 1))
                mm.then_inc(ln_var, 1)
                pe.wait_ge(ln_step, 6 * s + 6)
                for h in range(HALVES):
                    pe.matmul(bank[3 + h][:, 0:HT], one[0:S, :],
                              diag[:, h * BH:(h + 1) * BH, :].rearrange("s b t -> s (b t)"),
                              start=True, stop=True).then_inc(ln_spread, 1)

            def ring_bank(ring, name):
                k = ring.bank(name)
                pe.wait_ge(bank_free[k], ring.uses_before(name))
                return bank[k]

            def kept(ring, name, before=None):
                if before is None or ring.bank(before) != ring.bank(name):
                    pe.wait_ge(bank_free[ring.bank(name)], ring.uses_before(name) + 1)

            def latent_attention(n, rope, s):
                g0 = n * HEADS
                first, full, last = (ROPE_FIRST, ROPE_FULL, ROPE_LAST) if rope else (FOLD_FIRST, FOLD_FULL, FOLD_LAST)
                at0 = ring_at[f"lat{n}"]
                rg0 = ropes_at.get(n, 0)

                def head(ring, p, a, pr):
                    def fold_scores():
                        pe.wait_ge(w_in["w_qk"], 16 * (p + 1))
                        o = ring_bank(ring, "ww")
                        for c in range(QC):
                            mm = pe.matmul(o[:, c * DC:(c + 1) * DC], w_qk[:, c * P:(c + 1) * P], w_qk[:, QC * P:],
                                           start=True, stop=True)
                        mm.then_inc(ring_ready, 1)

                    def q(h):
                        if h == 0:
                            pe.wait_ge(w_in["w_q"], 16 * (p + 1))
                        o = ring_bank(ring, f"q{h}")
                        for c in range(C):
                            mm = pe.matmul(o[:, 0:HT], w_q[:, c, :], xn[:, c, half(h)], start=(c == 0), stop=(c == C - 1))
                            if h == 0 and c == 0:
                                mm.then_inc(w_used["w_qk"], 1)
                            if h == 0 and c == 1:
                                mm.then_inc(w_used["w_kc"], 1)
                        mm.then_inc(ring_ready, 1)

                    def big(c, h):
                        name = "abc"[c] + str(h)
                        if c == 0:
                            kept(ring, f"q{h}", name)
                            if h == 0:
                                pe.wait_ge(w_in["w_kc"], 16 * (p + 1))
                        o = ring_bank(ring, name)
                        pe.matmul(o[:, 0:HT], w_kc[:, c, :], q_t[:, half(h)], start=True, stop=True).then_inc(ring_ready, 1)

                    def fold_b():
                        kept(ring, "ww", "wb")
                        pe.wait_ge(w_in["w_kc"], 16 * (p + 1))
                        o = ring_bank(ring, "wb")
                        for c in range(QC):
                            mm = pe.matmul(o[:, 0:DC], w_kc[:, c, :], ww[:, c, :], start=(c == 0), stop=(c == QC - 1))
                            if c == 0:
                                mm.then_inc(w_used["w_q"], 1)
                        mm.then_inc(ring_ready, 1)

                    def qprime(h):
                        if rope:
                            kept(ring, "ww", f"p{h}")
                            pe.wait_ge(rope_added, 6 * pr + 3 * (h + 1))
                        else:
                            kept(ring, "wb", f"p{h}")
                            kept(ring, f"q{h}", f"p{h}")
                        o = ring_bank(ring, f"p{h}")
                        if rope:
                            for c in range(QC):
                                mm = pe.matmul(o[:, 0:HT], ww[:, c, :], qb[:, c, half(h)], start=(c == 0), stop=(c == QC - 1))
                                if h == 0 and c == 0:
                                    mm.then_inc(w_used["w_q"], 1)
                        else:
                            mm = pe.matmul(o[:, 0:HT], wb[:, :], q_t[:, half(h)], start=True, stop=True)
                        mm.then_inc(ring_ready, 1)

                    def fold_out():
                        pe.wait_ge(w_in["w_vo"], 16 * (a + 1))
                        for k in range(1 if rope else 2):
                            o = ring_bank(ring, f"v{k}")
                            cols = slice(0, D) if rope else slice(k * D // 2, (k + 1) * D // 2)
                            pe.matmul(o[:, cols], w_vo[:, 0:DC], w_vo[:, DC + cols.start:DC + cols.stop],
                                      start=True, stop=True).then_inc(ring_ready, 1)

                    def scores(b):
                        pe.matmul(bank[4 + b % 2][0:S, 0:L], qp[:, queries(b)], kv_t[:, b, :], start=True, stop=True)\
                          .then_inc(scores_ready, 1)

                    def turn(b):
                        pe.wait_ge(probs_ready, a * B + b + 1)
                        for c in range(KC):
                            mm = pe.transpose(bank[6][0:KP, c * S:(c + 1) * S], probs[:, b % 2, c * KP:(c + 1) * KP],
                                              ident[0:S, 0:S])
                        mm.then_inc(turned_ready, 1)

                    def values(b):
                        G = a * B + b
                        if b == BH:
                            pe.wait_ge(ctx_kept, a * HALVES + 1)
                        pe.wait_ge(probs_t_ready, G + 1)
                        for c in range(KC):
                            mm = pe.matmul(bank[7][:, (b % BH) * S:(b % BH + 1) * S], kv_r[:, b, c, :],
                                           probs_t[:, c, :], start=(c == 0), stop=(c == KC - 1))
                            if b == 1 and c == 0:
                                mm.then_inc(w_used["w_vo"], 1)
                        if b % BH == BH - 1:
                            mm.then_inc(ctx_ready, 1)

                    def project(m):
                        h, c = m // C, m % C
                        if c == 0:
                            pe.wait_ge(ctx_kept, a * HALVES + h + 1)
                            if h == 0:
                                kept(ring, "v0", "o0")
                                if not rope:
                                    kept(ring, "v1", "o0")
                        o = ring_bank(ring, f"o{m}")
                        pe.matmul(o[:, 0:HT], vo[:, c * P:(c + 1) * P], ctx_sb[:, half(h)], start=True, stop=True)\
                          .then_inc(ring_ready, 1)

                    for b in range(B + 1):
                        if a is not None and b < B:
                            scores(b)
                        if p is not None:
                            if b == 0:
                                fold_scores()
                                q(0)
                            if rope and b == 2:
                                big(2, 0)
                            if rope and b == 3:
                                big(1, 1)
                            if not rope and b == 3:
                                fold_b()
                            if b == 4:
                                qprime(0)
                        if a is not None:
                            if b == 1:
                                fold_out()
                            if b == 5:
                                project(0)
                            if b == 6:
                                project(2)
                        if p is not None and b == 7:
                            qprime(1)
                        if a is not None and b > 0:
                            turn(b - 1)
                        if p is not None:
                            if b == 0:
                                q(1)
                            if rope and b == 1:
                                big(0, 0)
                                big(1, 0)
                            if rope and b == 2:
                                big(0, 1)
                            if rope and b == 3:
                                big(2, 1)
                        if a is not None:
                            if b == 5:
                                project(1)
                            if b == 6:
                                project(3)
                            if b > 0:
                                values(b - 1)
                            if b == B:
                                for m in range(C, 2 * C):
                                    project(m)
                    if p is not None:
                        kept(ring, "p0")
                        kept(ring, "p1")

                if n == 0:
                    pe.wait_ge(consts_loaded, 32)
                pe.wait_ge(ln_done, HALVES * C * (s + 1))
                head(Ring(first, at0), g0, None, rg0)
                if n == 0:
                    pe.wait_ge(rope_r_step, B + 2)
                    pe.wait_ge(rope_t_step, 3)
                with pe.Fori(0, HEADS - 1) as i:
                    head(Ring(full, at0 + len(first), len(full), i), i + g0 + 1, i + g0, i + rg0 + 1)
                head(Ring(last, at0 + len(first) + (HEADS - 1) * len(full)), None, g0 + HEADS - 1, 0)

            def glu_layer(n, name, s):
                r0, at0, E = rounds_at[name], ring_at[name], GLU_E[n]
                rg = 0 if n == 0 else GLU_N[0] // 2
                N = GLU_N[n] // 2
                pe.wait_ge(ln_done, HALVES * C * (s + 1))
                if n == 0:
                    pe.wait_ge(w1_loaded, 16 * N_W1)
                for b in range(B):
                    for c in range(C):
                        mm = pe.matmul(bank[4][0:S, b * E:(b + 1) * E], xn[:, c, queries(b)], gate_w[n][:, c, :],
                                       start=(c == 0), stop=(c == C - 1))
                mm.then_inc(logits_ready, 1)

                def hidden(i, h, j, first):
                    ring = Ring(GLU_HALF, at0 + h * len(GLU_HALF), 2 * len(GLU_HALF), i)
                    if h == 0:
                        pe.wait_ge(gu_in[j], 16 * (i + rg + 1))
                    for k, kind in enumerate("gu"):
                        o = ring_bank(ring, f"{kind}{j}")
                        for c in range(C):
                            mm = pe.matmul(o[:, 0:HT], w_gu[:, j, k * C + c, :], xn[:, c, half(h)],
                                           start=(c == 0), stop=(c == C - 1))
                            if h == 1 and j == 0 and k == 0 and c == 0 and not first:
                                mm.then_inc(dn_used, 1)
                            if h == 1 and j == 1 and k == 0 and c == 0:
                                mm.then_inc(gu_used[0], 1)
                        mm.then_inc(ring_ready, 1)

                def shares(i, h):
                    ring = Ring(GLU_HALF, at0 + h * len(GLU_HALF), 2 * len(GLU_HALF), i)
                    if h == 0:
                        pe.wait_ge(sel_in, 16 * (i + rg + 1))
                    for j in range(2):
                        o = ring_bank(ring, f"s{j}")
                        pe.matmul(o[:, 0:HT], w_sel[0:E + 1, j, :], comb_t[0:E + 1, half(h)], start=True, stop=True)\
                          .then_inc(ring_ready, 1)

                def turn_comb():
                    pe.wait_ge(route_step, route_end[n])
                    for b in range(B):
                        mm = pe.transpose(bank[5 + b // BH][0:E + 1, (b % BH) * S:(b % BH + 1) * S],
                                          comb[n][:, b, :], ident[0:S, 0:S])
                        if b % BH == BH - 1:
                            mm.then_inc(comb_turned, 1)
                    pe.wait_ge(comb_kept, 2 * (n + 1))

                def body(i, first):
                    hidden(i, 0, 0, first)
                    hidden(i, 0, 1, first)
                    if first:
                        turn_comb()
                    shares(i, 0)
                    if not first:
                        down(i - 1, 1, r0, [(hid_ready, 4 * (i + rg))])
                    hidden(i, 1, 0, first)
                    hidden(i, 1, 1, first)
                    shares(i, 1)
                    down(i, 0, r0, [(dn_in, 16 * (i + rg + 1)), (hid_ready, 4 * (i + rg) + 2)])

                body(0, True)
                with pe.Fori(1, N) as i:
                    body(i, False)
                down(N - 1, 1, r0, [(hid_ready, 4 * (N + rg))])

            def down(i, h, r0, needs):
                u = 2 * (i + r0) + h
                for s_, v_ in needs:
                    pe.wait_ge(s_, v_)
                for c in range(C):
                    if not (isinstance(u, int) and u == 0):
                        pe.wait_ge(down_added, C * (u - 1) + c + 1)
                    for j in range(2):
                        mm = pe.matmul(bank[4 + c][:, 0:HT], w_dn[:, j, c * P:(c + 1) * P], hid[:, h, j, :],
                                       start=(j == 0), stop=(j == 1))
                        if h == 0 and c == 0 and j == 0:
                            mm.then_inc(gu_used[1], 1)
                        if h == 0 and c == 1 and j == 0:
                            mm.then_inc(sel_used, 1)
                    mm.then_inc(down_ready, 1)

            def plain_attention(s):
                pe.wait_ge(ln_done, HALVES * C * (s + 1))
                pe.wait_ge(w1_loaded, 16 * N_W1)
                with pe.Fori(0, B) as b:
                    here = bass.ds(b * S, S)
                    for m in range(C):
                        for c in range(C):
                            mm = pe.matmul(bank[0][:, m * S:(m + 1) * S], w1q_s[:, c, m * P:(m + 1) * P],
                                           xn[:, c, here], start=(c == 0), stop=(c == C - 1))
                    mm.then_inc(q1_ready, 1)
                    for m in range(C):
                        mm = pe.matmul(bank[1][:, m * S:(m + 1) * S], w1kv_s[:, m * P:(m + 1) * P],
                                       raw_s[:, bass.ds(b, 1), :].rearrange("p a s -> p (a s)"), start=True, stop=True)
                    mm.then_inc(q1_ready, 1)
                    pe.wait_ge(raw_b_ready, b + 1)
                    pe.matmul(bank[2][0:S, :], raw_b[:, :], w1kv_s[:, D:2 * D], start=True, stop=True).then_inc(q1_ready, 1)
                    pe.wait_ge(q1_kept, 3 * b + 2)
                    for r in range(4):
                        for c in range(C):
                            mm = pe.matmul(bank[4 + r][0:S, c * S:(c + 1) * S], q1[r * HD1:(r + 1) * HD1, c, :],
                                           k1[r * HD1:(r + 1) * HD1, c, :], start=True, stop=True)
                        mm.then_inc(s1_ready, 1)
                    pe.wait_ge(q1_kept, 3 * b + 3)
                    for r in range(4):
                        pe.wait_ge(s1_norm, 4 * b + r + 1)
                        for c in range(C):
                            mm = pe.transpose(bank[r % 2][0:S, c * S:(c + 1) * S], s1[:, r, c * S:(c + 1) * S],
                                              ident[0:S, 0:S])
                        mm.then_inc(p1_turned, 1)
                        pe.wait_ge(p1_kept, 4 * b + r + 1)
                        for c in range(C):
                            mm = pe.matmul(bank[3][r * HD1:(r + 1) * HD1, c * S:(c + 1) * S],
                                           v1[:, c * P + r * HD1:c * P + (r + 1) * HD1],
                                           pt1[:, r % 2, c * S:(c + 1) * S], start=True, stop=True)
                    mm.then_inc(c1_ready, 1)
                    pe.wait_ge(c1_kept, b + 1)
                    for m in range(C):
                        for c in range(C):
                            mm = pe.matmul(bank[2][:, m * S:(m + 1) * S], w1o_s[:, c, m * P:(m + 1) * P],
                                           c1[:, c * S:(c + 1) * S], start=(c == 0), stop=(c == C - 1))
                    mm.then_inc(o1_ready, 1)
                    pe.wait_ge(o1_added, b + 1)

            def sign_layer(s):
                r0, at0, N = rounds_at["sgn"], ring_at["sgn"], SGN_N // 2
                pe.wait_ge(ln_done, HALVES * C * (s + 1))

                def hidden(i, h, first):
                    ring = Ring(SIGN_ROUND, at0, 4, i)
                    for j in range(2):
                        if h == 0:
                            pe.wait_ge(sgn_up[j], i + 1)
                        o = ring_bank(ring, f"{h}{j}")
                        for c in range(C):
                            mm = pe.matmul(o[:, 0:HT], w_gu[:, j, c, :], xn[:, c, half(h)],
                                           start=(c == 0), stop=(c == C - 1))
                            if h == 1 and j == 0 and c == 0 and not first:
                                mm.then_inc(dn_used, 1)
                            if h == 1 and j == 1 and c == 0:
                                mm.then_inc(gu_used[0], 1)
                        mm.then_inc(ring_ready, 1)

                def kept_rows(i, h):
                    ring = Ring(SIGN_ROUND, at0, 4, i)
                    return [(bank_free[ring.bank(f"{h}{j}")], ring.uses_before(f"{h}{j}") + 1) for j in range(2)]

                def body(i, first):
                    hidden(i, 0, first)
                    if not first:
                        down(i - 1, 1, r0, kept_rows(i - 1, 1))
                    hidden(i, 1, first)
                    down(i, 0, r0, [(sgn_dn, i + 1)] + kept_rows(i, 0))

                body(0, True)
                with pe.Fori(1, N) as i:
                    body(i, False)
                down(N - 1, 1, r0, kept_rows(N - 1, 1))

            def ternary_layer(s):
                pe.wait_ge(ln_done, HALVES * C * (s + 1))
                pe.wait_ge(w2_tern, W2_STEPS)
                for h in range(HALVES):
                    for m in range(C):
                        for c in range(C):
                            mm = pe.matmul(bank[h * C + m][:, 0:HT], w2s[:, c, m * P:(m + 1) * P], xn[:, c, half(h)],
                                           start=(c == 0), stop=(c == C - 1))
                        mm.then_inc(t2_ready, 1)

            layer_norm(0)
            pe.wait_ge(w2_step, 2)
            pe.matmul(bank[7][:, 0:1], one[:, :], w2m[:, 0:1], start=True, stop=True).then_inc(w2_sum, 1)
            latent_attention(0, True, 0)
            if STAGES > 1:
                layer_norm(1)
                glu_layer(0, "glu0", 1)
            if STAGES > 2:
                layer_norm(2)
                plain_attention(2)
            if STAGES > 3:
                layer_norm(3)
                sign_layer(3)
            if STAGES > 4:
                layer_norm(4)
                latent_attention(1, False, 4)
            if STAGES > 5:
                layer_norm(5)
                ternary_layer(5)
            if STAGES > 6:
                layer_norm(6)
                latent_attention(2, True, 6)
            if STAGES > 7:
                layer_norm(7)
                glu_layer(1, "glu1", 7)

        @block.scalar
        def _(act):
            def squares(s):
                for h in range(HALVES):
                    for c in range(C):
                        act.wait_ge(ln_centred, HALVES * C * s + C * h + c + 1)
                        act.activation(sq[:, c, half(h)], xn[:, c, half(h)], ACT.Square).then_inc(ln_squared, 1)

            def keep(ring, name, out, width):
                act.wait_ge(ring_ready, ring.count(name))
                rows = out.shape[0]
                act.activation(out, bank[ring.bank(name)][0:rows, 0:width], ACT.Copy)\
                   .then_inc(bank_free[ring.bank(name)], 1)

            def latent_attention(n, rope):
                g0 = n * HEADS
                first, full, last = (ROPE_FIRST, ROPE_FULL, ROPE_LAST) if rope else (FOLD_FIRST, FOLD_FULL, FOLD_LAST)
                at0 = ring_at[f"lat{n}"]

                def head(ring, p, a):
                    def exponent(b):
                        G = a * B + b
                        act.wait_ge(max_ready, G + 1)
                        act.activation(probs[:, b % 2, :], bank[4 + b % 2][0:S, 0:L], ACT.Exp, bias=nmax[:, b:b + 1],
                                       scale=1.0, accum_out=psum_e[:, b:b + 1]).then_inc(exp_ready, 1)

                    def keep_turned(b):
                        act.wait_ge(turned_ready, a * B + b + 1)
                        act.activation(probs_t[:, :, :].rearrange("k c s -> k (c s)"), bank[6][0:KP, 0:KC * S],
                                       ACT.Copy).then_inc(probs_t_ready, 1)

                    def keep_ctx(h):
                        act.wait_ge(ctx_ready, a * HALVES + h + 1)
                        act.activation(ctx_sb[:, half(h)], bank[7][:, 0:HT], ACT.Copy).then_inc(ctx_kept, 1)

                    for b in range(B + 1):
                        if a is not None and b == BH + 1:
                            keep_ctx(0)
                        if a is not None and b < B:
                            exponent(b)
                        if p is not None:
                            if b == 0:
                                keep(ring, "ww", ww[:, :, :].rearrange("p c d -> p (c d)"), QC * DC)
                                keep(ring, "q0", q_t[:, half(0)], HT)
                            if not rope and b == 3:
                                keep(ring, "wb", wb[:, :], DC)
                            if b == 4:
                                keep(ring, "p0", qp[:, half(0)], HT)
                            if b == 7:
                                keep(ring, "p1", qp[:, half(1)], HT)
                        if a is not None:
                            if b == 1 and rope:
                                keep(ring, "v0", vo[:, :], D)
                            if b == 1 and not rope:
                                for k in range(2):
                                    act.wait_ge(ring_ready, ring.count(f"v{k}"))
                                    cols = slice(k * D // 2, (k + 1) * D // 2)
                                    act.activation(vo[:, cols], bank[ring.bank(f"v{k}")][:, cols], ACT.Copy)\
                                       .then_inc(bank_free[ring.bank(f"v{k}")], 1)
                            if b > 0:
                                keep_turned(b - 1)
                        if p is not None and b == 0:
                            keep(ring, "q1", q_t[:, half(1)], HT)
                        if a is not None and b == B:
                            keep_ctx(1)

                head(Ring(first, at0), g0, None)
                with act.Fori(0, HEADS - 1) as i:
                    head(Ring(full, at0 + len(first), len(full), i), i + g0 + 1, i + g0)
                head(Ring(last, at0 + len(first) + (HEADS - 1) * len(full)), None, g0 + HEADS - 1)

            def glu_layer(n, name):
                at0, E, N = ring_at[name], GLU_E[n], GLU_N[n] // 2
                rg = 0 if n == 0 else GLU_N[0] // 2
                if n == 0:
                    act.wait_ge(route_step, 2)
                    act.activation(rt[n][0][:, :, :], rt[n][0][:, :, :], ACT.Exp).then_inc(route_act, 1)
                else:
                    act.wait_ge(logits_ready, 2)
                    act.activation(rt[n][1][:, :, :].rearrange("s b e -> s (b e)"), bank[4][0:S, 0:B * E],
                                   ACT.Sigmoid).then_inc(route_act, 1)

                def body(i, first):
                    for h in range(HALVES):
                        ring = Ring(GLU_HALF, at0 + h * len(GLU_HALF), 2 * len(GLU_HALF), i)
                        for j in range(2):
                            act.wait_ge(ring_ready, ring.count(f"g{j}"))
                            act.activation(silu[:, j, :], bank[ring.bank(f"g{j}")][:, 0:HT], ACT.Silu)\
                               .then_inc(bank_free[ring.bank(f"g{j}")], 1)
                        if first and h == 0:
                            for k in range(2):
                                act.wait_ge(comb_turned, 2 * n + k + 1)
                                act.activation(comb_t[0:E + 1, half(k)], bank[5 + k][0:E + 1, 0:HT], ACT.Copy)\
                                   .then_inc(comb_kept, 1)
                        for j in range(2):
                            if not (first and h == 0 and n == 0):
                                act.wait_ge(hid_ready, 4 * (i + rg) + 2 * (h - 1) + j + 1)
                            keep(ring, f"s{j}", share[:, j, :], HT)

                body(0, True)
                with act.Fori(1, N) as i:
                    body(i, False)

            def plain_attention():
                with act.Fori(0, B) as b:
                    act.wait_ge(q1_ready, 3 * b + 1)
                    act.activation(q1[:, :, :].rearrange("p c s -> p (c s)"), bank[0][:, 0:C * S], ACT.Copy).then_inc(q1_kept, 1)
                    act.wait_ge(q1_ready, 3 * b + 2)
                    act.activation(k1[:, :, :].rearrange("p c s -> p (c s)"), bank[1][:, 0:C * S], ACT.Copy).then_inc(q1_kept, 1)
                    act.wait_ge(q1_ready, 3 * b + 3)
                    act.activation(v1[:, :], bank[2][0:S, :], ACT.Copy).then_inc(q1_kept, 1)
                    for r in range(5):
                        if r < 4:
                            act.wait_ge(s1_shift, 4 * b + r + 1)
                            act.activation(s1[:, r, :], s1[:, r, :], ACT.Exp).then_inc(s1_exp, 1)
                        if r > 0:
                            act.wait_ge(p1_turned, 4 * b + r)
                            act.activation(pt1[:, (r - 1) % 2, :], bank[(r - 1) % 2][0:S, 0:4 * S], ACT.Copy).then_inc(p1_kept, 1)
                    act.wait_ge(c1_ready, b + 1)
                    act.activation(c1[:, :], bank[3][:, 0:C * S], ACT.Copy).then_inc(c1_kept, 1)

            def sign_layer():
                r0, at0, N = rounds_at["sgn"], ring_at["sgn"], SGN_N // 2
                
                def body(i, first):
                    ring = Ring(SIGN_ROUND, at0, 4, i)
                    for j in range(2):
                        act.wait_ge(up_in[j], 16 * (i + 1))
                        act.wait_ge(gu_used[j], i + r0)
                        act.activation(w_gu[:, j, 0:C, :], raw_up[:, j, :, :], ACT.Sign).then_inc(sgn_up[j], 1)
                    act.wait_ge(dn1_in, 16 * (i + 1))
                    act.wait_ge(bank_free[ring.bank("11")], ring.uses_before("11"))
                    act.activation(sup[:, :], raw_dn[:, :, D], ACT.Copy).then_inc(sup_kept, 1)
                    act.wait_ge(sup_kept, i + 1)
                    for h in range(HALVES):
                        for j in range(2):
                            act.wait_ge(ring_ready, ring.count(f"{h}{j}"))
                            act.activation(hid[:, h, j, :], bank[ring.bank(f"{h}{j}")][:, 0:HT], ACT.Relu,
                                           scale=sup[:, j:j + 1])\
                               .then_inc(bank_free[ring.bank(f"{h}{j}")], 1)
                        if h == 0:
                            act.wait_ge(dn_used, i + r0)
                            act.activation(w_dn[:, :, :], raw_dn[:, :, 0:D], ACT.Sign).then_inc(sgn_dn, 1)

                with act.Fori(0, N) as i:
                    body(i, False)

            squares(0)
            latent_attention(0, True)
            if STAGES > 1:
                squares(1)
                glu_layer(0, "glu0")
            if STAGES > 2:
                squares(2)
                plain_attention()
            if STAGES > 3:
                squares(3)
                sign_layer()
            if STAGES > 4:
                squares(4)
                latent_attention(1, False)
            if STAGES > 5:
                squares(5)
            if STAGES > 6:
                squares(6)
                latent_attention(2, True)
            if STAGES > 7:
                squares(7)
                glu_layer(1, "glu1")

        @block.vector
        def _(dve):
            def layer_norm(s):
                k0, n0 = HALVES * C * s, 6 * s
                layer_input_ready(dve, s)
                for h in range(HALVES):
                    dve.wait_ge(ln_mean, HALVES * s + h + 1)
                    for c in range(C):
                        dve.tensor_tensor(xn[:, c, half(h)], x[:, c, half(h)], bank[h][:, 0:HT], ALU.subtract)\
                           .then_inc(ln_centred, 1)
                dve.wait_ge(ln_var, s + 1)
                dve.tensor_scalar(var[:, :], bank[2][0:S, 0:B], EPS, None, ALU.add).then_inc(ln_step, 1)
                dve.wait_ge(ln_pow, s + 1)
                dve.tensor_tensor(nwt[:, 1, :], nwt[:, 0, :], nwt[:, 0, :], ALU.mult).then_inc(ln_step, 1)
                dve.wait_ge(ln_step, n0 + 2)
                dve.tensor_tensor(nwt[:, 1, :], nwt[:, 1, :], var[:, :], ALU.mult).then_inc(ln_step, 1)
                dve.wait_ge(ln_step, n0 + 3)
                dve.tensor_scalar(nwt[:, 2, :], nwt[:, 1, :], -0.5, 1.5, ALU.mult, ALU.add).then_inc(ln_step, 1)
                dve.wait_ge(ln_step, n0 + 4)
                dve.tensor_tensor(rstd[:, :], nwt[:, 0, :], nwt[:, 2, :], ALU.mult).then_inc(ln_step, 1)
                dve.wait_ge(ln_step, n0 + 5)
                dve.tensor_tensor(diag[:, :, :], ident[0:S, 0:S].unsqueeze(1).broadcast_to([S, B, S]),
                                  rstd[:, :].unsqueeze(2).broadcast_to([S, B, S]), ALU.mult).then_inc(ln_step, 1)
                for h in range(HALVES):
                    dve.wait_ge(ln_spread, HALVES * s + h + 1)
                    for c in range(C):
                        dve.tensor_tensor(xn[:, c, half(h)], xn[:, c, half(h)], bank[3 + h][:, 0:HT], ALU.mult)\
                           .then_inc(ln_done, 1)

            def add_to_x(h, c, psum):
                return dve.tensor_tensor(x[:, c, half(h)], x[:, c, half(h)], psum, ALU.add)

            def latent_attention(n, rope):
                g0 = n * HEADS
                first, full, last = (ROPE_FIRST, ROPE_FULL, ROPE_LAST) if rope else (FOLD_FIRST, FOLD_FULL, FOLD_LAST)
                at0 = ring_at[f"lat{n}"]
                rg0 = ropes_at.get(n, 0)

                def head(ring, p, a, pr):
                    def row_max(b):
                        G = a * B + b
                        dve.wait_ge(scores_ready, G + 1)
                        dve.tensor_reduce(nmax[:, b:b + 1], bank[4 + b % 2][0:S, 0:L], AX_X, ALU.max, negate=True)\
                           .then_inc(max_ready, 1)

                    def normalise(b):
                        G = a * B + b
                        dve.wait_ge(exp_ready, G + 1)
                        dve.reciprocal(prec[:, b:b + 1], psum_e[:, b:b + 1]).then_inc(rec_ready, 1)
                        dve.wait_ge(rec_ready, G + 1)
                        dve.tensor_scalar(probs[:, b % 2, :], probs[:, b % 2, :], prec[:, b:b + 1], None, ALU.mult)\
                           .then_inc(probs_ready, 1)

                    def turn_query(c, h):
                        name = "abc"[c] + str(h)
                        o = bank[ring.bank(name)]
                        free = bank_free[ring.bank(name)]
                        dve.wait_ge(ring_ready, ring.count(name))

                        def product(out, lo, hi, kind, tlo):
                            t = rope_q[tlo:tlo + hi - lo, kind, c if kind == 0 or c == 2 else 1 - c, :]
                            return dve.tensor_tensor(out.rearrange("p (b s) -> p b s", b=BH),
                                                     o[lo:hi, 0:HT].rearrange("p (b s) -> p b s", b=BH),
                                                     t.unsqueeze(1).broadcast_to([hi - lo, BH, S]), ALU.mult)

                        product(qb[:, c, half(h)], 0, P, 0, 0)
                        dve.wait_ge(rope_added, 6 * pr + 3 * h)
                        if c < 2:
                            product(turned[:, 1 - c, :], 0, P, 1, 0).then_inc(free, 1)
                        else:
                            product(turned[0:R, 2, :], R, P, 1, 0)
                            product(turned[R:P, 2, :], 0, R, 1, R).then_inc(free, 1)

                    def add_out(m):
                        k = ring.bank(f"o{m}")
                        dve.wait_ge(ring_ready, ring.count(f"o{m}"))
                        add_to_x(m // C, m % C, bank[k][:, 0:HT]).then_inc(bank_free[k], 1)

                    for b in range(B + 1):
                        if a is not None and b < B:
                            row_max(b)
                        if p is not None and rope:
                            if b == 2:
                                turn_query(0, 0)
                            if b == 3:
                                turn_query(2, 0)
                            if b == 4:
                                turn_query(1, 1)
                        if a is not None:
                            if b == 5:
                                add_out(0)
                            if b == 6:
                                add_out(2)
                            if b < B:
                                normalise(b)
                        if p is not None and rope:
                            if b == 2:
                                turn_query(1, 0)
                            if b == 3:
                                turn_query(0, 1)
                            if b == 4:
                                turn_query(2, 1)
                        if a is not None:
                            if b == 5:
                                add_out(1)
                            if b == 6:
                                add_out(3)
                            if b == B:
                                for m in range(C, 2 * C):
                                    add_out(m)

                head(Ring(first, at0), g0, None, rg0)
                with dve.Fori(0, HEADS - 1) as i:
                    head(Ring(full, at0 + len(first), len(full), i), i + g0 + 1, i + g0, i + rg0 + 1)
                head(Ring(last, at0 + len(first) + (HEADS - 1) * len(full)), None, g0 + HEADS - 1, 0)

            def route(n):
                E = GLU_E[n]
                done = [route_end[0] if n else 0]
                score, v, one1, one2, left = (rt[n][k] for k in range(1, 6))
                first = rt[n][0]
                m, den = rs[n][0], rs[n][1]

                def step(ins):
                    ins.then_inc(route_step, 1)
                    done[0] += 1
                    dve.wait_ge(route_step, done[0])

                def wide(t):
                    return t[:, :].unsqueeze(2).broadcast_to([S, B, E])

                rev = revio[n][:, :].unsqueeze(1).broadcast_to([S, B, E])
                logits = bank[4][0:S, 0:B * E].rearrange("s (b e) -> s b e", b=B)
                if n == 0:
                    dve.wait_ge(logits_ready, 1)
                    step(dve.tensor_reduce(m[:, :], logits, AX_X, ALU.max))
                    step(dve.tensor_tensor(first[:, :, :], logits, wide(m), ALU.subtract))
                    dve.wait_ge(route_act, 1)
                    step(dve.tensor_reduce(den[:, :], first[:, :, :], AX_X, ALU.add))
                    step(dve.reciprocal(rs[n][2][:, :], den[:, :]))
                    step(dve.tensor_tensor(score[:, :, :], first[:, :, :], wide(rs[n][2]), ALU.mult))
                    pick = score
                else:
                    dve.wait_ge(route_act, 2)
                    dve.wait_ge(w1_loaded, 16 * N_W1)
                    step(dve.tensor_tensor(first[:, :, :], score[:, :, :],
                                           ebias[:, :].unsqueeze(1).broadcast_to([S, B, E]), ALU.add))
                    pick = first
                for k, hot in enumerate((one1, one2)):
                    step(dve.tensor_reduce(m[:, :], pick[:, :, :], AX_X, ALU.max))
                    step(dve.tensor_tensor(v[:, :, :], pick[:, :, :], wide(m), ALU.is_equal))
                    step(dve.tensor_tensor(v[:, :, :], v[:, :, :], rev, ALU.mult))
                    step(dve.tensor_reduce(den[:, :], v[:, :, :], AX_X, ALU.max))
                    step(dve.tensor_tensor(hot[:, :, :], v[:, :, :], wide(den), ALU.is_equal))
                    if k == 0:
                        step(dve.scalar_tensor_tensor(left[:, :, :], hot[:, :, :], -HUGE, pick[:, :, :], ALU.mult, ALU.add))
                        pick = left
                step(dve.tensor_tensor(one1[:, :, :], one1[:, :, :], one2[:, :, :], ALU.add))
                step(dve.tensor_tensor(one1[:, :, :], one1[:, :, :], score[:, :, :], ALU.mult))
                step(dve.tensor_reduce(m[:, :], one1[:, :, :], AX_X, ALU.add))
                step(dve.tensor_scalar(m[:, :], m[:, :], 1e-20, None, ALU.add))
                step(dve.reciprocal(rs[n][3][:, :], m[:, :]))
                step(dve.tensor_tensor(comb[n][:, :, 0:E], one1[:, :, :], wide(rs[n][3]), ALU.mult))
                return done[0]

            def glu_layer(n, name):
                r0, at0, N = rounds_at[name], ring_at[name], GLU_N[n] // 2
                assert route(n) == route_end[n]

                def rows(i, h):
                    ring = Ring(GLU_HALF, at0 + h * len(GLU_HALF), 2 * len(GLU_HALF), i)
                    for j in range(2):
                        k = ring.bank(f"u{j}")
                        dve.wait_ge(ring_ready, ring.count(f"u{j}"))
                        dve.wait_ge(bank_free[ring.bank(f"g{j}")], ring.uses_before(f"g{j}") + 1)
                        dve.tensor_tensor(hid[:, h, j, :], silu[:, j, :], bank[k][:, 0:HT], ALU.mult).then_inc(bank_free[k], 1)

                def body(i, first):
                    rows(i, 0)
                    if not first:
                        add_down(i - 1, 1, r0)
                    rows(i, 1)
                    add_down(i, 0, r0)

                body(0, True)
                with dve.Fori(1, N) as i:
                    body(i, False)
                add_down(N - 1, 1, r0)

            def add_down(i, h, r0, scale=None):
                for c in range(C):
                    k = C * (2 * (i + r0) + h) + c
                    dve.wait_ge(down_ready, k + 1)
                    if scale is None:
                        ins = add_to_x(h, c, bank[4 + c][:, 0:HT])
                    else:
                        ins = dve.scalar_tensor_tensor(x[:, c, half(h)], bank[4 + c][:, 0:HT], scale[:, c:c + 1],
                                                       x[:, c, half(h)], ALU.mult, ALU.add)
                    ins.then_inc(down_added, 1)

            def plain_attention():
                with dve.Fori(0, B) as b:
                    for r in range(5):
                        if r < 4:
                            s4 = s1[:, r, :].rearrange("s (c k) -> s c k", c=4)
                            dve.wait_ge(s1_ready, 4 * b + r + 1)
                            dve.scalar_tensor_tensor(s4, bank[4 + r][0:S, 0:4 * S].rearrange("s (c k) -> s c k", c=4),
                                                     SCALE1, mask[:, :].unsqueeze(1).broadcast_to([S, 4, S]),
                                                     ALU.mult, ALU.add).then_inc(s1_masked, 1)
                            dve.wait_ge(s1_masked, 4 * b + r + 1)
                            dve.tensor_reduce(m1[:, r, :], s4, AX_X, ALU.max).then_inc(s1_max, 1)
                        if r > 0:
                            s4 = s1[:, r - 1, :].rearrange("s (c k) -> s c k", c=4)
                            dve.wait_ge(s1_exp, 4 * b + r)
                            dve.tensor_reduce(z1[:, r - 1, :], s4, AX_X, ALU.add).then_inc(s1_sum, 1)
                            dve.wait_ge(s1_sum, 4 * b + r)
                            dve.reciprocal(z1[:, r - 1, :], z1[:, r - 1, :]).then_inc(s1_rec, 1)
                    dve.wait_ge(o1_ready, b + 1)
                    here = bass.ds(b * S, S)
                    dve.tensor_tensor(x[:, :, here], x[:, :, here],
                                      bank[2][:, 0:C * S].rearrange("p (c s) -> p c s", c=C), ALU.add).then_inc(o1_added, 1)

            def sign_layer():
                r0, N = rounds_at["sgn"], SGN_N // 2
                dve.wait_ge(scales_loaded, 32)
                dve.tensor_scalar(sdo[:, :], sdn[:, :], s_out[:, 0:1], None, ALU.mult).then_inc(sdo_ready, 1)
                dve.wait_ge(sdo_ready, 1)
                add_down(0, 0, r0, sdo)
                with dve.Fori(1, N) as i:
                    add_down(i - 1, 1, r0, sdo)
                    add_down(i, 0, r0, sdo)
                add_down(N - 1, 1, r0, sdo)

            def ternary_layer():
                for h in range(HALVES):
                    for m in range(C):
                        dve.wait_ge(t2_ready, h * C + m + 1)
                        dve.scalar_tensor_tensor(x[:, m, half(h)], bank[h * C + m][:, 0:HT], w2b[:, m:m + 1],
                                                 x[:, m, half(h)], ALU.add, ALU.add).then_inc(t2_added, 1)

            dve.memset(ones[:, :], 1.0 / D).then_inc(consts_set, 1)
            dve.memset(one[:, :], 1.0).then_inc(consts_set, 1)
            dve.wait_ge(consts_loaded, 48)
            dve.memset(comb[0][:, :, :], 1.0)
            dve.memset(comb[1][:, :, :], 1.0)
            H2 = DC // 2
            turned_r = rot_r
            wide_r = rope_r[:, 0, :, :].unsqueeze(1).broadcast_to([KP, B, KC, DC])
            dve.wait_ge(ctx_loaded, 96)
            for b in range(B):
                dve.tensor_tensor(turned_r[:, b, :, 0:H2], kv_r[:, b, :, H2:DC], rope_r[:, 1, :, 0:H2], ALU.mult)
                dve.tensor_tensor(turned_r[:, b, :, H2:DC], kv_r[:, b, :, 0:H2], rope_r[:, 1, :, H2:DC], ALU.mult)\
                   .then_inc(rope_r_step, 1)
            dve.wait_ge(rope_r_step, B)
            dve.tensor_tensor(kv_r[:, :, :, :], kv_r[:, :, :, :], wide_r, ALU.mult).then_inc(rope_r_step, 1)
            dve.wait_ge(rope_r_step, B + 1)
            dve.tensor_tensor(kv_r[:, :, :, :], kv_r[:, :, :, :], turned_r, ALU.add).then_inc(rope_r_step, 1)
            dve.wait_ge(w2_loaded, 16)
            dve.tensor_reduce(w2p[:, :], w2s[:, :, :].rearrange("p c (a d) -> p (c a) d", a=8), AX_X, ALU.add,
                              apply_absolute_value=True).then_inc(w2_step, 1)
            dve.wait_ge(w2_step, 1)
            dve.tensor_reduce(w2m[:, 0:1], w2p[:, :], AX_X, ALU.add).then_inc(w2_step, 1)
            dve.wait_ge(rope_r_step, B + 2)
            dve.wait_ge(rope_t_step, 3)
            layer_norm(0)
            dve.wait_ge(w2_sum, 1)
            dve.tensor_scalar(w2m[:, 1:2], bank[7][:, 0:1], 1.0 / (D * D), None, ALU.mult).then_inc(w2_step, 1)
            dve.wait_ge(w2_step, 3)
            dve.tensor_scalar(w2m[:, 2:3], w2m[:, 1:2], 1e-10, None, ALU.add).then_inc(w2_step, 1)
            dve.wait_ge(w2_step, 4)
            dve.reciprocal(w2m[:, 3:4], w2m[:, 2:3]).then_inc(w2_step, 1)
            latent_attention(0, True)
            if STAGES > 1:
                layer_norm(1)
                glu_layer(0, "glu0")
            if STAGES > 2:
                layer_norm(2)
                plain_attention()
            if STAGES > 3:
                layer_norm(3)
                sign_layer()
            if STAGES > 4:
                layer_norm(4)
                latent_attention(1, False)
            if STAGES > 5:
                layer_norm(5)
                ternary_layer()
            if STAGES > 6:
                layer_norm(6)
                latent_attention(2, True)
            if STAGES > 7:
                layer_norm(7)
                glu_layer(1, "glu1")

        @block.gpsimd
        def _(gp):
            def power(s):
                gp.wait_ge(ln_step, 6 * s + 1)
                gp.tensor_tensor(nwt[:, 0, :], var[:, :], half_pow[:, :], ALU.pow).then_inc(ln_pow, 1)

            def latent_attention(n, rope):
                first, full = ROPE_FIRST, ROPE_FULL
                at0 = ring_at[f"lat{n}"]

                def head(ring):
                    for h in range(HALVES):
                        for name, parts in (("b", (0, 1)), ("c", (2,))):
                            gp.wait_ge(bank_free[ring.bank(f"a{h}")], ring.uses_before(f"a{h}") + 1)
                            k = ring.bank(f"{name}{h}")
                            gp.wait_ge(bank_free[k], ring.uses_before(f"{name}{h}") + 1)
                            for c in parts:
                                gp.tensor_tensor(qb[:, c, half(h)], qb[:, c, half(h)], turned[:, c, :], ALU.add)\
                                  .then_inc(rope_added, 1)

                head(Ring(first, at0))
                with gp.Fori(0, HEADS - 1) as i:
                    head(Ring(full, at0 + len(first), len(full), i))

            def glu_layer(n, name):
                at0, N = ring_at[name], GLU_N[n] // 2
                with gp.Fori(0, N) as i:
                    for h in range(HALVES):
                        ring = Ring(GLU_HALF, at0 + h * len(GLU_HALF), 2 * len(GLU_HALF), i)
                        for j in range(2):
                            for kind in "us":
                                gp.wait_ge(bank_free[ring.bank(f"{kind}{j}")], ring.uses_before(f"{kind}{j}") + 1)
                            gp.tensor_tensor(hid[:, h, j, :], hid[:, h, j, :], share[:, j, :], ALU.mult).then_inc(hid_ready, 1)

            def plain_attention():
                with gp.Fori(0, B) as b:
                    gp.wait_ge(w1_loaded, 16 * N_W1)
                    gp.tensor_copy(raw_b[:, :], raw_s[:, bass.ds(b, 1), :].rearrange("p a s -> p (a s)")).then_inc(raw_b_ready, 1)
                    for r in range(5):
                        if r < 4:
                            s4 = s1[:, r, :].rearrange("s (c k) -> s c k", c=4)
                            gp.wait_ge(s1_max, 4 * b + r + 1)
                            gp.tensor_tensor(s4, s4, m1[:, r, :].unsqueeze(2).broadcast_to([S, 4, S]), ALU.subtract)\
                              .then_inc(s1_shift, 1)
                        if r > 0:
                            s4 = s1[:, r - 1, :].rearrange("s (c k) -> s c k", c=4)
                            gp.wait_ge(s1_rec, 4 * b + r)
                            gp.tensor_tensor(s4, s4, z1[:, r - 1, :].unsqueeze(2).broadcast_to([S, 4, S]), ALU.mult)\
                              .then_inc(s1_norm, 1)

            def ternary():
                gp.wait_ge(w2_step, 5)
                steps = [
                    lambda: gp.tensor_scalar(w2t[:, :, :], w2s[:, :, :], w2m[:, 3:4], MAGIC, ALU.mult, ALU.add),
                    lambda: gp.tensor_scalar(w2t[:, :, :], w2t[:, :, :], -MAGIC, 1.0, ALU.add, ALU.min),
                    lambda: gp.tensor_scalar(w2t[:, :, :], w2t[:, :, :], -1.0, w2m[:, 1:2], ALU.max, ALU.mult),
                    lambda: gp.tensor_tensor(w2t[:, :, :], w2t[:, :, :], w2s[:, :, :], ALU.subtract),
                    lambda: gp.tensor_tensor(w2s[:, :, :], w2s[:, :, :], w2t[:, :, :], ALU.add),
                ]
                for k, step in enumerate(steps):
                    if k:
                        gp.wait_ge(w2_tern, k)
                    step().then_inc(w2_tern, 1)

            gp.memset(half_pow[:, :], -0.5).then_inc(gp_set, 1)
            for n, e in enumerate(GLU_E):
                gp.iota(revio_i[n][:, :], pattern=[[-1, e]], base=e, channel_multiplier=0).then_inc(gp_set, 1)
            gp.wait_ge(gp_set, 3)
            for n in range(2):
                gp.tensor_copy(revio[n][:, :], revio_i[n][:, :]).then_inc(gp_set, 1)
            gp.wait_ge(ctx_loaded, 96)
            wide = [rope_t[:, k, :].unsqueeze(1).broadcast_to([P, B, L]) for k in range(2)]
            gp.tensor_tensor(kv_t[:, :, :], kv_t[:, :, :], wide[0], ALU.mult).then_inc(rope_t_step, 1)
            gp.tensor_tensor(rot_t, rot_t, wide[1], ALU.mult).then_inc(rope_t_step, 1)
            gp.wait_ge(rope_t_step, 2)
            gp.tensor_tensor(kv_t[:, :, :], kv_t[:, :, :], rot_t, ALU.add).then_inc(rope_t_step, 1)
            power(0)
            latent_attention(0, True)
            if STAGES > 1:
                power(1)
                ternary()
                glu_layer(0, "glu0")
            if STAGES > 2:
                power(2)
                plain_attention()
            if STAGES > 3:
                power(3)
            if STAGES > 4:
                power(4)
            if STAGES > 5:
                power(5)
            if STAGES > 6:
                power(6)
                latent_attention(2, True)
            if STAGES > 7:
                power(7)
                glu_layer(1, "glu1")


def kernel(**inputs):
    import numpy as np
    import concourse.bacc as bacc
    from concourse import mybir as mb
    from concourse.bass_utils import run_bass_kernel_spmd as run

    nc = bacc.Bacc("TRN2", target_bir_lowering=False, num_devices=1)
    arrays = {}

    def arg(name, a):
        a = np.ascontiguousarray(a)
        arrays["in_" + name] = a
        return nc.dram_tensor("in_" + name, a.shape, mb.dt.from_np(a.dtype), kind="ExternalInput").ap()

    a = {k: np.asarray(v) for k, v in inputs.items()}

    def rope_tables(length, dim):
        inv = (np.float32(1.0) / np.float32(10000.0) ** (np.arange(0, dim, 2, dtype=np.float32) / np.float32(dim))).astype(np.float32)
        f = np.arange(length, dtype=np.float32)[:, None] * inv[None, :]
        return np.repeat(np.sin(f), 2, axis=-1).astype(np.float32), np.repeat(np.cos(f), 2, axis=-1).astype(np.float32)

    def query_order(w):
        return np.concatenate([w[..., 0:128], w[..., 192:320], w[..., 128:192], w[..., 320:384]], axis=-1)

    sin, cos = rope_tables(S, 384)
    turn = np.concatenate([-sin[:, :192], sin[:, 192:]], axis=1)
    tq = np.stack([query_order(cos), query_order(turn)])
    tabs_q = tq.reshape(2, S, 3, 128).transpose(3, 0, 2, 1)
    sin, cos = rope_tables(L, DC)
    turn = np.concatenate([-sin[:, :64], sin[:, 64:]], axis=1)
    tk = np.stack([cos, turn])
    tabs_k = tk.transpose(2, 0, 1)
    tabs_r = tk.reshape(2, KC, KP, DC).transpose(2, 0, 1, 3)
    mask = np.where(np.tril(np.ones((S, S), bool)), np.float32(0), np.float32(MASKED)).astype(np.float32)

    latent = []
    for n, name in enumerate(("L0", "L2", "L3")):
        w = {k: a[f"{name}_xattn_{k}"] for k in ("Wq", "w_kc_q", "w_kc_kv", "W_qr", "W_kr", "Wo")}
        q_rank = w["W_qr"].transpose(0, 2, 1)
        kc = w["w_kc_q"]
        if name != "L2":
            q_rank, kc = query_order(q_rank), query_order(kc)
            kc = kc.reshape(HEADS, P, QC, P)
        else:
            kc = kc.reshape(HEADS, P, QC, P).transpose(0, 3, 2, 1)
        latent.append({
            "qk": arg(f"{name}_qk", np.concatenate([q_rank, w["W_kr"].transpose(0, 2, 1)], axis=2)),
            "q": arg(f"{name}_q", w["Wq"].reshape(HEADS, P, C, P).transpose(0, 3, 2, 1)),
            "kc": arg(f"{name}_kc", kc),
            "vo": arg(f"{name}_vo", np.concatenate([w["w_kc_kv"], w["Wo"].reshape(D, HEADS, P).transpose(1, 2, 0)], axis=2)),
        })

    def pad(w):
        rows = -w.shape[0] % (2 * P)
        return np.concatenate([w, np.zeros((rows, w.shape[1]), np.float32)], axis=0) if rows else w

    def hidden_first(w):
        return pad(w).reshape(-1, P, C, P).transpose(0, 3, 2, 1)

    def hidden_second(w):
        return pad(w).reshape(-1, 2, P, D).transpose(0, 2, 1, 3)

    def selection(E, F, total):
        n = -(-total // (2 * P)) * 2 * P
        sel = np.zeros((n, E + 1), np.float32)
        owner = np.minimum(np.arange(total) // F, E)
        sel[np.arange(total), owner] = 1.0
        return sel.reshape(-1, 2, P, E + 1).transpose(0, 3, 1, 2)

    def gated(name, wg, wu, wd, E, F):
        gu = np.concatenate([hidden_first(wg), hidden_first(wu)], axis=2)
        return arg(f"{name}_gu", gu), arg(f"{name}_dn", hidden_second(wd)), arg(f"{name}_sel", selection(E, F, wg.shape[0]))

    E0, F0 = a["L0_ffn_w_gate"].shape[:2]
    g0 = gated("L0", np.concatenate([a["L0_ffn_w_gate"].reshape(-1, D), a["L0_ffn_sw_gate"]]),
               np.concatenate([a["L0_ffn_w_up"].reshape(-1, D), a["L0_ffn_sw_up"]]),
               np.concatenate([a["L0_ffn_w_down"].transpose(0, 2, 1).reshape(-1, D), a["L0_ffn_sw_down"].T]), E0, F0)
    eg = a["L3_ffn_experts_gate_up"]
    E3, F3 = eg.shape[0], eg.shape[2] // 2
    g3 = gated("L3", np.concatenate([eg[:, :, :F3].transpose(0, 2, 1).reshape(-1, D), a["L3_ffn_shared_gate_w"].T]),
               np.concatenate([eg[:, :, F3:].transpose(0, 2, 1).reshape(-1, D), a["L3_ffn_shared_up_w"].T]),
               np.concatenate([a["L3_ffn_experts_down"].reshape(-1, D), a["L3_ffn_shared_down_w"]]), E3, F3)

    def in_first(w):
        return w.reshape(w.shape[0], C, P).transpose(2, 1, 0)

    ctx = a["ctx_512"]
    out = nc.dram_tensor("out_x", (P, C, T), mb.dt.float32, kind="ExternalOutput").ap()
    build(nc,
          arg("x", a["x"].reshape(T, C, P).transpose(2, 1, 0)),
          arg("ctx_t", ctx.transpose(2, 0, 1)),
          arg("ctx_r", ctx.reshape(B, KC, KP, DC).transpose(2, 0, 1, 3)),
          arg("tabs_q", tabs_q), arg("tabs_k", tabs_k), arg("tabs_r", tabs_r),
          arg("mask", mask), arg("ident", np.eye(P, dtype=np.float32)),
          latent,
          [arg("gate0", in_first(a["L0_ffn_gate_weight"])), arg("gate3", in_first(a["L3_ffn_gate_w"].T))],
          arg("bias3", a["L3_ffn_expert_bias"]),
          [g0[0], g3[0]], [g0[1], g3[1]], [g0[2], g3[2]],
          arg("w1q", in_first(a["L1_xattn_Wq"])), arg("w1kv", a["L1_xattn_Wkv_expand"].T),
          arg("w1o", in_first(a["L1_xattn_Wout"])),
          arg("up1", hidden_first(a["L1_ffn_up_weight"])), arg("dn1", np.concatenate(
              [hidden_second(a["L1_ffn_down_weight"].T),
               a["L1_ffn_up_scale"].reshape(-1, 2, P).transpose(0, 2, 1)[..., None]], axis=3)),
          arg("dn1s", a["L1_ffn_down_scale"].reshape(C, P).T),
          arg("out1s", a["L1_ffn_output_scale"]),
          arg("w2", in_first(a["L2_ffn_weight"])), arg("b2", a["L2_ffn_bias"].reshape(C, P).T),
          out)
    r = run(nc, [arrays], core_ids=[0])
    return r.results[0]["out_x"].transpose(2, 1, 0).reshape(B, S, D)
```

```python
from contextlib import ExitStack

import concourse.bass as bass
from concourse import mybir

ALU = mybir.AluOpType
ACT = mybir.ActivationFunctionType
F32 = mybir.dt.float32
AX_X = mybir.AxisListType.X

STAGES = 8

B, S, D = 8, 112, 512
L, DC = 375, 128
T = B * S
P = 128
C = D // P
HALVES = 2
HT = T // HALVES
BH = B // HALVES
KC, KP = 3, L // 3
LE = L + L % 2
HEADS = 16
QC = 3
R = 64
H1, HD1 = 16, 32
EPS = 1e-5
HUGE = 3.0e38
MASKED = -3.0e38
MAGIC = 12582912.0

ROPE_SLOTS = [(["ww", "q0"], []), (["q1"], ["a0"]), (["b0"], ["c0"]), (["a1"], ["t4"]),
              (["b1"], ["t5", "t6"]), (["c1"], ["t7", "v0"]), (["p0"], ["o0", "o1"]), (["o2"], ["o3", "p1"])]
FOLD_SLOTS = [(["ww"], ["q0"]), (["q1"], []), (["wb"], []), (["t4"], ["t5"]),
              (["p0"], ["t6"]), (["t7"], ["v0", "v1"]), ([], ["o0", "o1"]), (["o2"], ["o3", "p1"])]
HIGH_AFTER = (4, 6)
FOR_NEXT = ("ww", "q", "a", "b", "c", "wb", "p")
FOR_LAST = ("t",)


def slots_of(table, p, a, last):
    def keep(name):
        if name.startswith(FOR_NEXT):
            return p
        return last if name.startswith(FOR_LAST) else a
    return [tuple([n for n in part if keep(n)] for part in slot) for slot in table]


def names_of(slots):
    return [n for slot in slots for part in slot for n in part]


GLU_HALF = ["g0", "u0", "g1", "u1", "s0", "s1"]
SIGN_ROUND = ["00", "01", "10", "11"]
LOW = 32
NBANK = 4
SCALE1 = HD1 ** -0.5
W2_STEPS = 5
N_W1 = 4


class Ring:

    def __init__(self, names, at, per=0, i=0):
        self.at, self.per, self.i = at, per, i
        self.n = {name: k for k, name in enumerate(names)}

    def bank(self, name):
        return (self.at + self.n[name]) % NBANK

    def uses_before(self, name):
        return self.per // NBANK * self.i + (self.at + self.n[name]) // NBANK

    def count(self, name):
        return self.per * self.i + self.at + self.n[name] + 1


def latent_blocks(table, at):
    blocks = []
    for p, a, last, times in ((True, False, False, 1), (True, True, False, 1), (True, True, True, HEADS - 3),
                              (True, True, True, 1), (False, True, True, 1), (False, False, True, 1)):
        slots = slots_of(table, p, a, last)
        blocks.append((slots, at))
        at += len(names_of(slots)) * times
    return blocks, at


def run_latent(eng, table, at, head):
    (first, second, full, full_last, final, tail), _ = latent_blocks(table, at)
    head(Ring(names_of(first[0]), first[1]), first[0], 0, None, None, True)
    head(Ring(names_of(second[0]), second[1]), second[0], 1, 0, None, True)
    names = names_of(full[0])
    with eng.Fori(0, HEADS - 3) as i:
        head(Ring(names, full[1], len(names), i), full[0], i + 2, i + 1, i, True)
    head(Ring(names, full_last[1]), full_last[0], HEADS - 1, HEADS - 2, HEADS - 3, False)
    head(Ring(names_of(final[0]), final[1]), final[0], None, HEADS - 1, HEADS - 2, False)
    head(Ring(names_of(tail[0]), tail[1]), tail[0], None, None, HEADS - 1, False)


def build(nc, x_in, ctx_t, ctx_r, tabs_q, tabs_k, tabs_r, mask_in, ident_in,
          latent, gates, bias3, glu_gu, glu_dn, glu_sel, w1q, w1kv, w1o,
          up1, dn1, dn1s, out1s, w2, b2, out):
    GLU_E = [g.shape[2] for g in gates]
    GLU_N = [w.shape[0] for w in glu_gu]
    SGN_N = up1.shape[0]

    ctx = ExitStack()
    with ctx:
        def sb(name, shape, dt=F32):
            return ctx.enter_context(nc.sbuf_tensor(name, shape, dt))

        def sem(name):
            return ctx.enter_context(nc.semaphore(name))

        F32R = mybir.dt.float32r

        def parts(name, shape):
            return [sb(f"{name}_hi", shape, F32R), sb(f"{name}_lo", shape, F32R)]

        x = sb("x", [P, C, T])
        xn = sb("xn", [P, C, T])
        with nc.sbuf_tensor("sq", [P, C, T], F32) as sq:
            pass
        x_lo = sb("x_lo", [P, C, T], F32R)
        x_hi = sb("x_hi", [P, C, T], F32R)
        xs = [x_hi, x_lo]
        var = sb("var", [S, B])
        nwt = sb("nwt", [S, 3, B])
        rstd = sb("rstd", [S, B])
        half_pow = sb("half_pow", [S, B])
        diag = sb("diag", [S, B, S])
        ident = sb("ident", [P, P])
        ones = sb("ones", [P, P])
        one = sb("one", [P, P])
        mask = sb("mask", [S, S])
        kvs = parts("kv_t", [P, B, LE])
        kv_r = sb("kv_r", [KP, B, KC, DC])
        rope_q = sb("rope_q", [P, 2, QC, S])
        w2s = sb("w2s", [P, C, D])
        w2b = sb("w2b", [P, C])
        w2m = sb("w2m", [P, 4])
        w2p = sb("w2p", [P, C * 8])
        gate_w = [sb(f"gate_w{n}", [P, C, e]) for n, e in enumerate(GLU_E)]
        ebias = sb("ebias", [S, GLU_E[1]])
        revio_i = [sb(f"revio_i{n}", [S, e], mybir.dt.int32) for n, e in enumerate(GLU_E)]
        revio = [sb(f"revio{n}", [S, e]) for n, e in enumerate(GLU_E)]
        comb = [sb(f"comb{n}", [S, B, e + 1]) for n, e in enumerate(GLU_E)]
        sdn = sb("sdn", [P, C])
        s_out = sb("s_out", [P, 1])
        sdo = sb("sdo", [P, C])
        sup = sb("sup", [P, 2])
        w_qk = sb("w_qk", [R, QC * P + DC])
        w_q = sb("w_q", [P, C, P])
        w_kc = sb("w_kc", [P, QC, P])
        w_vo = sb("w_vo", [P, DC + D])
        with nc.sbuf_tensor("rot_r", [KP, B, KC, DC], F32) as rot_r, nc.sbuf_tensor("rope_r", [KP, 2, KC, DC], F32) as rope_r:
            pass
        w_gu = sb("w_gu", [P, 2, 2 * C, P])
        w_dn = sb("w_dn", [P, 2, D + 1])
        w_sel = sb("w_sel", [2 * LOW, 2, P])
        wb = sb("wb", [P, DC])
        ww_f = sb("ww_f", [P, QC, DC])

        with ExitStack() as space:
            def sb(name, shape, dt=F32):
                return space.enter_context(nc.sbuf_tensor(name, shape, dt))

            ws_q = parts("ws_q", [P, C, P])
            ww = parts("ww", [P, QC, DC])
            q_t = sb("q_t", [P, T])
            turned = sb("turned", [P, QC, HT])
            qp = sb("qp", [P, T])
            qps = parts("qp", [P, T])
            nmax = sb("nmax", [S, B])
            psum_e = sb("psum_e", [S, B])
            prec = sb("prec", [S, B])
            qbs = parts("qb", [P, QC, T])
            with ExitStack() as inner:
                def sb(name, shape, dt=F32):
                    return inner.enter_context(nc.sbuf_tensor(name, shape, dt))

                rot_t = sb("rot_t", [P, B, L])
                rope_t = sb("rope_t", [P, 2, L])
                kv_t = sb("kv_t", [P, B, LE])
            with ExitStack() as inner:
                qb = sb("qb", [P, QC, T])
                vo = parts("vo", [DC, D])
                ctxs = parts("ctx", [P, T])
                probs = sb("probs", [S, 2, L])
                probs_t = sb("probs_t", [KP, 2, KC, S])

        def sb(name, shape, dt=F32):
            return space.enter_context(nc.sbuf_tensor(name, shape, dt))

        with ExitStack() as space:
            ws_gu = parts("ws_gu", [P, 2, 2 * C, P])
            ws_dn = parts("ws_dn", [P, 2, D])
            silu = sb("silu", [P, 2, HT])
            share = sb("share", [P, 2, HT])
            hid = sb("hid", [P, HALVES, 2, HT])
            hids = parts("hid", [P, HALVES, 2, HT])
            sel = sb("sel", [2 * LOW, 2, P], F32R)
            comb_t = sb("comb_t", [2 * LOW, T], F32R)
            w2t = sb("w2t", [P, C, D])
            rt = [[sb(f"rt{n}_{k}", [S, B, e]) for k in range(6)] for n, e in enumerate(GLU_E)]
            rs = [[sb(f"rs{n}_{k}", [S, B]) for k in range(5)] for n in range(2)]
        with ExitStack() as space:
            q1 = sb("q1", [P, C, S])
            k1 = sb("k1", [P, C, S])
            v1 = sb("v1", [S, D])
            s1 = sb("s1", [S, 4, 4 * S])
            pt1 = sb("pt1", [S, 2, 4 * S])
            c1 = sb("c1", [P, C * S])
            m1 = sb("m1", [S, 4, 4])
            z1 = sb("z1", [S, 4, 4])
            raw_s = sb("raw_s", [P, B, S])
            raw_b = sb("raw_b", [P, S])
            w1q_s = sb("w1q_s", [P, C, D])
            w1kv_s = sb("w1kv_s", [P, 2 * D])
            w1o_s = sb("w1o_s", [P, C, D])

        bank = [ctx.enter_context(nc.psum_tensor(f"bank{n}", [P, 512], F32)) for n in range(8)]

        x_loaded = sem("x_loaded")
        consts_loaded = sem("consts_loaded")
        mask_loaded = sem("mask_loaded")
        ctx_loaded = sem("ctx_loaded")
        w1_loaded = sem("w1_loaded")
        w2_loaded = sem("w2_loaded")
        scales_loaded = sem("scales_loaded")
        gates_loaded = sem("gates_loaded")
        consts_set = sem("consts_set")
        gp_set = sem("gp_set")
        rope_r_step = sem("rope_r_step")
        rope_t_step, rope_k_step = sem("rope_t_step"), sem("rope_k_step")
        w2_step = sem("w2_step")
        w2_sum = sem("w2_sum")
        ln_mean = sem("ln_mean")
        ln_centred = sem("ln_centred")
        ln_squared = sem("ln_squared")
        ln_summed = sem("ln_summed")
        ln_var = sem("ln_var")
        ln_step = sem("ln_step")
        ln_pow = sem("ln_pow")
        ln_spread = sem("ln_spread")
        ln_done = sem("ln_done")
        ring_ready = sem("ring_ready")
        bank_free = [sem(f"bank_free{n}") for n in range(NBANK)]
        w_in = {k: sem(f"{k}_in") for k in ("w_qk", "w_q", "w_kc", "w_vo")}
        w_used = {k: sem(f"{k}_used") for k in ("w_qk", "w_q", "w_kc", "w_vo")}
        q_hi, q_split = sem("q_hi"), sem("q_split")
        qp_lo = sem("qp_lo")
        ww_hi, qp_hi, vo_hi, ctx_hi = sem("ww_hi"), sem("qp_hi"), sem("vo_hi"), sem("ctx_hi")
        x_hi_set, x_split = sem("x_hi_set"), [sem(f"x_split{h}") for h in range(HALVES)]
        qb_hi, qb_split = sem("qb_hi"), [sem(f"qb_split{h}") for h in range(HALVES)]
        kv_hi, kv_split = sem("kv_hi"), sem("kv_split")
        gu_hi = [sem(f"gu_hi{j}") for j in range(2)]
        gu_split = [sem(f"gu_split{j}") for j in range(2)]
        dn_hi, dn_split = sem("dn_hi"), sem("dn_split")
        hid_made, hid_hi = sem("hid_made"), sem("hid_hi")
        rope_added = sem("rope_added")
        scores_ready = sem("scores_ready")
        max_ready = sem("max_ready")
        exp_ready = sem("exp_ready")
        rec_ready = sem("rec_ready")
        probs_ready = sem("probs_ready")
        turned_ready = sem("turned_ready")
        probs_t_ready = sem("probs_t_ready")
        ctx_ready = sem("ctx_ready")
        ctx_kept = sem("ctx_kept")
        gu_in = [sem(f"gu_in{j}") for j in range(2)]
        sel_in, sel_kept, sel_used = sem("sel_in"), sem("sel_kept"), sem("sel_used")
        raw_b_ready = sem("raw_b_ready")
        w2_tern = sem("w2_tern")
        gu_used = [sem(f"gu_used{j}") for j in range(2)]
        dn_in = sem("dn_in")
        dn_used = sem("dn_used")
        hid_ready = sem("hid_ready")
        down_ready = sem("down_ready")
        down_added = sem("down_added")
        logits_ready = sem("logits_ready")
        route_act = sem("route_act")
        route_step = sem("route_step")
        comb_turned = sem("comb_turned")
        comb_hi, comb_kept = sem("comb_hi"), sem("comb_kept")
        q1_ready, q1_kept = sem("q1_ready"), sem("q1_kept")
        s1_ready, s1_masked, s1_max, s1_shift = sem("s1_ready"), sem("s1_masked"), sem("s1_max"), sem("s1_shift")
        s1_exp, s1_sum, s1_rec, s1_norm = sem("s1_exp"), sem("s1_sum"), sem("s1_rec"), sem("s1_norm")
        p1_turned, p1_kept = sem("p1_turned"), sem("p1_kept")
        c1_ready, c1_kept = sem("c1_ready"), sem("c1_kept")
        o1_ready, o1_added = sem("o1_ready"), sem("o1_added")
        up_in = [sem(f"up_in{j}") for j in range(2)]
        dn1_in = sem("dn1_in")
        sdo_ready = sem("sdo_ready")
        sup_kept = sem("sup_kept")
        t2_ready, t2_added = sem("t2_ready"), sem("t2_added")
        out_done = sem("out_done")

        block = ctx.enter_context(nc.Block())

        ring_at = {}
        at = 0
        ring_at["lat0"] = at
        at = latent_blocks(ROPE_SLOTS, at)[1]
        ring_at["glu0"] = at
        at += GLU_N[0] // 2 * 2 * len(GLU_HALF)
        ring_at["sgn"] = at
        at += SGN_N // 2 * 4
        ring_at["lat1"] = at
        at = latent_blocks(FOLD_SLOTS, at)[1]
        ring_at["lat2"] = at
        at = latent_blocks(ROPE_SLOTS, at)[1]
        ring_at["glu1"] = at
        at += GLU_N[1] // 2 * 2 * len(GLU_HALF)
        ring_at["end"] = at
        assert all(v % NBANK == 0 for v in ring_at.values())
        ring_after = {"lat0": "glu0", "glu0": "sgn", "sgn": "lat1", "lat1": "lat2", "lat2": "glu1", "glu1": "end"}
        rounds_at = {"glu0": 0, "sgn": GLU_N[0] // 2, "glu1": GLU_N[0] // 2 + SGN_N // 2}
        rounds_all = rounds_at["glu1"] + GLU_N[1] // 2
        table = {0: ROPE_SLOTS, 1: FOLD_SLOTS, 2: ROPE_SLOTS}
        ropes_at = {0: 0, 1: HEADS, 2: HEADS}
        outs_at = {0: 0, 1: HEADS, 2: 3 * HEADS}
        outs_of = {0: 1, 1: 2, 2: 1}
        route_end = [22, 22 + 18]

        splits_before = {0: 0, 1: 1, 3: 2, 4: 3, 6: 4, 7: 5}

        def half(h):
            return slice(h * HT, (h + 1) * HT)

        def queries(b):
            return slice(b * S, (b + 1) * S)

        def layer_input_ready(eng, stage):
            if stage == 0:
                eng.wait_ge(x_loaded, 16)
            elif stage in (1, 5, 7):
                layer = {1: "lat0", 5: "lat1", 7: "lat2"}[stage]
                for n in range(NBANK):
                    eng.wait_ge(bank_free[n], ring_at[ring_after[layer]] // NBANK)
            elif stage in (2, 4, 8):
                rounds = {2: rounds_at["sgn"], 4: rounds_at["glu1"], 8: rounds_all}[stage]
                eng.wait_ge(down_added, rounds * 2 * C)
            elif stage == 3:
                eng.wait_ge(o1_added, B)
            elif stage == 6:
                eng.wait_ge(t2_added, HALVES * C)

        @block.sync
        def _(sp):
            sp.dma_start(x[:, :, :], x_in).then_inc(x_loaded, 16)
            sp.dma_start(ident[:, :], ident_in).then_inc(consts_loaded, 16)
            sp.dma_start(rope_q[:, :, :, :], tabs_q).then_inc(consts_loaded, 16)

            def context_loads():
                sp.dma_start(rot_t[0:DC // 2, :, :], ctx_t[DC // 2:DC]).then_inc(ctx_loaded, 16)
                sp.dma_start(rot_t[DC // 2:DC, :, :], ctx_t[0:DC // 2]).then_inc(ctx_loaded, 16)
                sp.dma_start(rope_t[:, :, :], tabs_k).then_inc(ctx_loaded, 16)
                sp.dma_start(kv_t[:, :, 0:L], ctx_t).then_inc(ctx_loaded, 16)
                sp.dma_start(kv_r[:, :, :, :], ctx_r).then_inc(ctx_loaded, 16)
                sp.dma_start(rope_r[:, :, :, :], tabs_r).then_inc(ctx_loaded, 16)

            def latent_loads(n):
                w = latent[n]

                def load(h, g):
                    if n or not isinstance(g, int):
                        sp.wait_ge(w_used["w_qk"], g)
                    sp.dma_start(w_qk[:, :], w["qk"][h]).then_inc(w_in["w_qk"], 16)
                    if n or not isinstance(g, int):
                        sp.wait_ge(q_split, g)
                    sp.dma_start(w_q[:, :, :], w["q"][h]).then_inc(w_in["w_q"], 16)
                    if isinstance(h, int) and n == 0:
                        context_loads()
                        small_loads()
                    sp.wait_ge(w_used["w_kc"], g + 1)
                    sp.dma_start(w_kc[:, :, :], w["kc"][h]).then_inc(w_in["w_kc"], 16)
                    if n or not isinstance(g, int):
                        sp.wait_ge(w_used["w_vo"], g)
                    sp.dma_start(w_vo[:, :], w["vo"][h]).then_inc(w_in["w_vo"], 16)

                load(0, n * HEADS)
                with sp.Fori(1, HEADS) as h:
                    load(h, h + n * HEADS)

            def glu_loads(n, name):
                r0 = rounds_at[name]
                g0 = 0 if n == 0 else GLU_N[0] // 2

                def load(i, first):
                    for j in range(2):
                        if not first:
                            sp.wait_ge(gu_split[j], i + r0)
                        sp.dma_start(w_gu[:, j, :, :], glu_gu[n][2 * i + j]).then_inc(gu_in[j], 16)
                    if n or not first:
                        sp.wait_ge(sel_kept, i + g0)
                    sp.dma_start(w_sel[:, :, :], glu_sel[n][i]).then_inc(sel_in, 16)
                    if not first:
                        sp.wait_ge(dn_split, i + r0)
                    sp.dma_start(w_dn[:, :, 0:D], glu_dn[n][i]).then_inc(dn_in, 16)

                load(0, r0 == 0)
                with sp.Fori(1, GLU_N[n] // 2) as i:
                    load(i, False)

            def sign_loads():
                def load(i):
                    for j in range(2):
                        sp.wait_ge(gu_split[j], i + rounds_at["sgn"])
                        sp.dma_start(w_gu[:, j, 0:C, :], up1[2 * i + j]).then_inc(up_in[j], 16)
                    sp.wait_ge(dn_split, i + rounds_at["sgn"])
                    sp.dma_start(w_dn[:, :, :], dn1[i]).then_inc(dn1_in, 16)

                with sp.Fori(0, SGN_N // 2) as i:
                    load(i)

            def small_loads():
                sp.dma_start(w2s[:, :, :], w2).then_inc(w2_loaded, 16)
                sp.dma_start(w2b[:, :], b2).then_inc(gates_loaded, 16)
                sp.dma_start(mask[:, :], mask_in).then_inc(mask_loaded, 16)
                for n in range(2):
                    sp.dma_start(gate_w[n][:, :, :], gates[n]).then_inc(gates_loaded, 16)
                sp.dma_start(ebias[:, :], bias3.partition_broadcast(S)).then_inc(gates_loaded, 16)
                sp.dma_start(sdn[:, :], dn1s).then_inc(scales_loaded, 16)
                sp.dma_start(s_out[:, :], out1s.partition_broadcast(P)).then_inc(scales_loaded, 16)

            latent_loads(0)
            if STAGES > 1:
                sp.wait_ge(rope_r_step, B + 2)
                glu_loads(0, "glu0")
            if STAGES > 2:
                layer_input_ready(sp, 2)
                sp.dma_start(raw_s[:, :, :], ctx_t[:, :, 0:S]).then_inc(w1_loaded, 16)
                sp.dma_start(w1q_s[:, :, :], w1q).then_inc(w1_loaded, 16)
                sp.dma_start(w1kv_s[:, :], w1kv).then_inc(w1_loaded, 16)
                sp.dma_start(w1o_s[:, :, :], w1o).then_inc(w1_loaded, 16)
            if STAGES > 3:
                sign_loads()
            if STAGES > 4:
                latent_loads(1)
            if STAGES > 6:
                latent_loads(2)
            if STAGES > 7:
                glu_loads(1, "glu1")
            layer_input_ready(sp, STAGES)
            sp.dma_start(out, x[:, :, :]).then_inc(out_done, 16)
            sp.wait_ge(out_done, 16)

        @block.tensor
        def _(pe):
            def layer_norm(s):
                layer_input_ready(pe, s)
                if s == 0:
                    pe.wait_ge(consts_set, 2)
                for h in range(HALVES):
                    for c in range(C):
                        mm = pe.matmul(bank[h][:, 0:HT], ones[:, :], x[:, c, half(h)], start=(c == 0), stop=(c == C - 1))
                        if s in (2, 4) and h == 0 and c == 0:
                            mm.then_inc(dn_used, 1)
                    mm.then_inc(ln_mean, 1)
                for b in range(B):
                    if b % BH == 0:
                        pe.wait_ge(ln_summed, 6 * s + 3 * (b // BH + 1))
                    mm = pe.matmul(bank[2][0:S, b:b + 1], sq[:, 0, queries(b)], ones[:, 0:1], start=True, stop=True)
                mm.then_inc(ln_var, 1)
                pe.wait_ge(ln_step, 6 * s + 6)
                for h in range(HALVES):
                    pe.matmul(bank[3 + h][:, 0:HT], one[0:S, :],
                              diag[:, h * BH:(h + 1) * BH, :].rearrange("s b t -> s (b t)"),
                              start=True, stop=True).then_inc(ln_spread, 1)

            def ring_bank(ring, name):
                k = ring.bank(name)
                pe.wait_ge(bank_free[k], ring.uses_before(name))
                return bank[k]

            def kept(ring, name, before=None):
                if before is None or ring.bank(before) != ring.bank(name):
                    pe.wait_ge(bank_free[ring.bank(name)], ring.uses_before(name) + 1)

            def parts_product(out, ws, xs_, first=True, last=True):
                for k, (w, v) in enumerate(zip(ws, xs_)):
                    for m, (a, b) in enumerate(((0, 0), (0, 1), (1, 0))[:3 if len(w) == 2 else 2]):
                        mm = pe.matmul(out, w[a], v[b], start=(first and k == 0 and m == 0),
                                       stop=(last and k == len(ws) - 1 and m == (2 if len(w) == 2 else 1)))
                        yield mm

            def latent_attention(n, rope, s):
                def head(ring, slots, p, a, last, more):
                    gp_ = None if p is None else p + n * HEADS
                    ga = None if a is None else a + n * HEADS
                    gl = None if last is None else last + n * HEADS

                    def fold_scores():
                        pe.wait_ge(w_in["w_qk"], 16 * (gp_ + 1))
                        o = ring_bank(ring, "ww")
                        for c in range(QC):
                            mm = pe.matmul(o[:, c * DC:(c + 1) * DC], w_qk[:, c * P:(c + 1) * P], w_qk[:, QC * P:],
                                           start=True, stop=True)
                        mm.then_inc(ring_ready, 1)

                    def q(h):
                        if h == 0:
                            pe.wait_ge(q_split, gp_ + 1)
                        if h == 1 and last is None and a is None:
                            pe.wait_ge(x_split[1], C * (splits_before[s] + 1))
                        o = ring_bank(ring, f"q{h}")
                        mms = parts_product(o[:, 0:HT], [[w[:, c, :] for w in ws_q] for c in range(C)],
                                            [[v[:, c, half(h)] for v in xs] for c in range(C)])
                        for k, mm in enumerate(mms):
                            if h == 0 and k == 0:
                                mm.then_inc(w_used["w_qk"], 1)
                            if h == 0 and k == 1:
                                mm.then_inc(w_used["w_kc"], 1)
                        mm.then_inc(ring_ready, 1)

                    def big(name):
                        c, h = "abc".index(name[0]), int(name[1])
                        if c == 0:
                            kept(ring, f"q{h}", name)
                            if h == 0:
                                pe.wait_ge(w_in["w_kc"], 16 * (gp_ + 1))
                        o = ring_bank(ring, name)
                        pe.matmul(o[:, 0:HT], w_kc[:, c, :], q_t[:, half(h)], start=True, stop=True).then_inc(ring_ready, 1)

                    def fold_b():
                        kept(ring, "ww", "wb")
                        pe.wait_ge(w_in["w_kc"], 16 * (gp_ + 1))
                        o = ring_bank(ring, "wb")
                        for c in range(QC):
                            mm = pe.matmul(o[:, 0:DC], w_kc[:, c, :], ww_f[:, c, :], start=(c == 0),
                                           stop=(c == QC - 1))
                            if c == 0:
                                mm.then_inc(w_used["w_q"], 1)
                        mm.then_inc(ring_ready, 1)

                    def folded_query(h):
                        if rope:
                            kept(ring, "ww", f"p{h}")
                            pe.wait_ge(qb_split[h], QC * (p + ropes_at[n] + 1))
                        else:
                            kept(ring, "wb", f"p{h}")
                            kept(ring, f"q{h}", f"p{h}")
                        o = ring_bank(ring, f"p{h}")
                        if rope:
                            mms = parts_product(o[:, 0:HT], [[w[:, c, :] for w in ww] for c in range(QC)],
                                                [[v[:, c, half(h)] for v in qbs] for c in range(QC)])
                            for k, mm in enumerate(mms):
                                if h == 0 and k == 0:
                                    mm.then_inc(w_used["w_q"], 1)
                        else:
                            mm = pe.matmul(o[:, 0:HT], wb[:, :], q_t[:, half(h)], start=True, stop=True)
                        mm.then_inc(ring_ready, 1)

                    def fold_out(name):
                        if name == "v0":
                            pe.wait_ge(w_in["w_vo"], 16 * (ga + 1))
                        o = ring_bank(ring, name)
                        k, width = int(name[1]), D // outs_of[n]
                        pe.matmul(o[:, 0:width], w_vo[:, 0:DC], w_vo[:, DC + k * width:DC + (k + 1) * width],
                                  start=True, stop=True).then_inc(ring_ready, 1)

                    def project(name, g):
                        m = int(name[1])
                        h, c = m // C, m % C
                        if c == 0:
                            pe.wait_ge(ctx_kept, g * HALVES + h + 1)
                            if h == 0:
                                kept(ring, "v0", name)
                                if not rope:
                                    kept(ring, "v1", name)
                        o = ring_bank(ring, name)
                        mms = parts_product(o[:, 0:HT], [[w[:, c * P:(c + 1) * P] for w in vo]], [[v[:, half(h)] for v in ctxs]])
                        for k, mm in enumerate(mms):
                            if m == 1 and k == 0:
                                mm.then_inc(w_used["w_vo"], 1)
                        mm.then_inc(ring_ready, 1)

                    def use(name):
                        if name == "ww":
                            fold_scores()
                        elif name == "wb":
                            fold_b()
                        elif name[0] == "q":
                            q(int(name[1]))
                        elif name[0] in "abc":
                            big(name)
                        elif name[0] == "p":
                            folded_query(int(name[1]))
                        elif name[0] == "v":
                            fold_out(name)
                        elif name[0] == "o":
                            project(name, ga)
                        elif name[0] == "t":
                            project(name, gl)

                    def scores(b):
                        if b == 0:
                            if n == 0 and last is None:
                                pe.wait_ge(kv_split, 1)
                            pe.wait_ge(qp_lo, 2 * ga + 1)
                        if b == BH:
                            pe.wait_ge(qp_lo, 2 * ga + 2)
                        mms = parts_product(bank[4 + b % 2][0:S, 0:LE], [[v[:, queries(b)] for v in qps]],
                                            [[v[:, b, :] for v in kvs]])
                        for mm in mms:
                            pass
                        mm.then_inc(scores_ready, 1)

                    def turn(g, b):
                        if not (isinstance(g, int) and g * B + b == 0):
                            pe.wait_ge(probs_t_ready, g * B + b)
                        pe.wait_ge(probs_ready, g * B + b + 1)
                        for c in range(KC):
                            mm = pe.transpose(bank[6][0:KP, c * S:(c + 1) * S], probs[:, b % 2, c * KP:(c + 1) * KP],
                                              ident[0:S, 0:S])
                        mm.then_inc(turned_ready, 1)

                    def values(g, b):
                        if n == 0 and last is None and b == 0:
                            pe.wait_ge(rope_r_step, B + 2)
                        if b % BH == 0 and not (isinstance(g, int) and g + b == 0):
                            pe.wait_ge(ctx_kept, g * HALVES + b // BH)
                        pe.wait_ge(probs_t_ready, g * B + b + 1)
                        for c in range(KC):
                            mm = pe.matmul(bank[7][:, (b % BH) * S:(b % BH + 1) * S], kv_r[:, b, c, :],
                                           probs_t[:, b % 2, c, :], start=(c == 0), stop=(c == KC - 1))
                        if b % BH == BH - 1:
                            mm.then_inc(ctx_ready, 1)

                    for b, (before, after) in enumerate(slots):
                        if a is not None:
                            scores(b)
                        for name in before:
                            use(name)
                        g, behind = (ga, b - 1) if b else (gl, B - 1)
                        if g is not None:
                            turn(g, behind)
                        for name in after:
                            use(name)
                        g, behind = (ga, b - 2) if b > 1 else (gl, B + b - 2)
                        if g is not None:
                            values(g, behind)

                pe.wait_ge(x_split[0], C * (splits_before[s] + 1))
                run_latent(pe, table[n], ring_at[f"lat{n}"], head)

            def glu_layer(n, name, s):
                r0, at0, E = rounds_at[name], ring_at[name], GLU_E[n]
                rg = 0 if n == 0 else GLU_N[0] // 2
                N = GLU_N[n] // 2
                pe.wait_ge(ln_done, HALVES * C * (s + 1))
                if n == 0:
                    pe.wait_ge(gates_loaded, 16 * 4)
                for b in range(B):
                    for c in range(C):
                        mm = pe.matmul(bank[4][0:S, b * E:(b + 1) * E], xn[:, c, queries(b)], gate_w[n][:, c, :],
                                       start=(c == 0), stop=(c == C - 1))
                mm.then_inc(logits_ready, 1)

                def hidden(i, h, j, first):
                    ring = Ring(GLU_HALF, at0 + h * len(GLU_HALF), 2 * len(GLU_HALF), i)
                    if h == 0:
                        pe.wait_ge(gu_split[j], i + r0 + 1)
                        if first:
                            pe.wait_ge(x_split[0], C * (splits_before[s] + 1))
                    elif first and j == 0:
                        pe.wait_ge(x_split[1], C * (splits_before[s] + 1))
                    for k, kind in enumerate("gu"):
                        o = ring_bank(ring, f"{kind}{j}")
                        mms = parts_product(o[:, 0:HT], [[w[:, j, k * C + c, :] for w in ws_gu] for c in range(C)],
                                            [[v[:, c, half(h)] for v in xs] for c in range(C)])
                        for m, mm in enumerate(mms):
                            if h == 1 and j == 0 and k == 0 and m == 0 and not first:
                                mm.then_inc(dn_used, 1)
                            if h == 1 and j == 1 and k == 0 and m == 0:
                                mm.then_inc(gu_used[0], 1)
                        mm.then_inc(ring_ready, 1)

                def shares(i, h):
                    ring = Ring(GLU_HALF, at0 + h * len(GLU_HALF), 2 * len(GLU_HALF), i)
                    if h == 0:
                        pe.wait_ge(sel_kept, i + rg + 1)
                    for j in range(2):
                        o = ring_bank(ring, f"s{j}")
                        pe.matmul(o[:, 0:HT], sel[:, j, :], comb_t[:, half(h)], start=True, stop=True)\
                          .then_inc(ring_ready, 1)

                def turn_comb():
                    pe.wait_ge(route_step, route_end[n])
                    for b in range(B):
                        mm = pe.transpose(bank[5 + b // BH][0:E + 1, (b % BH) * S:(b % BH + 1) * S],
                                          comb[n][:, b, :], ident[0:S, 0:S])
                        if b % BH == BH - 1:
                            mm.then_inc(comb_turned, 1)
                    pe.wait_ge(comb_kept, 2 * (n + 1))

                def body(i, first):
                    hidden(i, 0, 0, first)
                    hidden(i, 0, 1, first)
                    if first:
                        turn_comb()
                    shares(i, 0)
                    if not first:
                        down(i - 1, 1, r0, ws_dn, [])
                    hidden(i, 1, 0, first)
                    hidden(i, 1, 1, first)
                    shares(i, 1)
                    down(i, 0, r0, ws_dn, [(dn_split, i + r0 + 1)])

                body(0, True)
                with pe.Fori(1, N) as i:
                    body(i, False)
                down(N - 1, 1, r0, ws_dn, [])

            def down(i, h, r0, ws, needs):
                u = 2 * (i + r0) + h
                for s_, v_ in needs:
                    pe.wait_ge(s_, v_)
                pe.wait_ge(hid_ready, 2 * u + 2)
                for c in range(C):
                    if not (isinstance(u, int) and u == 0):
                        pe.wait_ge(down_added, C * (u - 1) + c + 1)
                    mms = parts_product(bank[4 + c][:, 0:HT], [[w[:, j, c * P:(c + 1) * P] for w in ws] for j in range(2)],
                                        [[v[:, h, j, :] for v in hids] for j in range(2)])
                    for m, mm in enumerate(mms):
                        if h == 0 and c == 0 and m == 0:
                            mm.then_inc(gu_used[1], 1)
                        if h == 0 and c == 1 and m == 0:
                            mm.then_inc(sel_used, 1)
                    mm.then_inc(down_ready, 1)

            def plain_attention(s):
                pe.wait_ge(ln_done, HALVES * C * (s + 1))
                pe.wait_ge(w1_loaded, 16 * N_W1)
                with pe.Fori(0, B) as b:
                    here = bass.ds(b * S, S)
                    for m in range(C):
                        for c in range(C):
                            mm = pe.matmul(bank[0][:, m * S:(m + 1) * S], w1q_s[:, c, m * P:(m + 1) * P],
                                           xn[:, c, here], start=(c == 0), stop=(c == C - 1))
                    mm.then_inc(q1_ready, 1)
                    for m in range(C):
                        mm = pe.matmul(bank[1][:, m * S:(m + 1) * S], w1kv_s[:, m * P:(m + 1) * P],
                                       raw_s[:, bass.ds(b, 1), :].rearrange("p a s -> p (a s)"), start=True, stop=True)
                    mm.then_inc(q1_ready, 1)
                    pe.wait_ge(raw_b_ready, b + 1)
                    pe.matmul(bank[2][0:S, :], raw_b[:, :], w1kv_s[:, D:2 * D], start=True, stop=True).then_inc(q1_ready, 1)
                    pe.wait_ge(q1_kept, 3 * b + 2)
                    for r in range(4):
                        for c in range(C):
                            mm = pe.matmul(bank[4 + r][0:S, c * S:(c + 1) * S], q1[r * HD1:(r + 1) * HD1, c, :],
                                           k1[r * HD1:(r + 1) * HD1, c, :], start=True, stop=True)
                        mm.then_inc(s1_ready, 1)
                    pe.wait_ge(q1_kept, 3 * b + 3)
                    for r in range(4):
                        pe.wait_ge(s1_norm, 4 * b + r + 1)
                        for c in range(C):
                            mm = pe.transpose(bank[r % 2][0:S, c * S:(c + 1) * S], s1[:, r, c * S:(c + 1) * S],
                                              ident[0:S, 0:S])
                        mm.then_inc(p1_turned, 1)
                        pe.wait_ge(p1_kept, 4 * b + r + 1)
                        for c in range(C):
                            mm = pe.matmul(bank[3][r * HD1:(r + 1) * HD1, c * S:(c + 1) * S],
                                           v1[:, c * P + r * HD1:c * P + (r + 1) * HD1],
                                           pt1[:, r % 2, c * S:(c + 1) * S], start=True, stop=True)
                    mm.then_inc(c1_ready, 1)
                    pe.wait_ge(c1_kept, b + 1)
                    for m in range(C):
                        for c in range(C):
                            mm = pe.matmul(bank[2][:, m * S:(m + 1) * S], w1o_s[:, c, m * P:(m + 1) * P],
                                           c1[:, c * S:(c + 1) * S], start=(c == 0), stop=(c == C - 1))
                    mm.then_inc(o1_ready, 1)
                    pe.wait_ge(o1_added, b + 1)

            def sign_layer(s):
                r0, at0, N = rounds_at["sgn"], ring_at["sgn"], SGN_N // 2
                pe.wait_ge(ln_done, HALVES * C * (s + 1))

                def hidden(i, h, first):
                    ring = Ring(SIGN_ROUND, at0, 4, i)
                    for j in range(2):
                        if h == 0:
                            pe.wait_ge(gu_split[j], i + r0 + 1)
                            if first and j == 0:
                                pe.wait_ge(x_split[0], C * (splits_before[s] + 1))
                        elif first and j == 0:
                            pe.wait_ge(x_split[1], C * (splits_before[s] + 1))
                        o = ring_bank(ring, f"{h}{j}")
                        mms = parts_product(o[:, 0:HT], [[ws_gu[0][:, j, c, :]] for c in range(C)],
                                            [[v[:, c, half(h)] for v in xs] for c in range(C)])
                        for m, mm in enumerate(mms):
                            if h == 1 and j == 0 and m == 0 and not first:
                                mm.then_inc(dn_used, 1)
                            if h == 1 and j == 1 and m == 0:
                                mm.then_inc(gu_used[0], 1)
                        mm.then_inc(ring_ready, 1)

                def body(i, first):
                    hidden(i, 0, first)
                    if not first:
                        down(i - 1, 1, r0, ws_dn[0:1], [])
                    hidden(i, 1, first)
                    down(i, 0, r0, ws_dn[0:1], [(dn_split, i + r0 + 1)])

                body(0, True)
                with pe.Fori(1, N) as i:
                    body(i, False)
                down(N - 1, 1, r0, ws_dn[0:1], [])

            def ternary_layer(s):
                pe.wait_ge(ln_done, HALVES * C * (s + 1))
                pe.wait_ge(w2_tern, W2_STEPS)
                for h in range(HALVES):
                    for m in range(C):
                        for c in range(C):
                            mm = pe.matmul(bank[h * C + m][:, 0:HT], w2s[:, c, m * P:(m + 1) * P], xn[:, c, half(h)],
                                           start=(c == 0), stop=(c == C - 1))
                        mm.then_inc(t2_ready, 1)

            layer_norm(0)
            latent_attention(0, True, 0)
            pe.wait_ge(w2_step, 2)
            pe.matmul(bank[7][:, 0:1], one[:, :], w2m[:, 0:1], start=True, stop=True).then_inc(w2_sum, 1)
            if STAGES > 1:
                layer_norm(1)
                glu_layer(0, "glu0", 1)
            if STAGES > 2:
                layer_norm(2)
                plain_attention(2)
            if STAGES > 3:
                layer_norm(3)
                sign_layer(3)
            if STAGES > 4:
                layer_norm(4)
                latent_attention(1, False, 4)
            if STAGES > 5:
                layer_norm(5)
                ternary_layer(5)
            if STAGES > 6:
                layer_norm(6)
                latent_attention(2, True, 6)
            if STAGES > 7:
                layer_norm(7)
                glu_layer(1, "glu1", 7)

        @block.scalar
        def _(act):
            def squares(s):
                for h in range(HALVES):
                    for c in range(C):
                        act.wait_ge(ln_centred, HALVES * C * s + C * h + c + 1)
                        act.activation(sq[:, c, half(h)], xn[:, c, half(h)], ACT.Square).then_inc(ln_squared, 1)
                for h in range(HALVES if s in splits_before else 0):
                    for c in range(C):
                        act.wait_ge(ln_done, HALVES * C * s + C * h + c + 1)
                        act.activation(x_hi[:, c, half(h)], xn[:, c, half(h)], ACT.Copy).then_inc(x_hi_set, 1)

            def keep(ring, name, out, width):
                act.wait_ge(ring_ready, ring.count(name))
                rows = out.shape[0]
                act.activation(out, bank[ring.bank(name)][0:rows, 0:width], ACT.Copy)\
                   .then_inc(bank_free[ring.bank(name)], 1)

            def latent_attention(n, rope):
                def split_query_weights(g, p):
                    act.wait_ge(w_in["w_q"], 16 * (g + 1))
                    if not (isinstance(g, int) and g == 0):
                        act.wait_ge(w_used["w_q"], g)
                    act.activation(ws_q[0][:, :, :], w_q[:, :, :], ACT.Copy).then_inc(q_hi, 1)

                def head(ring, slots, p, a, last, more):
                    gp_ = None if p is None else p + n * HEADS
                    ga = None if a is None else a + n * HEADS
                    gl = None if last is None else last + n * HEADS

                    def high(name, out, width, done):
                        act.wait_ge(ring_ready, ring.count(name))
                        act.activation(out, bank[ring.bank(name)][:, 0:width], ACT.Copy).then_inc(done, 1)

                    def use(name):
                        if name == "ww" and rope:
                            high("ww", ww[0][:, :, :].rearrange("p c d -> p (c d)"), QC * DC, ww_hi)
                        elif name == "ww":
                            keep(ring, "ww", ww_f[:, :, :].rearrange("p c d -> p (c d)"), QC * DC)
                        elif name == "wb":
                            keep(ring, "wb", wb[:, :], DC)
                        elif name[0] == "q":
                            keep(ring, name, q_t[:, half(int(name[1]))], HT)
                        elif name[0] == "p":
                            h = int(name[1])
                            keep(ring, name, qp[:, half(h)], HT)
                            act.wait_ge(bank_free[ring.bank(name)], ring.uses_before(name) + 1)
                            act.activation(qps[0][:, half(h)], qp[:, half(h)], ACT.Copy).then_inc(qp_hi, 1)
                        elif name[0] == "v":
                            width = D // outs_of[n]
                            k = int(name[1])
                            high(name, vo[0][:, k * width:(k + 1) * width], width, vo_hi)

                    def turned_high(h):
                        for c in range(QC):
                            act.wait_ge(rope_added, 6 * (p + ropes_at[n]) + 3 * h + c + 1)
                            act.activation(qbs[0][:, c, half(h)], qb[:, c, half(h)], ACT.Copy).then_inc(qb_hi, 1)

                    def exponent(b):
                        act.wait_ge(max_ready, ga * B + b + 1)
                        act.activation(probs[:, b % 2, :], bank[4 + b % 2][0:S, 0:L], ACT.Exp, bias=nmax[:, b:b + 1],
                                       scale=1.0, accum_out=psum_e[:, b:b + 1]).then_inc(exp_ready, 1)

                    def keep_turned(g, b):
                        act.wait_ge(turned_ready, g * B + b + 1)
                        act.activation(probs_t[:, b % 2, :, :].rearrange("k c s -> k (c s)"), bank[6][0:KP, 0:KC * S],
                                       ACT.Copy).then_inc(probs_t_ready, 1)

                    def high_ctx(g, h):
                        act.wait_ge(ctx_ready, g * HALVES + h + 1)
                        act.activation(ctxs[0][:, half(h)], bank[7][:, 0:HT], ACT.Copy).then_inc(ctx_hi, 1)

                    for b, (before, after) in enumerate(slots):
                        g, behind = (ga, b - 1) if b else (gl, B - 1)
                        if n == 0 and a is None and last is None and b == 2:
                            act.wait_ge(rope_k_step, 2)
                            act.wait_ge(rope_t_step, 1)
                            act.activation(kvs[0][:, :, :], kv_t[:, :, :], ACT.Copy).then_inc(kv_hi, 1)
                        if b == 2 and gl is not None:
                            high_ctx(gl, 1)
                        if b == BH + 2 and a is not None:
                            high_ctx(ga, 0)
                        if a is not None:
                            exponent(b)
                        for name in before:
                            use(name)
                        if g is not None:
                            keep_turned(g, behind)
                        for name in after:
                            use(name)
                        if p is not None and rope and b in HIGH_AFTER:
                            turned_high(HIGH_AFTER.index(b))
                        if more and b == 6:
                            split_query_weights(gp_ + 1, p)

                split_query_weights(n * HEADS, 0)
                run_latent(act, table[n], ring_at[f"lat{n}"], head)

            def early_split(n, j, rg, r0):
                act.wait_ge(gu_in[j], 16 * (rg + 1))
                if r0:
                    act.wait_ge(gu_used[j], r0)
                act.activation(ws_gu[0][:, j, :, :], w_gu[:, j, :, :], ACT.Copy).then_inc(gu_hi[j], 1)

            def keep_selection(i, rg, r0):
                act.wait_ge(sel_in, 16 * (i + rg + 1))
                if not (isinstance(i, int) and i + r0 == 0):
                    act.wait_ge(sel_used, i + r0)
                act.activation(sel[:, :, :], w_sel[:, :, :], ACT.Copy).then_inc(sel_kept, 1)

            def glu_layer(n, name):
                at0, E, N = ring_at[name], GLU_E[n], GLU_N[n] // 2
                rg = 0 if n == 0 else GLU_N[0] // 2
                for j in range(2):
                    early_split(n, j, rg, rounds_at[name])
                keep_selection(0, rg, rounds_at[name])
                if n == 0:
                    act.wait_ge(route_step, 2)
                    act.activation(rt[n][0][:, :, :], rt[n][0][:, :, :], ACT.Exp).then_inc(route_act, 1)
                else:
                    act.wait_ge(logits_ready, 2)
                    act.activation(rt[n][1][:, :, :].rearrange("s b e -> s (b e)"), bank[4][0:S, 0:B * E],
                                   ACT.Sigmoid).then_inc(route_act, 1)

                r0 = rounds_at[name]

                def split_first(i, j):
                    act.wait_ge(gu_in[j], 16 * (i + rg + 1))
                    if not (isinstance(i, int) and i + r0 == 0):
                        act.wait_ge(gu_used[j], i + r0)
                    act.activation(ws_gu[0][:, j, :, :], w_gu[:, j, :, :], ACT.Copy).then_inc(gu_hi[j], 1)

                def split_second(i):
                    act.wait_ge(dn_in, 16 * (i + rg + 1))
                    if not (isinstance(i, int) and i + r0 == 0):
                        act.wait_ge(dn_used, i + r0)
                    act.activation(ws_dn[0][:, :, :], w_dn[:, :, 0:D], ACT.Copy).then_inc(dn_hi, 1)

                def body(i, first, more):
                    for h in range(HALVES):
                        ring = Ring(GLU_HALF, at0 + h * len(GLU_HALF), 2 * len(GLU_HALF), i)
                        for j in range(2):
                            act.wait_ge(ring_ready, ring.count(f"g{j}"))
                            act.activation(silu[:, j, :], bank[ring.bank(f"g{j}")][:, 0:HT], ACT.Silu)\
                               .then_inc(bank_free[ring.bank(f"g{j}")], 1)
                            if h == 1 and j == 0:
                                split_second(i)
                                if more:
                                    split_first(i + 1, 0)
                        if first and h == 0:
                            for k in range(2):
                                act.wait_ge(comb_turned, 2 * n + k + 1)
                                act.activation(comb_t[0:E + 1, half(k)], bank[5 + k][0:E + 1, 0:HT], ACT.Copy)\
                                   .then_inc(comb_hi, 1)
                        for j in range(2):
                            if not (first and h == 0 and n == 0):
                                act.wait_ge(hid_made, 4 * (i + rg) + 2 * (h - 1) + j + 1)
                            keep(ring, f"s{j}", share[:, j, :], HT)
                        high_rows(i, h, r0, [(hid_made, 4 * (i + rg) + 2 * h + j + 1) for j in range(2)])
                        if h == 1 and more:
                            keep_selection(i + 1, rg, r0)
                            split_first(i + 1, 1)

                body(0, True, True)
                with act.Fori(1, N - 1) as i:
                    body(i, False, True)
                body(N - 1, False, False)

            def high_rows(i, h, r0, needs):
                for j in range(2):
                    act.wait_ge(*needs[j])
                    act.activation(hids[0][:, h, j, :], hid[:, h, j, :], ACT.Copy).then_inc(hid_hi, 1)

            def plain_attention():
                with act.Fori(0, B) as b:
                    act.wait_ge(q1_ready, 3 * b + 1)
                    act.activation(q1[:, :, :].rearrange("p c s -> p (c s)"), bank[0][:, 0:C * S], ACT.Copy).then_inc(q1_kept, 1)
                    act.wait_ge(q1_ready, 3 * b + 2)
                    act.activation(k1[:, :, :].rearrange("p c s -> p (c s)"), bank[1][:, 0:C * S], ACT.Copy).then_inc(q1_kept, 1)
                    act.wait_ge(q1_ready, 3 * b + 3)
                    act.activation(v1[:, :], bank[2][0:S, :], ACT.Copy).then_inc(q1_kept, 1)
                    for r in range(5):
                        if r < 4:
                            act.wait_ge(s1_shift, 4 * b + r + 1)
                            act.activation(s1[:, r, :], s1[:, r, :], ACT.Exp).then_inc(s1_exp, 1)
                        if r > 0:
                            act.wait_ge(p1_turned, 4 * b + r)
                            act.activation(pt1[:, (r - 1) % 2, :], bank[(r - 1) % 2][0:S, 0:4 * S], ACT.Copy).then_inc(p1_kept, 1)
                    act.wait_ge(c1_ready, b + 1)
                    act.activation(c1[:, :], bank[3][:, 0:C * S], ACT.Copy).then_inc(c1_kept, 1)

            def sign_layer():
                r0, at0, N = rounds_at["sgn"], ring_at["sgn"], SGN_N // 2
                
                def sign_first(i, j):
                    act.wait_ge(up_in[j], 16 * (i + 1))
                    act.wait_ge(gu_used[j], i + r0)
                    act.activation(ws_gu[0][:, j, 0:C, :], w_gu[:, j, 0:C, :], ACT.Sign).then_inc(gu_split[j], 1)

                def body(i, more):
                    ring = Ring(SIGN_ROUND, at0, 4, i)
                    act.wait_ge(dn1_in, 16 * (i + 1))
                    act.wait_ge(bank_free[ring.bank("11")], ring.uses_before("11"))
                    act.activation(sup[:, :], w_dn[:, :, D], ACT.Copy).then_inc(sup_kept, 1)
                    act.wait_ge(sup_kept, i + 1)
                    for h in range(HALVES):
                        for j in range(2):
                            act.wait_ge(ring_ready, ring.count(f"{h}{j}"))
                            act.activation(hid[:, h, j, :], bank[ring.bank(f"{h}{j}")][:, 0:HT], ACT.Relu,
                                           scale=sup[:, j:j + 1])\
                               .then_inc(bank_free[ring.bank(f"{h}{j}")], 1)
                            if h == 1 and j == 0:
                                act.wait_ge(dn_used, i + r0)
                                act.activation(ws_dn[0][:, :, :], w_dn[:, :, 0:D], ACT.Sign).then_inc(dn_split, 1)
                                if more:
                                    sign_first(i + 1, 0)
                        high_rows(i, h, r0, [(bank_free[ring.bank(f"{h}{j}")], ring.uses_before(f"{h}{j}") + 1)
                                             for j in range(2)])
                        if h == 1 and more:
                            sign_first(i + 1, 1)

                for j in range(2):
                    sign_first(0, j)
                with act.Fori(0, N - 1) as i:
                    body(i, True)
                body(N - 1, False)

            squares(0)
            latent_attention(0, True)
            if STAGES > 1:
                squares(1)
                glu_layer(0, "glu0")
            if STAGES > 2:
                squares(2)
                plain_attention()
            if STAGES > 3:
                squares(3)
                sign_layer()
            if STAGES > 4:
                squares(4)
                latent_attention(1, False)
            if STAGES > 5:
                squares(5)
            if STAGES > 6:
                squares(6)
                latent_attention(2, True)
            if STAGES > 7:
                squares(7)
                glu_layer(1, "glu1")

        @block.vector
        def _(dve):
            def layer_norm(s):
                n0 = 6 * s
                layer_input_ready(dve, s)
                for h in range(HALVES):
                    dve.wait_ge(ln_mean, HALVES * s + h + 1)
                    for c in range(C):
                        dve.tensor_tensor(xn[:, c, half(h)], x[:, c, half(h)], bank[h][:, 0:HT], ALU.subtract)\
                           .then_inc(ln_centred, 1)
                    for k, (to, c) in enumerate(((0, 1), (2, 3), (0, 2))):
                        if k < 2:
                            dve.wait_ge(ln_squared, HALVES * C * s + C * h + c + 1)
                        else:
                            dve.wait_ge(ln_summed, 6 * s + 3 * h + k)
                        dve.tensor_tensor(sq[:, to, half(h)], sq[:, to, half(h)], sq[:, c, half(h)], ALU.add)\
                           .then_inc(ln_summed, 1)
                dve.wait_ge(ln_var, s + 1)
                dve.tensor_scalar(var[:, :], bank[2][0:S, 0:B], EPS, None, ALU.add).then_inc(ln_step, 1)
                dve.wait_ge(ln_pow, s + 1)
                dve.tensor_tensor(nwt[:, 1, :], nwt[:, 0, :], nwt[:, 0, :], ALU.mult).then_inc(ln_step, 1)
                dve.wait_ge(ln_step, n0 + 2)
                dve.tensor_tensor(nwt[:, 1, :], nwt[:, 1, :], var[:, :], ALU.mult).then_inc(ln_step, 1)
                dve.wait_ge(ln_step, n0 + 3)
                dve.tensor_scalar(nwt[:, 2, :], nwt[:, 1, :], -0.5, 1.5, ALU.mult, ALU.add).then_inc(ln_step, 1)
                dve.wait_ge(ln_step, n0 + 4)
                dve.tensor_tensor(rstd[:, :], nwt[:, 0, :], nwt[:, 2, :], ALU.mult).then_inc(ln_step, 1)
                dve.wait_ge(ln_step, n0 + 5)
                dve.tensor_tensor(diag[:, :, :], ident[0:S, 0:S].unsqueeze(1).broadcast_to([S, B, S]),
                                  rstd[:, :].unsqueeze(2).broadcast_to([S, B, S]), ALU.mult).then_inc(ln_step, 1)
                for h in range(HALVES):
                    dve.wait_ge(ln_spread, HALVES * s + h + 1)
                    for c in range(C):
                        dve.tensor_tensor(xn[:, c, half(h)], xn[:, c, half(h)], bank[3 + h][:, 0:HT], ALU.mult)\
                           .then_inc(ln_done, 1)
                for c in range(C if s in splits_before else 0):
                    dve.wait_ge(x_hi_set, HALVES * C * splits_before[s] + c + 1)
                    dve.tensor_tensor(x_lo[:, c, half(0)], xn[:, c, half(0)], x_hi[:, c, half(0)].bitcast(F32),
                                      ALU.subtract).then_inc(x_split[0], 1)

            def add_to_x(h, c, psum):
                return dve.tensor_tensor(x[:, c, half(h)], x[:, c, half(h)], psum, ALU.add)

            def latent_attention(n, rope):
                def head(ring, slots, p, a, last, more):
                    ga = None if a is None else a + n * HEADS
                    gl = None if last is None else last + n * HEADS

                    def low(name, out, high, width, done, count):
                        k = ring.bank(name)
                        dve.wait_ge(done, count)
                        dve.tensor_tensor(out, bank[k][:, 0:width], high.bitcast(F32), ALU.subtract).then_inc(bank_free[k], 1)

                    def turn_query(name):
                        c, h = "abc".index(name[0]), int(name[1])
                        o = bank[ring.bank(name)]
                        free = bank_free[ring.bank(name)]
                        dve.wait_ge(ring_ready, ring.count(name))

                        def product(out, lo, hi, kind, tlo):
                            t = rope_q[tlo:tlo + hi - lo, kind, c if kind == 0 or c == 2 else 1 - c, :]
                            return dve.tensor_tensor(out.rearrange("p (b s) -> p b s", b=BH),
                                                     o[lo:hi, 0:HT].rearrange("p (b s) -> p b s", b=BH),
                                                     t.unsqueeze(1).broadcast_to([hi - lo, BH, S]), ALU.mult)

                        product(qb[:, c, half(h)], 0, P, 0, 0)
                        before = 6 * (p + ropes_at[n]) + 3 * h
                        if not (isinstance(before, int) and before == 0):
                            dve.wait_ge(rope_added, before)
                        if c < 2:
                            product(turned[:, 1 - c, :], 0, P, 1, 0).then_inc(free, 1)
                        else:
                            product(turned[0:R, 2, :], R, P, 1, 0)
                            product(turned[R:P, 2, :], 0, R, 1, R).then_inc(free, 1)

                    def add_out(name):
                        k, m = ring.bank(name), int(name[1])
                        dve.wait_ge(ring_ready, ring.count(name))
                        add_to_x(m // C, m % C, bank[k][:, 0:HT]).then_inc(bank_free[k], 1)

                    def use(name):
                        if name == "ww" and rope:
                            low("ww", ww[1][:, :, :].rearrange("p c d -> p (c d)"),
                                ww[0][:, :, :].rearrange("p c d -> p (c d)"), QC * DC, ww_hi, p + ropes_at[n] + 1)
                        elif name[0] in "abc":
                            turn_query(name)
                        elif name[0] == "v":
                            k, width = int(name[1]), D // outs_of[n]
                            cols = slice(k * width, (k + 1) * width)
                            low(name, vo[1][:, cols], vo[0][:, cols], width, vo_hi, outs_at[n] + outs_of[n] * a + k + 1)
                        elif name[0] in "ot":
                            add_out(name)

                    def row_max(b):
                        dve.wait_ge(scores_ready, ga * B + b + 1)
                        dve.tensor_reduce(nmax[:, b:b + 1], bank[4 + b % 2][0:S, 0:L], AX_X, ALU.max, negate=True)\
                           .then_inc(max_ready, 1)

                    def normalise(b):
                        G = ga * B + b
                        dve.wait_ge(exp_ready, G + 1)
                        dve.reciprocal(prec[:, b:b + 1], psum_e[:, b:b + 1]).then_inc(rec_ready, 1)
                        dve.wait_ge(rec_ready, G + 1)
                        dve.tensor_scalar(probs[:, b % 2, :], probs[:, b % 2, :], prec[:, b:b + 1], None, ALU.mult)\
                           .then_inc(probs_ready, 1)

                    def low_turned():
                        for c in range(QC):
                            dve.wait_ge(qb_hi, 6 * (p + ropes_at[n]) + 3 + c + 1)
                            dve.tensor_tensor(qbs[1][:, c, half(1)], qb[:, c, half(1)], qbs[0][:, c, half(1)].bitcast(F32),
                                              ALU.subtract).then_inc(qb_split[1], 1)

                    def low_ctx(g, h):
                        dve.wait_ge(ctx_hi, g * HALVES + h + 1)
                        dve.tensor_tensor(ctxs[1][:, half(h)], bank[7][:, 0:HT], ctxs[0][:, half(h)].bitcast(F32),
                                          ALU.subtract).then_inc(ctx_kept, 1)

                    for b, (before, after) in enumerate(slots):
                        if b == 2 and gl is not None:
                            low_ctx(gl, 1)
                        if b == BH + 2 and a is not None:
                            low_ctx(ga, 0)
                        if a is not None:
                            row_max(b)
                        if b == HIGH_AFTER[1] + 1 and rope and p is not None:
                            low_turned()
                        for name in before:
                            use(name)
                        if a is not None:
                            normalise(b)
                        for name in after:
                            use(name)
                    if n == 0 and a is None and last is None:
                        context_rest()

                run_latent(dve, table[n], ring_at[f"lat{n}"], head)

            def route(n):
                E = GLU_E[n]
                done = [route_end[0] if n else 0]
                score, v, one1, one2, left = (rt[n][k] for k in range(1, 6))
                first = rt[n][0]
                m, den = rs[n][0], rs[n][1]

                def step(ins):
                    ins.then_inc(route_step, 1)
                    done[0] += 1
                    dve.wait_ge(route_step, done[0])

                def wide(t):
                    return t[:, :].unsqueeze(2).broadcast_to([S, B, E])

                rev = revio[n][:, :].unsqueeze(1).broadcast_to([S, B, E])
                logits = bank[4][0:S, 0:B * E].rearrange("s (b e) -> s b e", b=B)
                if n == 0:
                    dve.wait_ge(logits_ready, 1)
                    step(dve.tensor_reduce(m[:, :], logits, AX_X, ALU.max))
                    step(dve.tensor_tensor(first[:, :, :], logits, wide(m), ALU.subtract))
                    dve.wait_ge(route_act, 1)
                    step(dve.tensor_reduce(den[:, :], first[:, :, :], AX_X, ALU.add))
                    step(dve.reciprocal(rs[n][2][:, :], den[:, :]))
                    step(dve.tensor_tensor(score[:, :, :], first[:, :, :], wide(rs[n][2]), ALU.mult))
                    pick = score
                else:
                    dve.wait_ge(route_act, 2)
                    step(dve.tensor_tensor(first[:, :, :], score[:, :, :],
                                           ebias[:, :].unsqueeze(1).broadcast_to([S, B, E]), ALU.add))
                    pick = first
                for k, hot in enumerate((one1, one2)):
                    step(dve.tensor_reduce(m[:, :], pick[:, :, :], AX_X, ALU.max))
                    step(dve.tensor_tensor(v[:, :, :], pick[:, :, :], wide(m), ALU.is_equal))
                    step(dve.tensor_tensor(v[:, :, :], v[:, :, :], rev, ALU.mult))
                    step(dve.tensor_reduce(den[:, :], v[:, :, :], AX_X, ALU.max))
                    step(dve.tensor_tensor(hot[:, :, :], v[:, :, :], wide(den), ALU.is_equal))
                    if k == 0:
                        step(dve.scalar_tensor_tensor(left[:, :, :], hot[:, :, :], -HUGE, pick[:, :, :], ALU.mult, ALU.add))
                        pick = left
                step(dve.tensor_tensor(one1[:, :, :], one1[:, :, :], one2[:, :, :], ALU.add))
                step(dve.tensor_tensor(one1[:, :, :], one1[:, :, :], score[:, :, :], ALU.mult))
                step(dve.tensor_reduce(m[:, :], one1[:, :, :], AX_X, ALU.add))
                step(dve.tensor_scalar(m[:, :], m[:, :], 1e-20, None, ALU.add))
                step(dve.reciprocal(rs[n][3][:, :], m[:, :]))
                step(dve.tensor_tensor(comb[n][:, :, 0:E], one1[:, :, :], wide(rs[n][3]), ALU.mult))
                return done[0]

            def glu_layer(n, name):
                r0, at0, N, E1 = rounds_at[name], ring_at[name], GLU_N[n] // 2, GLU_E[n] + 1
                dve.tensor_scalar(comb_t[:, :].rearrange("e (a p) -> e a p", p=P),
                                  one[0:2 * LOW, :].unsqueeze(1).broadcast_to([2 * LOW, T // P, P]), 0.0, None, ALU.mult)
                assert route(n) == route_end[n]

                def rows(i, h):
                    ring = Ring(GLU_HALF, at0 + h * len(GLU_HALF), 2 * len(GLU_HALF), i)
                    for j in range(2):
                        k = ring.bank(f"u{j}")
                        dve.wait_ge(ring_ready, ring.count(f"u{j}"))
                        dve.wait_ge(bank_free[ring.bank(f"g{j}")], ring.uses_before(f"g{j}") + 1)
                        dve.tensor_tensor(hid[:, h, j, :], silu[:, j, :], bank[k][:, 0:HT], ALU.mult).then_inc(bank_free[k], 1)

                def body(i, first):
                    rows(i, 0)
                    if first:
                        for k in range(2):
                            dve.wait_ge(comb_hi, 2 * n + k + 1)
                            dve.tensor_tensor(comb_t[LOW:LOW + E1, half(k)], bank[5 + k][0:E1, 0:HT],
                                              comb_t[0:E1, half(k)].bitcast(F32), ALU.subtract).then_inc(comb_kept, 1)
                    if not first:
                        add_down(i - 1, 1, r0)
                    rows(i, 1)
                    add_down(i, 0, r0)

                body(0, True)
                with dve.Fori(1, N) as i:
                    body(i, False)
                add_down(N - 1, 1, r0)

            def add_down(i, h, r0, scale=None):
                for c in range(C):
                    k = C * (2 * (i + r0) + h) + c
                    dve.wait_ge(down_ready, k + 1)
                    if scale is None:
                        ins = add_to_x(h, c, bank[4 + c][:, 0:HT])
                    else:
                        ins = dve.scalar_tensor_tensor(x[:, c, half(h)], bank[4 + c][:, 0:HT], scale[:, c:c + 1],
                                                       x[:, c, half(h)], ALU.mult, ALU.add)
                    ins.then_inc(down_added, 1)

            def plain_attention():
                dve.wait_ge(mask_loaded, 16)
                with dve.Fori(0, B) as b:
                    for r in range(5):
                        if r < 4:
                            s4 = s1[:, r, :].rearrange("s (c k) -> s c k", c=4)
                            dve.wait_ge(s1_ready, 4 * b + r + 1)
                            dve.scalar_tensor_tensor(s4, bank[4 + r][0:S, 0:4 * S].rearrange("s (c k) -> s c k", c=4),
                                                     SCALE1, mask[:, :].unsqueeze(1).broadcast_to([S, 4, S]),
                                                     ALU.mult, ALU.add).then_inc(s1_masked, 1)
                            dve.wait_ge(s1_masked, 4 * b + r + 1)
                            dve.tensor_reduce(m1[:, r, :], s4, AX_X, ALU.max).then_inc(s1_max, 1)
                        if r > 0:
                            s4 = s1[:, r - 1, :].rearrange("s (c k) -> s c k", c=4)
                            dve.wait_ge(s1_exp, 4 * b + r)
                            dve.tensor_reduce(z1[:, r - 1, :], s4, AX_X, ALU.add).then_inc(s1_sum, 1)
                            dve.wait_ge(s1_sum, 4 * b + r)
                            dve.reciprocal(z1[:, r - 1, :], z1[:, r - 1, :]).then_inc(s1_rec, 1)
                    dve.wait_ge(o1_ready, b + 1)
                    here = bass.ds(b * S, S)
                    dve.tensor_tensor(x[:, :, here], x[:, :, here],
                                      bank[2][:, 0:C * S].rearrange("p (c s) -> p c s", c=C), ALU.add).then_inc(o1_added, 1)

            def sign_layer():
                r0, N = rounds_at["sgn"], SGN_N // 2
                dve.wait_ge(scales_loaded, 32)
                dve.tensor_scalar(sdo[:, :], sdn[:, :], s_out[:, 0:1], None, ALU.mult).then_inc(sdo_ready, 1)
                dve.wait_ge(sdo_ready, 1)
                add_down(0, 0, r0, sdo)
                with dve.Fori(1, N) as i:
                    add_down(i - 1, 1, r0, sdo)
                    add_down(i, 0, r0, sdo)
                add_down(N - 1, 1, r0, sdo)

            def ternary_layer():
                for h in range(HALVES):
                    for m in range(C):
                        dve.wait_ge(t2_ready, h * C + m + 1)
                        dve.scalar_tensor_tensor(x[:, m, half(h)], bank[h * C + m][:, 0:HT], w2b[:, m:m + 1],
                                                 x[:, m, half(h)], ALU.add, ALU.add).then_inc(t2_added, 1)

            dve.memset(ones[:, :], 1.0 / D).then_inc(consts_set, 1)
            dve.memset(one[:, :], 1.0).then_inc(consts_set, 1)
            dve.memset(comb[0][:, :, :], 1.0)
            dve.memset(comb[1][:, :, :], 1.0)
            dve.wait_ge(consts_loaded, 32)
            layer_norm(0)
            dve.wait_ge(ctx_loaded, 96)
            dve.wait_ge(rope_t_step, 1)
            dve.tensor_tensor(kv_t[:, :, 0:L], kv_t[:, :, 0:L],
                              rope_t[:, 0, :].unsqueeze(1).broadcast_to([P, B, L]), ALU.mult).then_inc(rope_k_step, 1)
            dve.wait_ge(rope_k_step, 1)
            dve.wait_ge(rope_t_step, 2)
            dve.tensor_tensor(kv_t[:, :, 0:L], kv_t[:, :, 0:L], rot_t[:, :, :], ALU.add).then_inc(rope_k_step, 1)
            dve.wait_ge(rope_k_step, 2)

            def context_rest():
                dve.wait_ge(kv_hi, 1)
                dve.tensor_tensor(kvs[1][:, :, :], kv_t[:, :, :], kvs[0][:, :, :].bitcast(F32), ALU.subtract)\
                   .then_inc(kv_split, 1)
                H2 = DC // 2
                for b in range(B):
                    dve.tensor_tensor(rot_r[:, b, :, 0:H2], kv_r[:, b, :, H2:DC], rope_r[:, 1, :, 0:H2], ALU.mult)
                    dve.tensor_tensor(rot_r[:, b, :, H2:DC], kv_r[:, b, :, 0:H2], rope_r[:, 1, :, H2:DC], ALU.mult)\
                       .then_inc(rope_r_step, 1)
                dve.wait_ge(rope_r_step, B)
                dve.tensor_tensor(kv_r[:, :, :, :], kv_r[:, :, :, :],
                                  rope_r[:, 0, :, :].unsqueeze(1).broadcast_to([KP, B, KC, DC]), ALU.mult)\
                   .then_inc(rope_r_step, 1)
                dve.wait_ge(rope_r_step, B + 1)
                dve.tensor_tensor(kv_r[:, :, :, :], kv_r[:, :, :, :], rot_r[:, :, :, :], ALU.add).then_inc(rope_r_step, 1)

            def ternary_scale():
                dve.wait_ge(w2_loaded, 16)
                dve.tensor_reduce(w2p[:, :], w2s[:, :, :].rearrange("p c (a d) -> p (c a) d", a=8), AX_X, ALU.add,
                                  apply_absolute_value=True).then_inc(w2_step, 1)
                dve.wait_ge(w2_step, 1)
                dve.tensor_reduce(w2m[:, 0:1], w2p[:, :], AX_X, ALU.add).then_inc(w2_step, 1)
                dve.wait_ge(w2_sum, 1)
                dve.tensor_scalar(w2m[:, 1:2], bank[7][:, 0:1], 1.0 / (D * D), None, ALU.mult).then_inc(w2_step, 1)
                dve.wait_ge(w2_step, 3)
                dve.tensor_scalar(w2m[:, 2:3], w2m[:, 1:2], 1e-10, None, ALU.add).then_inc(w2_step, 1)
                dve.wait_ge(w2_step, 4)
                dve.reciprocal(w2m[:, 3:4], w2m[:, 2:3]).then_inc(w2_step, 1)

            latent_attention(0, True)
            ternary_scale()
            if STAGES > 1:
                layer_norm(1)
                glu_layer(0, "glu0")
            if STAGES > 2:
                layer_norm(2)
                plain_attention()
            if STAGES > 3:
                layer_norm(3)
                sign_layer()
            if STAGES > 4:
                layer_norm(4)
                latent_attention(1, False)
            if STAGES > 5:
                layer_norm(5)
                ternary_layer()
            if STAGES > 6:
                layer_norm(6)
                latent_attention(2, True)
            if STAGES > 7:
                layer_norm(7)
                glu_layer(1, "glu1")

        @block.gpsimd
        def _(gp):
            def power(s):
                gp.wait_ge(ln_step, 6 * s + 1)
                gp.tensor_tensor(nwt[:, 0, :], var[:, :], half_pow[:, :], ALU.pow).then_inc(ln_pow, 1)

            def low_x(s):
                for c in range(C):
                    gp.wait_ge(x_hi_set, HALVES * C * splits_before[s] + C + c + 1)
                    gp.tensor_tensor(x_lo[:, c, half(1)], xn[:, c, half(1)], x_hi[:, c, half(1)].bitcast(F32),
                                     ALU.subtract).then_inc(x_split[1], 1)

            def latent_attention(n, rope):
                def low_query_weights(g):
                    gp.wait_ge(q_hi, g + 1)
                    gp.tensor_tensor(ws_q[1][:, :, :], w_q[:, :, :], ws_q[0][:, :, :].bitcast(F32), ALU.subtract)\
                      .then_inc(q_split, 1)

                def head(ring, slots, p, a, last, more):
                    def add_turned(h, name, chunks):
                        k = ring.bank(f"{name}{h}")
                        gp.wait_ge(bank_free[k], ring.uses_before(f"{name}{h}") + 1)
                        for c in chunks:
                            gp.tensor_tensor(qb[:, c, half(h)], qb[:, c, half(h)], turned[:, c, :], ALU.add)\
                              .then_inc(rope_added, 1)

                    def low_turned(h, chunks):
                        for c in chunks:
                            gp.wait_ge(qb_hi, 6 * (p + ropes_at[n]) + 3 * h + c + 1)
                            gp.tensor_tensor(qbs[1][:, c, half(h)], qb[:, c, half(h)], qbs[0][:, c, half(h)].bitcast(F32),
                                             ALU.subtract).then_inc(qb_split[h], 1)

                    def low_query(h):
                        gp.wait_ge(qp_hi, 2 * (p + n * HEADS) + h + 1)
                        gp.tensor_tensor(qps[1][:, half(h)], qp[:, half(h)], qps[0][:, half(h)].bitcast(F32),
                                         ALU.subtract).then_inc(qp_lo, 1)

                    if p is None:
                        return
                    if rope:
                        for h in range(HALVES):
                            gp.wait_ge(bank_free[ring.bank(f"a{h}")], ring.uses_before(f"a{h}") + 1)
                            add_turned(h, "b", (0, 1))
                            add_turned(h, "c", (2,))
                            if h == 0:
                                low_turned(h, (0, 1, 2))
                    low_query(0)
                    if more:
                        low_query_weights(p + n * HEADS + 1)
                    low_query(1)

                low_query_weights(n * HEADS)
                run_latent(gp, table[n], ring_at[f"lat{n}"], head)

            def low_first(j, i, rg, r0):
                gp.wait_ge(gu_hi[j], i + rg + 1)
                gp.tensor_tensor(ws_gu[1][:, j, :, :], w_gu[:, j, :, :], ws_gu[0][:, j, :, :].bitcast(F32), ALU.subtract)\
                  .then_inc(gu_split[j], 1)

            def low_rows(i, h, r0):
                for j in range(2):
                    gp.wait_ge(hid_hi, 4 * (i + r0) + 2 * h + j + 1)
                    gp.tensor_tensor(hids[1][:, h, j, :], hid[:, h, j, :], hids[0][:, h, j, :].bitcast(F32),
                                     ALU.subtract).then_inc(hid_ready, 1)

            def glu_layer(n, name):
                at0, N, r0 = ring_at[name], GLU_N[n] // 2, rounds_at[name]
                rg = 0 if n == 0 else GLU_N[0] // 2

                def body(i, more):
                    for h in range(HALVES):
                        ring = Ring(GLU_HALF, at0 + h * len(GLU_HALF), 2 * len(GLU_HALF), i)
                        if h == 1:
                            gp.wait_ge(dn_hi, i + rg + 1)
                            gp.tensor_tensor(ws_dn[1][:, :, :], w_dn[:, :, 0:D], ws_dn[0][:, :, :].bitcast(F32),
                                             ALU.subtract).then_inc(dn_split, 1)
                            if more:
                                low_first(0, i + 1, rg, r0)
                        for j in range(2):
                            for kind in "us":
                                gp.wait_ge(bank_free[ring.bank(f"{kind}{j}")], ring.uses_before(f"{kind}{j}") + 1)
                            gp.tensor_tensor(hid[:, h, j, :], hid[:, h, j, :], share[:, j, :], ALU.mult).then_inc(hid_made, 1)
                        low_rows(i, h, r0)
                    if more:
                        low_first(1, i + 1, rg, r0)

                with gp.Fori(0, N - 1) as i:
                    body(i, True)
                body(N - 1, False)

            def sign_layer():
                with gp.Fori(0, SGN_N // 2) as i:
                    for h in range(HALVES):
                        low_rows(i, h, rounds_at["sgn"])

            def plain_attention():
                with gp.Fori(0, B) as b:
                    gp.wait_ge(w1_loaded, 16 * N_W1)
                    gp.tensor_copy(raw_b[:, :], raw_s[:, bass.ds(b, 1), :].rearrange("p a s -> p (a s)")).then_inc(raw_b_ready, 1)
                    for r in range(5):
                        if r < 4:
                            s4 = s1[:, r, :].rearrange("s (c k) -> s c k", c=4)
                            gp.wait_ge(s1_max, 4 * b + r + 1)
                            gp.tensor_tensor(s4, s4, m1[:, r, :].unsqueeze(2).broadcast_to([S, 4, S]), ALU.subtract)\
                              .then_inc(s1_shift, 1)
                        if r > 0:
                            s4 = s1[:, r - 1, :].rearrange("s (c k) -> s c k", c=4)
                            gp.wait_ge(s1_rec, 4 * b + r)
                            gp.tensor_tensor(s4, s4, z1[:, r - 1, :].unsqueeze(2).broadcast_to([S, 4, S]), ALU.mult)\
                              .then_inc(s1_norm, 1)

            def ternary():
                gp.wait_ge(w2_step, 5)
                steps = [
                    lambda: gp.tensor_scalar(w2t[:, :, :], w2s[:, :, :], w2m[:, 3:4], MAGIC, ALU.mult, ALU.add),
                    lambda: gp.tensor_scalar(w2t[:, :, :], w2t[:, :, :], -MAGIC, 1.0, ALU.add, ALU.min),
                    lambda: gp.tensor_scalar(w2t[:, :, :], w2t[:, :, :], -1.0, w2m[:, 1:2], ALU.max, ALU.mult),
                    lambda: gp.tensor_tensor(w2t[:, :, :], w2t[:, :, :], w2s[:, :, :], ALU.subtract),
                    lambda: gp.tensor_tensor(w2s[:, :, :], w2s[:, :, :], w2t[:, :, :], ALU.add),
                ]
                for k, step in enumerate(steps):
                    if k:
                        gp.wait_ge(w2_tern, k)
                    step().then_inc(w2_tern, 1)

            gp.memset(half_pow[:, :], -0.5).then_inc(gp_set, 1)
            for n, e in enumerate(GLU_E):
                gp.iota(revio_i[n][:, :], pattern=[[-1, e]], base=e, channel_multiplier=0).then_inc(gp_set, 1)
            gp.wait_ge(gp_set, 3)
            for n in range(2):
                gp.tensor_copy(revio[n][:, :], revio_i[n][:, :]).then_inc(gp_set, 1)
            gp.memset(kv_t[:, :, L:LE], 0.0).then_inc(rope_t_step, 1)
            power(0)
            gp.wait_ge(ctx_loaded, 96)
            gp.tensor_tensor(rot_t[:, :, :], rot_t[:, :, :], rope_t[:, 1, :].unsqueeze(1).broadcast_to([P, B, L]), ALU.mult)\
              .then_inc(rope_t_step, 1)
            low_x(0)
            latent_attention(0, True)
            if STAGES > 1:
                power(1)
                low_x(1)
                for j in range(2):
                    low_first(j, 0, 0, 0)
                ternary()
                glu_layer(0, "glu0")
            if STAGES > 2:
                power(2)
                plain_attention()
            if STAGES > 3:
                power(3)
                low_x(3)
                sign_layer()
            if STAGES > 4:
                power(4)
                low_x(4)
                latent_attention(1, False)
            if STAGES > 5:
                power(5)
            if STAGES > 6:
                power(6)
                low_x(6)
                latent_attention(2, True)
            if STAGES > 7:
                power(7)
                low_x(7)
                for j in range(2):
                    low_first(j, 0, GLU_N[0] // 2, rounds_at["glu1"])
                glu_layer(1, "glu1")


def kernel(**inputs):
    import numpy as np
    import concourse.bacc as bacc
    from concourse import mybir as mb
    from concourse.bass_utils import run_bass_kernel_spmd as run

    nc = bacc.Bacc("TRN2", target_bir_lowering=False, num_devices=1)
    arrays = {}

    def arg(name, a):
        a = np.ascontiguousarray(a)
        arrays["in_" + name] = a
        return nc.dram_tensor("in_" + name, a.shape, mb.dt.from_np(a.dtype), kind="ExternalInput").ap()

    a = {k: np.asarray(v) for k, v in inputs.items()}

    def rope_tables(length, dim):
        inv = (np.float32(1.0) / np.float32(10000.0) ** (np.arange(0, dim, 2, dtype=np.float32) / np.float32(dim))).astype(np.float32)
        f = np.arange(length, dtype=np.float32)[:, None] * inv[None, :]
        return np.repeat(np.sin(f), 2, axis=-1).astype(np.float32), np.repeat(np.cos(f), 2, axis=-1).astype(np.float32)

    def query_order(w):
        return np.concatenate([w[..., 0:128], w[..., 192:320], w[..., 128:192], w[..., 320:384]], axis=-1)

    sin, cos = rope_tables(S, 384)
    turn = np.concatenate([-sin[:, :192], sin[:, 192:]], axis=1)
    tq = np.stack([query_order(cos), query_order(turn)])
    tabs_q = tq.reshape(2, S, 3, 128).transpose(3, 0, 2, 1)
    sin, cos = rope_tables(L, DC)
    turn = np.concatenate([-sin[:, :64], sin[:, 64:]], axis=1)
    tk = np.stack([cos, turn])
    tabs_k = tk.transpose(2, 0, 1)
    tabs_r = tk.reshape(2, KC, KP, DC).transpose(2, 0, 1, 3)
    mask = np.where(np.tril(np.ones((S, S), bool)), np.float32(0), np.float32(MASKED)).astype(np.float32)

    latent = []
    for n, name in enumerate(("L0", "L2", "L3")):
        w = {k: a[f"{name}_xattn_{k}"] for k in ("Wq", "w_kc_q", "w_kc_kv", "W_qr", "W_kr", "Wo")}
        q_rank = w["W_qr"].transpose(0, 2, 1)
        kc = w["w_kc_q"]
        if name != "L2":
            q_rank, kc = query_order(q_rank), query_order(kc)
            kc = kc.reshape(HEADS, P, QC, P)
        else:
            kc = kc.reshape(HEADS, P, QC, P).transpose(0, 3, 2, 1)
        latent.append({
            "qk": arg(f"{name}_qk", np.concatenate([q_rank, w["W_kr"].transpose(0, 2, 1)], axis=2)),
            "q": arg(f"{name}_q", w["Wq"].reshape(HEADS, P, C, P).transpose(0, 3, 2, 1)),
            "kc": arg(f"{name}_kc", kc),
            "vo": arg(f"{name}_vo", np.concatenate([w["w_kc_kv"], w["Wo"].reshape(D, HEADS, P).transpose(1, 2, 0)], axis=2)),
        })

    def pad(w):
        rows = -w.shape[0] % (2 * P)
        return np.concatenate([w, np.zeros((rows, w.shape[1]), np.float32)], axis=0) if rows else w

    def hidden_first(w):
        return pad(w).reshape(-1, P, C, P).transpose(0, 3, 2, 1)

    def hidden_second(w):
        return pad(w).reshape(-1, 2, P, D).transpose(0, 2, 1, 3)

    def selection(E, F, total):
        n = -(-total // (2 * P)) * 2 * P
        sel = np.zeros((n, 2 * LOW), np.float32)
        owner = np.minimum(np.arange(total) // F, E)
        sel[np.arange(total), owner] = 1.0
        sel[np.arange(total), LOW + owner] = 1.0
        return sel.reshape(-1, 2, P, 2 * LOW).transpose(0, 3, 1, 2)

    def gated(name, wg, wu, wd, E, F):
        gu = np.concatenate([hidden_first(wg), hidden_first(wu)], axis=2)
        return arg(f"{name}_gu", gu), arg(f"{name}_dn", hidden_second(wd)), arg(f"{name}_sel", selection(E, F, wg.shape[0]))

    E0, F0 = a["L0_ffn_w_gate"].shape[:2]
    g0 = gated("L0", np.concatenate([a["L0_ffn_w_gate"].reshape(-1, D), a["L0_ffn_sw_gate"]]),
               np.concatenate([a["L0_ffn_w_up"].reshape(-1, D), a["L0_ffn_sw_up"]]),
               np.concatenate([a["L0_ffn_w_down"].transpose(0, 2, 1).reshape(-1, D), a["L0_ffn_sw_down"].T]), E0, F0)
    eg = a["L3_ffn_experts_gate_up"]
    E3, F3 = eg.shape[0], eg.shape[2] // 2
    g3 = gated("L3", np.concatenate([eg[:, :, :F3].transpose(0, 2, 1).reshape(-1, D), a["L3_ffn_shared_gate_w"].T]),
               np.concatenate([eg[:, :, F3:].transpose(0, 2, 1).reshape(-1, D), a["L3_ffn_shared_up_w"].T]),
               np.concatenate([a["L3_ffn_experts_down"].reshape(-1, D), a["L3_ffn_shared_down_w"]]), E3, F3)

    def in_first(w):
        return w.reshape(w.shape[0], C, P).transpose(2, 1, 0)

    ctx = a["ctx_512"]
    out = nc.dram_tensor("out_x", (P, C, T), mb.dt.float32, kind="ExternalOutput").ap()
    build(nc,
          arg("x", a["x"].reshape(T, C, P).transpose(2, 1, 0)),
          arg("ctx_t", ctx.transpose(2, 0, 1)),
          arg("ctx_r", ctx.reshape(B, KC, KP, DC).transpose(2, 0, 1, 3)),
          arg("tabs_q", tabs_q), arg("tabs_k", tabs_k), arg("tabs_r", tabs_r),
          arg("mask", mask), arg("ident", np.eye(P, dtype=np.float32)),
          latent,
          [arg("gate0", in_first(a["L0_ffn_gate_weight"])), arg("gate3", in_first(a["L3_ffn_gate_w"].T))],
          arg("bias3", a["L3_ffn_expert_bias"]),
          [g0[0], g3[0]], [g0[1], g3[1]], [g0[2], g3[2]],
          arg("w1q", in_first(a["L1_xattn_Wq"])), arg("w1kv", a["L1_xattn_Wkv_expand"].T),
          arg("w1o", in_first(a["L1_xattn_Wout"])),
          arg("up1", hidden_first(a["L1_ffn_up_weight"])), arg("dn1", np.concatenate(
              [hidden_second(a["L1_ffn_down_weight"].T),
               a["L1_ffn_up_scale"].reshape(-1, 2, P).transpose(0, 2, 1)[..., None]], axis=3)),
          arg("dn1s", a["L1_ffn_down_scale"].reshape(C, P).T),
          arg("out1s", a["L1_ffn_output_scale"]),
          arg("w2", in_first(a["L2_ffn_weight"])), arg("b2", a["L2_ffn_bias"].reshape(C, P).T),
          out)
    r = run(nc, [arrays], core_ids=[0])
    return r.results[0]["out_x"].transpose(2, 1, 0).reshape(B, S, D)
```

```python
from contextlib import ExitStack

import concourse.bass as bass
from concourse import mybir

ALU = mybir.AluOpType
ACT = mybir.ActivationFunctionType
F32 = mybir.dt.float32
AX_X = mybir.AxisListType.X

B, S, D = 8, 112, 512
L, DC = 375, 128
T = B * S
P = 128
C = D // P
HALVES = 2
HT = T // HALVES
BH = B // HALVES
KC, KP = 3, L // 3
LE = L + L % 2
HEADS = 16
QC = 3
R = 64
H1, HD1 = 16, 32
EPS = 1e-5
HUGE = 3.0e38
MASKED = -3.0e38
MAGIC = 12582912.0

ROPE_SLOTS = [(["ww", "q0"], []), (["q1"], ["a0"]), (["b0"], ["c0"]), (["t4"], ["a1"]),
              (["b1"], ["t5", "t6"]), (["c1"], ["t7", "v0"]), (["p0"], ["o0", "o1"]), (["o2"], ["o3", "p1"])]
FOLD_SLOTS = [(["ww", "q0"], []), (["q1"], []), (["wb"], []), (["t4"], ["t5"]),
              (["t6"], ["t7"]), (["v0", "v1"], []), (["p0"], ["o0", "o1"]), (["o2"], ["o3", "p1"])]
SPLIT_AFTER = 5
HIGH_AFTER = {3: (0, (0, 1, 2)), 5: (1, (0, 1)), 6: (1, (2,))}
FOR_NEXT = ("ww", "q", "a", "b", "c", "wb", "p")
FOR_LAST = ("t",)


def slots_of(table, p, a, last):
    def keep(name):
        if name.startswith(FOR_NEXT):
            return p
        return last if name.startswith(FOR_LAST) else a
    return [tuple([n for n in part if keep(n)] for part in slot) for slot in table]


def names_of(slots):
    return [n for slot in slots for part in slot for n in part]


GLU_HALF = ["g0", "u0", "g1", "u1", "s0", "s1"]
SIGN_ROUND = ["00", "01", "10", "11"]
LOW = 32
NBANK = 4
SCALE1 = HD1 ** -0.5
W2_STEPS = 5
N_W1 = 4


class Ring:

    def __init__(self, names, at, per=0, i=0):
        self.at, self.per, self.i = at, per, i
        self.n = {name: k for k, name in enumerate(names)}

    def bank(self, name):
        return (self.at + self.n[name]) % NBANK

    def uses_before(self, name):
        return self.per // NBANK * self.i + (self.at + self.n[name]) // NBANK

    def count(self, name):
        return self.per * self.i + self.at + self.n[name] + 1


def latent_blocks(table, at):
    blocks = []
    for p, a, last, times in ((True, False, False, 1), (True, True, False, 1), (True, True, True, HEADS - 3),
                              (True, True, True, 1), (False, True, True, 1), (False, False, True, 1)):
        slots = slots_of(table, p, a, last)
        blocks.append((slots, at))
        at += len(names_of(slots)) * times
    return blocks, at


def run_latent(eng, table, at, head):
    (first, second, full, full_last, final, tail), _ = latent_blocks(table, at)
    head(Ring(names_of(first[0]), first[1]), first[0], 0, None, None, True)
    head(Ring(names_of(second[0]), second[1]), second[0], 1, 0, None, True)
    names = names_of(full[0])
    with eng.Fori(0, HEADS - 3) as i:
        head(Ring(names, full[1], len(names), i), full[0], i + 2, i + 1, i, True)
    head(Ring(names, full_last[1]), full_last[0], HEADS - 1, HEADS - 2, HEADS - 3, False)
    head(Ring(names_of(final[0]), final[1]), final[0], None, HEADS - 1, HEADS - 2, False)
    head(Ring(names_of(tail[0]), tail[1]), tail[0], None, None, HEADS - 1, False)


def run_batches(eng, batch):
    batch(0, 0, True)
    batch(1, 1, True)
    with eng.Fori(1, B // 2 - 1) as i:
        batch(2 * i, 0, True)
        batch(2 * i + 1, 1, True)
    batch(B - 2, 0, True)
    batch(B - 1, 1, False)


def build(nc, x_in, ctx_t, ctx_r, tabs_q, tabs_k, tabs_r, mask_in, ident_in,
          latent, gates, bias3, glu_gu, glu_dn, glu_sel, w1q, w1kv, w1o,
          up1, dn1, dn1s, out1s, w2, b2, out):
    GLU_E = [g.shape[2] for g in gates]
    GLU_N = [w.shape[0] for w in glu_gu]
    SGN_N = up1.shape[0]

    ctx = ExitStack()
    with ctx:
        def sb(name, shape, dt=F32):
            return ctx.enter_context(nc.sbuf_tensor(name, shape, dt))

        def sem(name):
            return ctx.enter_context(nc.semaphore(name))

        F32R = mybir.dt.float32r

        def parts(name, shape):
            return [sb(f"{name}_hi", shape, F32R), sb(f"{name}_lo", shape, F32R)]

        x = sb("x", [P, C, T])
        xn = sb("xn", [P, C, T])
        with nc.sbuf_tensor("sq", [P, C, T], F32) as sq:
            pass
        x_lo = sb("x_lo", [P, C, T], F32R)
        x_hi = sb("x_hi", [P, C, T], F32R)
        xs = [x_hi, x_lo]
        var = sb("var", [S, B])
        nwt = sb("nwt", [S, 3, B])
        rstd = sb("rstd", [S, B])
        half_pow = sb("half_pow", [S, B])
        diag = sb("diag", [S, B, S])
        ident = sb("ident", [P, P])
        ones = sb("ones", [P, P])
        one = sb("one", [P, P])
        mask = sb("mask", [S, S])
        kvs = parts("kv_t", [P, B, LE])
        kv_r = sb("kv_r", [KP, B, KC, DC])
        rope_q = sb("rope_q", [P, 2, QC, S])
        w2s = sb("w2s", [P, C, D])
        w2b = sb("w2b", [P, C])
        w2m = sb("w2m", [P, 4])
        w2p = sb("w2p", [P, C * 8])
        gate_w = [sb(f"gate_w{n}", [P, C, e]) for n, e in enumerate(GLU_E)]
        ebias = sb("ebias", [S, GLU_E[1]])
        revio_i = [sb(f"revio_i{n}", [S, e], mybir.dt.int32) for n, e in enumerate(GLU_E)]
        revio = [sb(f"revio{n}", [S, e]) for n, e in enumerate(GLU_E)]
        comb = [sb(f"comb{n}", [S, B, e + 1]) for n, e in enumerate(GLU_E)]
        sdn = sb("sdn", [P, C])
        s_out = sb("s_out", [P, 1])
        sdo = sb("sdo", [P, C])
        sup = sb("sup", [P, 2])
        w_qk = sb("w_qk", [R, QC * P + DC])
        w_q = sb("w_q", [P, C, P])
        w_kc = sb("w_kc", [P, QC, P])
        w_vo = sb("w_vo", [P, DC + D])
        with nc.sbuf_tensor("rot_r", [KP, B, KC, DC], F32) as rot_r, nc.sbuf_tensor("rope_r", [KP, 2, KC, DC], F32) as rope_r:
            pass
        w_gu = sb("w_gu", [P, 2, 2 * C, P])
        w_dn = sb("w_dn", [P, 2, D + 1])
        w_sel = sb("w_sel", [2 * LOW, 2, P])
        wb = sb("wb", [P, DC])
        ww_f = sb("ww_f", [P, QC, DC])

        with ExitStack() as space:
            def sb(name, shape, dt=F32):
                return space.enter_context(nc.sbuf_tensor(name, shape, dt))

            ws_q = parts("ws_q", [P, C, P])
            ww = parts("ww", [P, QC, DC])
            q_t = sb("q_t", [P, T])
            turned = sb("turned", [P, QC, HT])
            qp = sb("qp", [P, T])
            qps = parts("qp", [P, T])
            nmax = sb("nmax", [S, B])
            psum_e = sb("psum_e", [S, B])
            prec = sb("prec", [S, B])
            qbs = parts("qb", [P, QC, T])
            with ExitStack() as inner:
                def sb(name, shape, dt=F32):
                    return inner.enter_context(nc.sbuf_tensor(name, shape, dt))

                rot_t = sb("rot_t", [P, B, L])
                rope_t = sb("rope_t", [P, 2, L])
                kv_t = sb("kv_t", [P, B, LE])
            with ExitStack() as inner:
                qb = sb("qb", [P, QC, T])
                vo = parts("vo", [DC, D])
                ctxs = parts("ctx", [P, T])
                probs = sb("probs", [S, 2, L])
                probs_t = sb("probs_t", [KP, 2, KC, S])

        def sb(name, shape, dt=F32):
            return space.enter_context(nc.sbuf_tensor(name, shape, dt))

        with ExitStack() as space:
            ws_gu = parts("ws_gu", [P, 2, 2 * C, P])
            ws_dn = parts("ws_dn", [P, 2, D])
            silu = sb("silu", [P, 2, HT])
            share = sb("share", [P, 2, HT])
            hid = sb("hid", [P, HALVES, 2, HT])
            hids = parts("hid", [P, HALVES, 2, HT])
            sel = sb("sel", [2 * LOW, 2, P], F32R)
            comb_t = sb("comb_t", [2 * LOW, T], F32R)
            w2t = sb("w2t", [P, C, D])
            rt = [[sb(f"rt{n}_{k}", [S, B, e]) for k in range(6)] for n, e in enumerate(GLU_E)]
            rs = [[sb(f"rs{n}_{k}", [S, B]) for k in range(5)] for n in range(2)]
        with ExitStack() as space:
            q1 = sb("q1", [P, 2, C, S])
            k1 = sb("k1", [P, 2, C, S])
            v1 = sb("v1", [S, 2, D])
            s1 = sb("s1", [S, 4, 4 * S])
            pt1 = sb("pt1", [S, 2, 4 * S])
            c1 = sb("c1", [P, C * S])
            m1 = sb("m1", [S, 4, 4])
            z1 = sb("z1", [S, 4, 4])
            raw_s = sb("raw_s", [P, B, S])
            raw_b = sb("raw_b", [P, S])
            w1q_s = sb("w1q_s", [P, C, D])
            w1kv_s = sb("w1kv_s", [P, 2 * D])
            w1o_s = sb("w1o_s", [P, C, D])

        bank = [ctx.enter_context(nc.psum_tensor(f"bank{n}", [P, 512], F32)) for n in range(8)]

        x_loaded = sem("x_loaded")
        consts_loaded = sem("consts_loaded")
        mask_loaded = sem("mask_loaded")
        ctx_loaded = sem("ctx_loaded")
        w1_loaded = sem("w1_loaded")
        w2_loaded = sem("w2_loaded")
        scales_loaded = sem("scales_loaded")
        gates_loaded = sem("gates_loaded")
        consts_set = sem("consts_set")
        gp_set = sem("gp_set")
        rope_r_step = sem("rope_r_step")
        rope_t_step, rope_k_step = sem("rope_t_step"), sem("rope_k_step")
        w2_step = sem("w2_step")
        w2_sum = sem("w2_sum")
        ln_mean = sem("ln_mean")
        ln_centred = sem("ln_centred")
        ln_squared = sem("ln_squared")
        ln_summed = sem("ln_summed")
        ln_var = sem("ln_var")
        ln_step = [sem(f"ln_step{h}") for h in range(HALVES)]
        ln_pow = sem("ln_pow")
        ln_spread = sem("ln_spread")
        ln_done = sem("ln_done")
        ring_ready = sem("ring_ready")
        bank_free = [sem(f"bank_free{n}") for n in range(NBANK)]
        w_in = {k: sem(f"{k}_in") for k in ("w_qk", "w_q", "w_kc", "w_vo")}
        w_used = {k: sem(f"{k}_used") for k in ("w_qk", "w_kc", "w_vo")}
        q_hi, q_split = sem("q_hi"), sem("q_split")
        qp_lo = sem("qp_lo")
        ww_hi, qp_hi, vo_hi, ctx_hi = sem("ww_hi"), sem("qp_hi"), sem("vo_hi"), sem("ctx_hi")
        x_hi_set, x_split = sem("x_hi_set"), [sem(f"x_split{h}") for h in range(HALVES)]
        qb_hi, qb_split = sem("qb_hi"), [sem(f"qb_split{h}") for h in range(HALVES)]
        kv_hi, kv_split = sem("kv_hi"), sem("kv_split")
        gu_hi = [sem(f"gu_hi{j}") for j in range(2)]
        gu_split = [sem(f"gu_split{j}") for j in range(2)]
        dn_hi, dn_split = sem("dn_hi"), sem("dn_split")
        hid_made, hid_hi = sem("hid_made"), sem("hid_hi")
        rope_added = sem("rope_added")
        scores_ready = sem("scores_ready")
        max_ready = sem("max_ready")
        exp_ready = sem("exp_ready")
        rec_ready = sem("rec_ready")
        probs_ready = sem("probs_ready")
        turned_ready = sem("turned_ready")
        probs_t_ready = sem("probs_t_ready")
        ctx_ready = sem("ctx_ready")
        ctx_kept = sem("ctx_kept")
        gu_in = [sem(f"gu_in{j}") for j in range(2)]
        sel_in, sel_kept, sel_used = sem("sel_in"), sem("sel_kept"), sem("sel_used")
        raw_b_ready = sem("raw_b_ready")
        w2_tern = sem("w2_tern")
        gu_used = [sem(f"gu_used{j}") for j in range(2)]
        dn_in = sem("dn_in")
        dn_used = sem("dn_used")
        hid_ready = sem("hid_ready")
        down_ready = sem("down_ready")
        down_added = sem("down_added")
        logits_ready = sem("logits_ready")
        route_act = sem("route_act")
        route_step = sem("route_step")
        comb_turned = sem("comb_turned")
        comb_hi, comb_kept = sem("comb_hi"), sem("comb_kept")
        q1_ready, q1_kept = sem("q1_ready"), sem("q1_kept")
        s1_ready, s1_masked, s1_max = sem("s1_ready"), sem("s1_masked"), sem("s1_max")
        s1_exp, s1_rec, s1_norm = sem("s1_exp"), sem("s1_rec"), sem("s1_norm")
        p1_turned, p1_kept = sem("p1_turned"), sem("p1_kept")
        c1_ready, c1_kept = sem("c1_ready"), sem("c1_kept")
        o1_ready, o1_added = sem("o1_ready"), sem("o1_added")
        up_in = [sem(f"up_in{j}") for j in range(2)]
        dn1_in = sem("dn1_in")
        sdo_ready = sem("sdo_ready")
        sup_kept = sem("sup_kept")
        t2_ready, t2_added = sem("t2_ready"), sem("t2_added")
        out_done = sem("out_done")

        block = ctx.enter_context(nc.Block())

        ring_at = {}
        at = 0
        ring_at["lat0"] = at
        at = latent_blocks(ROPE_SLOTS, at)[1]
        ring_at["glu0"] = at
        at += GLU_N[0] // 2 * 2 * len(GLU_HALF)
        ring_at["sgn"] = at
        at += SGN_N // 2 * 4
        ring_at["lat1"] = at
        at = latent_blocks(FOLD_SLOTS, at)[1]
        ring_at["lat2"] = at
        at = latent_blocks(ROPE_SLOTS, at)[1]
        ring_at["glu1"] = at
        at += GLU_N[1] // 2 * 2 * len(GLU_HALF)
        ring_at["end"] = at
        assert all(v % NBANK == 0 for v in ring_at.values())
        ring_after = {"lat0": "glu0", "glu0": "sgn", "sgn": "lat1", "lat1": "lat2", "lat2": "glu1", "glu1": "end"}
        rounds_at = {"glu0": 0, "sgn": GLU_N[0] // 2, "glu1": GLU_N[0] // 2 + SGN_N // 2}
        rounds_all = rounds_at["glu1"] + GLU_N[1] // 2
        table = {0: ROPE_SLOTS, 1: FOLD_SLOTS, 2: ROPE_SLOTS}
        ropes_at = {0: 0, 1: HEADS, 2: HEADS}
        outs_at = {0: 0, 1: HEADS, 2: 3 * HEADS}
        outs_of = {0: 1, 1: 2, 2: 1}
        route_end = [22, 22 + 18]

        splits_before = {0: 0, 1: 1, 3: 2, 4: 3, 6: 4, 7: 5}

        def half(h):
            return slice(h * HT, (h + 1) * HT)

        def queries(b):
            return slice(b * S, (b + 1) * S)

        def layer_input_ready(eng, stage, early=False):
            if stage == 0:
                eng.wait_ge(x_loaded, 16)
            elif stage in (1, 5, 7):
                layer = {1: "lat0", 5: "lat1", 7: "lat2"}[stage]
                for n in range(NBANK):
                    eng.wait_ge(bank_free[n], ring_at[ring_after[layer]] // NBANK - (1 if early and n else 0))
            elif stage in (2, 4, 8):
                rounds = {2: rounds_at["sgn"], 4: rounds_at["glu1"], 8: rounds_all}[stage]
                eng.wait_ge(down_added, rounds * 2 * C - (C if early else 0))
            elif stage == 3:
                eng.wait_ge(o1_added, B)
            elif stage == 6:
                eng.wait_ge(t2_added, C if early else HALVES * C)

        @block.sync
        def _(sp):
            sp.dma_start(x[:, :, :], x_in).then_inc(x_loaded, 16)
            sp.dma_start(ident[:, :], ident_in).then_inc(consts_loaded, 16)
            sp.dma_start(rope_q[:, :, :, :], tabs_q).then_inc(consts_loaded, 16)

            def context_loads():
                sp.dma_start(rot_t[0:DC // 2, :, :], ctx_t[DC // 2:DC]).then_inc(ctx_loaded, 16)
                sp.dma_start(rot_t[DC // 2:DC, :, :], ctx_t[0:DC // 2]).then_inc(ctx_loaded, 16)
                sp.dma_start(rope_t[:, :, :], tabs_k).then_inc(ctx_loaded, 16)
                sp.dma_start(kv_t[:, :, 0:L], ctx_t).then_inc(ctx_loaded, 16)
                sp.dma_start(kv_r[:, :, :, :], ctx_r).then_inc(ctx_loaded, 16)
                sp.dma_start(rope_r[:, :, :, :], tabs_r).then_inc(ctx_loaded, 16)

            def latent_loads(n):
                w = latent[n]

                def query_loads(h, g):
                    if n or not isinstance(g, int) or g:
                        sp.wait_ge(w_used["w_qk"], g)
                    sp.dma_start(w_qk[:, :], w["qk"][h]).then_inc(w_in["w_qk"], 16)
                    if n or not isinstance(g, int) or g:
                        sp.wait_ge(q_split, g)
                    sp.dma_start(w_q[:, :, :], w["q"][h]).then_inc(w_in["w_q"], 16)

                def fold_load(h, g):
                    sp.wait_ge(w_used["w_kc"], g + 1)
                    sp.dma_start(w_kc[:, :, :], w["kc"][h]).then_inc(w_in["w_kc"], 16)

                def output_load(h, g):
                    if n or not isinstance(g, int) or g:
                        sp.wait_ge(w_used["w_vo"], g)
                    sp.dma_start(w_vo[:, :], w["vo"][h]).then_inc(w_in["w_vo"], 16)

                at = n * HEADS
                query_loads(0, at)
                if n == 0:
                    context_loads()
                    small_loads()
                fold_load(0, at)
                query_loads(1, at + 1)
                output_load(0, at)
                with sp.Fori(1, HEADS - 1) as h:
                    fold_load(h, h + at)
                    query_loads(h + 1, h + at + 1)
                    output_load(h, h + at)
                fold_load(HEADS - 1, at + HEADS - 1)
                output_load(HEADS - 1, at + HEADS - 1)

            def glu_loads(n, name):
                r0 = rounds_at[name]
                g0 = 0 if n == 0 else GLU_N[0] // 2

                def load(i, first):
                    for j in range(2):
                        if not first:
                            sp.wait_ge(gu_split[j], i + r0)
                        sp.dma_start(w_gu[:, j, :, :], glu_gu[n][2 * i + j]).then_inc(gu_in[j], 16)
                    if n or not first:
                        sp.wait_ge(sel_kept, i + g0)
                    sp.dma_start(w_sel[:, :, :], glu_sel[n][i]).then_inc(sel_in, 16)
                    if not first:
                        sp.wait_ge(dn_split, i + r0)
                    sp.dma_start(w_dn[:, :, 0:D], glu_dn[n][i]).then_inc(dn_in, 16)

                load(0, r0 == 0)
                with sp.Fori(1, GLU_N[n] // 2) as i:
                    load(i, False)

            def sign_loads():
                def load(i):
                    for j in range(2):
                        sp.wait_ge(gu_split[j], i + rounds_at["sgn"])
                        sp.dma_start(w_gu[:, j, 0:C, :], up1[2 * i + j]).then_inc(up_in[j], 16)
                    sp.wait_ge(dn_split, i + rounds_at["sgn"])
                    sp.dma_start(w_dn[:, :, :], dn1[i]).then_inc(dn1_in, 16)

                with sp.Fori(0, SGN_N // 2) as i:
                    load(i)

            def small_loads():
                sp.dma_start(w2s[:, :, :], w2).then_inc(w2_loaded, 16)
                sp.dma_start(w2b[:, :], b2).then_inc(gates_loaded, 16)
                sp.dma_start(mask[:, :], mask_in).then_inc(mask_loaded, 16)
                for n in range(2):
                    sp.dma_start(gate_w[n][:, :, :], gates[n]).then_inc(gates_loaded, 16)
                sp.dma_start(ebias[:, :], bias3.partition_broadcast(S)).then_inc(gates_loaded, 16)
                sp.dma_start(sdn[:, :], dn1s).then_inc(scales_loaded, 16)
                sp.dma_start(s_out[:, :], out1s.partition_broadcast(P)).then_inc(scales_loaded, 16)

            latent_loads(0)
            sp.wait_ge(rope_r_step, B + 2)
            glu_loads(0, "glu0")
            layer_input_ready(sp, 2)
            sp.dma_start(raw_s[:, :, :], ctx_t[:, :, 0:S]).then_inc(w1_loaded, 16)
            sp.dma_start(w1q_s[:, :, :], w1q).then_inc(w1_loaded, 16)
            sp.dma_start(w1kv_s[:, :], w1kv).then_inc(w1_loaded, 16)
            sp.dma_start(w1o_s[:, :, :], w1o).then_inc(w1_loaded, 16)
            sign_loads()
            latent_loads(1)
            latent_loads(2)
            glu_loads(1, "glu1")
            layer_input_ready(sp, 8)
            sp.dma_start(out, x[:, :, :]).then_inc(out_done, 16)
            sp.wait_ge(out_done, 16)

        @block.tensor
        def _(pe):
            def layer_norm(s):
                if s == 0:
                    pe.wait_ge(consts_set, 2)
                for h in range(HALVES):
                    layer_input_ready(pe, s, early=(h == 0))
                    for c in range(C):
                        mm = pe.matmul(bank[h][:, 0:HT], ones[:, :], x[:, c, half(h)], start=(c == 0), stop=(c == C - 1))
                        if s in (2, 4) and h == 0 and c == 0:
                            mm.then_inc(dn_used, 1)
                    mm.then_inc(ln_mean, 1)
                for b in range(B):
                    if b % BH == 0:
                        pe.wait_ge(ln_summed, 6 * s + 3 * (b // BH + 1))
                    mm = pe.matmul(bank[2][0:S, b:b + 1], sq[:, 0, queries(b)], ones[:, 0:1], start=True, stop=True)
                    if b % BH == BH - 1:
                        mm.then_inc(ln_var, 1)
                for h in range(HALVES):
                    pe.wait_ge(ln_step[h], 6 * s + 6)
                    pe.matmul(bank[3 + h][:, 0:HT], one[0:S, :],
                              diag[:, h * BH:(h + 1) * BH, :].rearrange("s b t -> s (b t)"),
                              start=True, stop=True).then_inc(ln_spread, 1)

            def ring_bank(ring, name):
                k = ring.bank(name)
                pe.wait_ge(bank_free[k], ring.uses_before(name))
                return bank[k]

            def kept(ring, name, before=None):
                if before is None or ring.bank(before) != ring.bank(name):
                    pe.wait_ge(bank_free[ring.bank(name)], ring.uses_before(name) + 1)

            def parts_product(out, ws, xs_):
                for k, (w, v) in enumerate(zip(ws, xs_)):
                    for m, (a, b) in enumerate(((0, 0), (0, 1), (1, 0))[:3 if len(w) == 2 else 2]):
                        mm = pe.matmul(out, w[a], v[b], start=(k == 0 and m == 0),
                                       stop=(k == len(ws) - 1 and m == (2 if len(w) == 2 else 1)))
                        yield mm

            def latent_attention(n, rope, s):
                def head(ring, slots, p, a, last, more):
                    gp_ = None if p is None else p + n * HEADS
                    ga = None if a is None else a + n * HEADS
                    gl = None if last is None else last + n * HEADS

                    def fold_scores():
                        pe.wait_ge(w_in["w_qk"], 16 * (gp_ + 1))
                        o = ring_bank(ring, "ww")
                        for c in range(QC):
                            mm = pe.matmul(o[:, c * DC:(c + 1) * DC], w_qk[:, c * P:(c + 1) * P], w_qk[:, QC * P:],
                                           start=True, stop=True)
                        mm.then_inc(ring_ready, 1)

                    def q(h):
                        if h == 0:
                            pe.wait_ge(q_split, gp_ + 1)
                        if h == 1 and last is None and a is None:
                            pe.wait_ge(x_split[1], C * (splits_before[s] + 1))
                        o = ring_bank(ring, f"q{h}")
                        mms = parts_product(o[:, 0:HT], [[w[:, c, :] for w in ws_q] for c in range(C)],
                                            [[v[:, c, half(h)] for v in xs] for c in range(C)])
                        for k, mm in enumerate(mms):
                            if h == 0 and k == 0:
                                mm.then_inc(w_used["w_qk"], 1)
                            if h == 0 and k == 1:
                                mm.then_inc(w_used["w_kc"], 1)
                        mm.then_inc(ring_ready, 1)

                    def big(name):
                        c, h = "abc".index(name[0]), int(name[1])
                        if c == 0:
                            kept(ring, f"q{h}", name)
                            if h == 0:
                                pe.wait_ge(w_in["w_kc"], 16 * (gp_ + 1))
                        o = ring_bank(ring, name)
                        pe.matmul(o[:, 0:HT], w_kc[:, c, :], q_t[:, half(h)], start=True, stop=True).then_inc(ring_ready, 1)

                    def fold_b():
                        kept(ring, "ww", "wb")
                        pe.wait_ge(w_in["w_kc"], 16 * (gp_ + 1))
                        o = ring_bank(ring, "wb")
                        for c in range(QC):
                            mm = pe.matmul(o[:, 0:DC], w_kc[:, c, :], ww_f[:, c, :], start=(c == 0),
                                           stop=(c == QC - 1))
                        mm.then_inc(ring_ready, 1)

                    def folded_query(h):
                        if rope:
                            kept(ring, "ww", f"p{h}")
                            pe.wait_ge(qb_split[h], QC * (p + ropes_at[n] + 1))
                        else:
                            kept(ring, "wb", f"p{h}")
                            kept(ring, f"q{h}", f"p{h}")
                        o = ring_bank(ring, f"p{h}")
                        if rope:
                            mms = parts_product(o[:, 0:HT], [[w[:, c, :] for w in ww] for c in range(QC)],
                                                [[v[:, c, half(h)] for v in qbs] for c in range(QC)])
                            for mm in mms:
                                pass
                        else:
                            mm = pe.matmul(o[:, 0:HT], wb[:, :], q_t[:, half(h)], start=True, stop=True)
                        mm.then_inc(ring_ready, 1)

                    def fold_out(name):
                        if name == "v0":
                            pe.wait_ge(w_in["w_vo"], 16 * (ga + 1))
                        o = ring_bank(ring, name)
                        k, width = int(name[1]), D // outs_of[n]
                        pe.matmul(o[:, 0:width], w_vo[:, 0:DC], w_vo[:, DC + k * width:DC + (k + 1) * width],
                                  start=True, stop=True).then_inc(ring_ready, 1)

                    def project(name, g):
                        m = int(name[1])
                        h, c = m // C, m % C
                        if c == 0:
                            pe.wait_ge(ctx_kept, g * HALVES + h + 1)
                            if h == 0:
                                kept(ring, "v0", name)
                                if not rope:
                                    kept(ring, "v1", name)
                        o = ring_bank(ring, name)
                        mms = parts_product(o[:, 0:HT], [[w[:, c * P:(c + 1) * P] for w in vo]], [[v[:, half(h)] for v in ctxs]])
                        for k, mm in enumerate(mms):
                            if m == 1 and k == 0:
                                mm.then_inc(w_used["w_vo"], 1)
                        mm.then_inc(ring_ready, 1)

                    def use(name):
                        if name == "ww":
                            fold_scores()
                        elif name == "wb":
                            fold_b()
                        elif name[0] == "q":
                            q(int(name[1]))
                        elif name[0] in "abc":
                            big(name)
                        elif name[0] == "p":
                            folded_query(int(name[1]))
                        elif name[0] == "v":
                            fold_out(name)
                        elif name[0] == "o":
                            project(name, ga)
                        elif name[0] == "t":
                            project(name, gl)

                    def scores(b):
                        if b == 0:
                            if n == 0 and last is None:
                                pe.wait_ge(kv_split, 1)
                            pe.wait_ge(qp_lo, 2 * ga + 1)
                        if b == BH:
                            pe.wait_ge(qp_lo, 2 * ga + 2)
                        mms = parts_product(bank[4 + b % 2][0:S, 0:LE], [[v[:, queries(b)] for v in qps]],
                                            [[v[:, b, :] for v in kvs]])
                        for mm in mms:
                            pass
                        mm.then_inc(scores_ready, 1)

                    def turn(g, b):
                        if not (isinstance(g, int) and g * B + b == 0):
                            pe.wait_ge(probs_t_ready, g * B + b)
                        pe.wait_ge(probs_ready, g * B + b + 1)
                        for c in range(KC):
                            mm = pe.transpose(bank[6][0:KP, c * S:(c + 1) * S], probs[:, b % 2, c * KP:(c + 1) * KP],
                                              ident[0:S, 0:S])
                        mm.then_inc(turned_ready, 1)

                    def values(g, b):
                        if n == 0 and last is None and b == 0:
                            pe.wait_ge(rope_r_step, B + 2)
                        if b % BH == 0 and not (isinstance(g, int) and g + b == 0):
                            pe.wait_ge(ctx_kept, g * HALVES + b // BH)
                        pe.wait_ge(probs_t_ready, g * B + b + 1)
                        for c in range(KC):
                            mm = pe.matmul(bank[7][:, (b % BH) * S:(b % BH + 1) * S], kv_r[:, b, c, :],
                                           probs_t[:, b % 2, c, :], start=(c == 0), stop=(c == KC - 1))
                        if b % BH == BH - 1:
                            mm.then_inc(ctx_ready, 1)

                    for b, (before, after) in enumerate(slots):
                        if a is not None:
                            scores(b)
                        for name in before:
                            use(name)
                        g, behind = (ga, b - 1) if b else (gl, B - 1)
                        if g is not None:
                            turn(g, behind)
                        for name in after:
                            use(name)
                        g, behind = (ga, b - 2) if b > 1 else (gl, B + b - 2)
                        if g is not None:
                            values(g, behind)

                pe.wait_ge(x_split[0], C * (splits_before[s] + 1))
                run_latent(pe, table[n], ring_at[f"lat{n}"], head)

            def glu_layer(n, name, s):
                r0, at0, E = rounds_at[name], ring_at[name], GLU_E[n]
                rg = 0 if n == 0 else GLU_N[0] // 2
                N = GLU_N[n] // 2
                if n == 0:
                    pe.wait_ge(gates_loaded, 16 * 4)
                for b in range(B):
                    if b % BH == 0:
                        pe.wait_ge(ln_done, HALVES * C * s + C * (b // BH + 1))
                    for c in range(C):
                        mm = pe.matmul(bank[7][0:S, b * E:(b + 1) * E], xn[:, c, queries(b)], gate_w[n][:, c, :],
                                       start=(c == 0), stop=(c == C - 1))
                mm.then_inc(logits_ready, 1)
                if n == 0:
                    pe.wait_ge(w2_step, 2)
                    pe.matmul(bank[4][:, 0:1], one[:, :], w2m[:, 0:1], start=True, stop=True).then_inc(w2_sum, 1)

                def hidden(i, h, j, first):
                    ring = Ring(GLU_HALF, at0 + h * len(GLU_HALF), 2 * len(GLU_HALF), i)
                    if h == 0:
                        pe.wait_ge(gu_split[j], i + r0 + 1)
                        if first:
                            pe.wait_ge(x_split[0], C * (splits_before[s] + 1))
                    elif first and j == 0:
                        pe.wait_ge(x_split[1], C * (splits_before[s] + 1))
                    for k, kind in enumerate("gu"):
                        o = ring_bank(ring, f"{kind}{j}")
                        mms = parts_product(o[:, 0:HT], [[w[:, j, k * C + c, :] for w in ws_gu] for c in range(C)],
                                            [[v[:, c, half(h)] for v in xs] for c in range(C)])
                        for m, mm in enumerate(mms):
                            if h == 1 and j == 0 and k == 0 and m == 0 and not first:
                                mm.then_inc(dn_used, 1)
                            if h == 1 and j == 1 and k == 0 and m == 0:
                                mm.then_inc(gu_used[0], 1)
                        mm.then_inc(ring_ready, 1)

                def shares(i, h):
                    ring = Ring(GLU_HALF, at0 + h * len(GLU_HALF), 2 * len(GLU_HALF), i)
                    if h == 0:
                        pe.wait_ge(sel_kept, i + rg + 1)
                    for j in range(2):
                        o = ring_bank(ring, f"s{j}")
                        pe.matmul(o[:, 0:HT], sel[:, j, :], comb_t[:, half(h)], start=True, stop=True)\
                          .then_inc(ring_ready, 1)

                def turn_comb():
                    pe.wait_ge(route_step, route_end[n])
                    for b in range(B):
                        mm = pe.transpose(bank[5 + b // BH][0:E + 1, (b % BH) * S:(b % BH + 1) * S],
                                          comb[n][:, b, :], ident[0:S, 0:S])
                        if b % BH == BH - 1:
                            mm.then_inc(comb_turned, 1)
                    pe.wait_ge(comb_kept, 2 * (n + 1))

                def body(i, first):
                    hidden(i, 0, 0, first)
                    hidden(i, 0, 1, first)
                    if first:
                        turn_comb()
                    shares(i, 0)
                    if not first:
                        down(i - 1, 1, r0, ws_dn, [])
                    hidden(i, 1, 0, first)
                    hidden(i, 1, 1, first)
                    shares(i, 1)
                    down(i, 0, r0, ws_dn, [(dn_split, i + r0 + 1)])

                body(0, True)
                with pe.Fori(1, N) as i:
                    body(i, False)
                down(N - 1, 1, r0, ws_dn, [])

            def down(i, h, r0, ws, needs):
                u = 2 * (i + r0) + h
                for s_, v_ in needs:
                    pe.wait_ge(s_, v_)
                pe.wait_ge(hid_ready, 2 * u + 2)
                for c in range(C):
                    if not (isinstance(u, int) and u == 0):
                        pe.wait_ge(down_added, C * (u - 1) + c + 1)
                    mms = parts_product(bank[4 + c][:, 0:HT], [[w[:, j, c * P:(c + 1) * P] for w in ws] for j in range(2)],
                                        [[v[:, h, j, :] for v in hids] for j in range(2)])
                    for m, mm in enumerate(mms):
                        if h == 0 and c == 0 and m == 0:
                            mm.then_inc(gu_used[1], 1)
                        if h == 0 and c == 1 and m == 0:
                            mm.then_inc(sel_used, 1)
                    mm.then_inc(down_ready, 1)

            def plain_attention(s):
                def key(b, side):
                    for m in range(C):
                        mm = pe.matmul(bank[2][:, m * S:(m + 1) * S], w1kv_s[:, m * P:(m + 1) * P],
                                       raw_s[:, bass.ds(b, 1), :].rearrange("p a s -> p (a s)"), start=True, stop=True)
                    mm.then_inc(q1_ready, 1)

                def query(b, side):
                    for m in range(C):
                        for c in range(C):
                            mm = pe.matmul(bank[2][:, m * S:(m + 1) * S], w1q_s[:, c, m * P:(m + 1) * P],
                                           xn[:, c, bass.ds(b * S, S)], start=(c == 0), stop=(c == C - 1))
                    mm.then_inc(q1_ready, 1)

                def value(b, side):
                    pe.wait_ge(raw_b_ready, b + 1)
                    pe.matmul(bank[2][0:S, :], raw_b[:, :], w1kv_s[:, D:2 * D], start=True, stop=True).then_inc(q1_ready, 1)

                def project(b):
                    pe.wait_ge(c1_kept, b + 1)
                    for m in range(C):
                        for c in range(C):
                            mm = pe.matmul(bank[2][:, m * S:(m + 1) * S], w1o_s[:, c, m * P:(m + 1) * P],
                                           c1[:, c * S:(c + 1) * S], start=(c == 0), stop=(c == C - 1))
                    mm.then_inc(o1_ready, 1)

                def turn(G, r):
                    pe.wait_ge(s1_norm, G + 1)
                    for c in range(C):
                        mm = pe.transpose(bank[r % 2][0:S, c * S:(c + 1) * S], s1[:, r, c * S:(c + 1) * S],
                                          ident[0:S, 0:S])
                    mm.then_inc(p1_turned, 1)

                def values(b, side, r):
                    if r == 0 and not (isinstance(b, int) and b == 0):
                        pe.wait_ge(c1_kept, b)
                    pe.wait_ge(p1_kept, 4 * b + r + 1)
                    for c in range(C):
                        mm = pe.matmul(bank[3][r * HD1:(r + 1) * HD1, c * S:(c + 1) * S],
                                       v1[:, side, c * P + r * HD1:c * P + (r + 1) * HD1],
                                       pt1[:, r % 2, c * S:(c + 1) * S], start=True, stop=True)
                    if r == 3:
                        mm.then_inc(c1_ready, 1)

                def batch(b, side, more):
                    first = isinstance(b, int) and b == 0
                    for r in range(4):
                        if r == 0:
                            pe.wait_ge(q1_kept, 3 * b + 2)
                        if not first:
                            pe.wait_ge(s1_masked, 4 * b + r - 3)
                        for c in range(C):
                            mm = pe.matmul(bank[4 + r][0:S, c * S:(c + 1) * S], q1[r * HD1:(r + 1) * HD1, side, c, :],
                                           k1[r * HD1:(r + 1) * HD1, side, c, :], start=True, stop=True)
                        mm.then_inc(s1_ready, 1)
                        if r == 0:
                            pe.wait_ge(q1_kept, 3 * b + 3)
                        if r == 0 and more:
                            key(b + 1, 1 - side)
                        if r == 1 and more:
                            pe.wait_ge(q1_kept, 3 * b + 4)
                            query(b + 1, 1 - side)
                        if r == 2 and not first:
                            if more:
                                pe.wait_ge(q1_kept, 3 * b + 5)
                            project(b - 1)
                        if r == 3 and more:
                            if first:
                                pe.wait_ge(q1_kept, 3 * b + 5)
                            else:
                                pe.wait_ge(o1_added, b)
                            value(b + 1, 1 - side)
                        if not (first and r == 0):
                            turn(4 * b + r - 1, (r - 1) % 4)
                        if not (first and r < 2):
                            values(b if r > 1 else b - 1, side if r > 1 else 1 - side, (r - 2) % 4)

                pe.wait_ge(ln_done, HALVES * C * (s + 1))
                pe.wait_ge(w1_loaded, 16 * N_W1)
                key(0, 0)
                pe.wait_ge(q1_kept, 1)
                query(0, 0)
                pe.wait_ge(q1_kept, 2)
                value(0, 0)
                run_batches(pe, batch)
                turn(4 * B - 1, 3)
                values(B - 1, (B - 1) % 2, 2)
                values(B - 1, (B - 1) % 2, 3)
                pe.wait_ge(o1_added, B - 1)
                project(B - 1)

            def sign_layer(s):
                r0, at0, N = rounds_at["sgn"], ring_at["sgn"], SGN_N // 2
                pe.wait_ge(ln_done, HALVES * C * (s + 1))

                def hidden(i, h, first):
                    ring = Ring(SIGN_ROUND, at0, 4, i)
                    for j in range(2):
                        if h == 0:
                            pe.wait_ge(gu_split[j], i + r0 + 1)
                            if first and j == 0:
                                pe.wait_ge(x_split[0], C * (splits_before[s] + 1))
                        elif first and j == 0:
                            pe.wait_ge(x_split[1], C * (splits_before[s] + 1))
                        o = ring_bank(ring, f"{h}{j}")
                        mms = parts_product(o[:, 0:HT], [[ws_gu[0][:, j, c, :]] for c in range(C)],
                                            [[v[:, c, half(h)] for v in xs] for c in range(C)])
                        for m, mm in enumerate(mms):
                            if h == 1 and j == 0 and m == 0 and not first:
                                mm.then_inc(dn_used, 1)
                            if h == 1 and j == 1 and m == 0:
                                mm.then_inc(gu_used[0], 1)
                        mm.then_inc(ring_ready, 1)

                def body(i, first):
                    hidden(i, 0, first)
                    if not first:
                        down(i - 1, 1, r0, ws_dn[0:1], [])
                    hidden(i, 1, first)
                    down(i, 0, r0, ws_dn[0:1], [(dn_split, i + r0 + 1)])

                body(0, True)
                with pe.Fori(1, N) as i:
                    body(i, False)
                down(N - 1, 1, r0, ws_dn[0:1], [])

            def ternary_layer(s):
                pe.wait_ge(ln_done, HALVES * C * (s + 1))
                pe.wait_ge(w2_tern, W2_STEPS)
                for h in range(HALVES):
                    for m in range(C):
                        for c in range(C):
                            mm = pe.matmul(bank[h * C + m][:, 0:HT], w2s[:, c, m * P:(m + 1) * P], xn[:, c, half(h)],
                                           start=(c == 0), stop=(c == C - 1))
                        mm.then_inc(t2_ready, 1)

            layer_norm(0)
            latent_attention(0, True, 0)
            layer_norm(1)
            glu_layer(0, "glu0", 1)
            layer_norm(2)
            plain_attention(2)
            layer_norm(3)
            sign_layer(3)
            layer_norm(4)
            latent_attention(1, False, 4)
            layer_norm(5)
            ternary_layer(5)
            layer_norm(6)
            latent_attention(2, True, 6)
            layer_norm(7)
            glu_layer(1, "glu1", 7)

        @block.scalar
        def _(act):
            def squares(s, meanwhile):
                for h in range(HALVES):
                    for c in range(C):
                        act.wait_ge(ln_centred, HALVES * C * s + C * h + c + 1)
                        act.activation(sq[:, c, half(h)], xn[:, c, half(h)], ACT.Square).then_inc(ln_squared, 1)
                meanwhile()
                for h in range(HALVES if s in splits_before else 0):
                    for c in range(C):
                        act.wait_ge(ln_done, HALVES * C * s + C * h + c + 1)
                        act.activation(x_hi[:, c, half(h)], xn[:, c, half(h)], ACT.Copy).then_inc(x_hi_set, 1)

            def keep(ring, name, out, width):
                act.wait_ge(ring_ready, ring.count(name))
                rows = out.shape[0]
                act.activation(out, bank[ring.bank(name)][0:rows, 0:width], ACT.Copy)\
                   .then_inc(bank_free[ring.bank(name)], 1)

            def split_query_weights(g):
                act.wait_ge(w_in["w_q"], 16 * (g + 1))
                act.activation(ws_q[0][:, :, :], w_q[:, :, :], ACT.Copy).then_inc(q_hi, 1)

            def latent_attention(n, rope):
                def head(ring, slots, p, a, last, more):
                    gp_ = None if p is None else p + n * HEADS
                    ga = None if a is None else a + n * HEADS
                    gl = None if last is None else last + n * HEADS

                    def high(name, out, width, done):
                        act.wait_ge(ring_ready, ring.count(name))
                        act.activation(out, bank[ring.bank(name)][:, 0:width], ACT.Copy).then_inc(done, 1)

                    def use(name):
                        if name == "ww" and rope:
                            high("ww", ww[0][:, :, :].rearrange("p c d -> p (c d)"), QC * DC, ww_hi)
                        elif name == "ww":
                            keep(ring, "ww", ww_f[:, :, :].rearrange("p c d -> p (c d)"), QC * DC)
                        elif name == "wb":
                            keep(ring, "wb", wb[:, :], DC)
                        elif name[0] == "q":
                            keep(ring, name, q_t[:, half(int(name[1]))], HT)
                        elif name[0] == "p":
                            h = int(name[1])
                            keep(ring, name, qp[:, half(h)], HT)
                            act.wait_ge(bank_free[ring.bank(name)], ring.uses_before(name) + 1)
                            act.activation(qps[0][:, half(h)], qp[:, half(h)], ACT.Copy).then_inc(qp_hi, 1)
                        elif name[0] == "v":
                            width = D // outs_of[n]
                            k = int(name[1])
                            high(name, vo[0][:, k * width:(k + 1) * width], width, vo_hi)

                    def turned_high(h, chunks):
                        for c in chunks:
                            act.wait_ge(rope_added, 6 * (p + ropes_at[n]) + 3 * h + c + 1)
                            act.activation(qbs[0][:, c, half(h)], qb[:, c, half(h)], ACT.Copy).then_inc(qb_hi, 1)

                    def exponent(b):
                        act.wait_ge(max_ready, ga * B + b + 1)
                        act.activation(probs[:, b % 2, :], bank[4 + b % 2][0:S, 0:L], ACT.Exp, bias=nmax[:, b:b + 1],
                                       scale=1.0, accum_out=psum_e[:, b:b + 1]).then_inc(exp_ready, 1)

                    def keep_turned(g, b):
                        act.wait_ge(turned_ready, g * B + b + 1)
                        act.activation(probs_t[:, b % 2, :, :].rearrange("k c s -> k (c s)"), bank[6][0:KP, 0:KC * S],
                                       ACT.Copy).then_inc(probs_t_ready, 1)

                    def high_ctx(g, h):
                        act.wait_ge(ctx_ready, g * HALVES + h + 1)
                        act.activation(ctxs[0][:, half(h)], bank[7][:, 0:HT], ACT.Copy).then_inc(ctx_hi, 1)

                    for b, (before, after) in enumerate(slots):
                        g, behind = (ga, b - 1) if b else (gl, B - 1)
                        if n == 0 and a is None and last is None and b == 2:
                            act.wait_ge(rope_k_step, 2)
                            act.wait_ge(rope_t_step, 1)
                            act.activation(kvs[0][:, :, :], kv_t[:, :, :], ACT.Copy).then_inc(kv_hi, 1)
                        if b == 2 and gl is not None:
                            high_ctx(gl, 1)
                        if b == BH + 2 and a is not None:
                            high_ctx(ga, 0)
                        if a is not None:
                            exponent(b)
                        for name in before:
                            use(name)
                        if g is not None:
                            keep_turned(g, behind)
                        for name in after:
                            use(name)
                        if p is not None and rope and b in HIGH_AFTER:
                            turned_high(*HIGH_AFTER[b])
                        if more and b == SPLIT_AFTER:
                            split_query_weights(gp_ + 1)

                run_latent(act, table[n], ring_at[f"lat{n}"], head)

            def first_round(n, name):
                rg = 0 if n == 0 else GLU_N[0] // 2
                for j in range(2):
                    split_first(0, j, rg, rounds_at[name])
                keep_selection(0, rg, rounds_at[name])

            def split_first(i, j, rg, r0):
                act.wait_ge(gu_in[j], 16 * (i + rg + 1))
                if not (isinstance(i, int) and i + r0 == 0):
                    act.wait_ge(gu_used[j], i + r0)
                act.activation(ws_gu[0][:, j, :, :], w_gu[:, j, :, :], ACT.Copy).then_inc(gu_hi[j], 1)

            def keep_selection(i, rg, r0):
                act.wait_ge(sel_in, 16 * (i + rg + 1))
                if not (isinstance(i, int) and i + r0 == 0):
                    act.wait_ge(sel_used, i + r0)
                act.activation(sel[:, :, :], w_sel[:, :, :], ACT.Copy).then_inc(sel_kept, 1)

            def glu_layer(n, name):
                at0, E, N = ring_at[name], GLU_E[n], GLU_N[n] // 2
                rg = 0 if n == 0 else GLU_N[0] // 2
                if n == 0:
                    act.wait_ge(route_step, 2)
                    act.activation(rt[n][0][:, :, :], rt[n][0][:, :, :], ACT.Exp).then_inc(route_act, 1)
                else:
                    act.wait_ge(logits_ready, 2)
                    act.activation(rt[n][1][:, :, :].rearrange("s b e -> s (b e)"), bank[7][0:S, 0:B * E],
                                   ACT.Sigmoid).then_inc(route_act, 1)

                r0 = rounds_at[name]

                def split_second(i):
                    act.wait_ge(dn_in, 16 * (i + rg + 1))
                    if not (isinstance(i, int) and i + r0 == 0):
                        act.wait_ge(dn_used, i + r0)
                    act.activation(ws_dn[0][:, :, :], w_dn[:, :, 0:D], ACT.Copy).then_inc(dn_hi, 1)

                def body(i, first, more):
                    for h in range(HALVES):
                        ring = Ring(GLU_HALF, at0 + h * len(GLU_HALF), 2 * len(GLU_HALF), i)
                        for j in range(2):
                            act.wait_ge(ring_ready, ring.count(f"g{j}"))
                            act.activation(silu[:, j, :], bank[ring.bank(f"g{j}")][:, 0:HT], ACT.Silu)\
                               .then_inc(bank_free[ring.bank(f"g{j}")], 1)
                            if h == 1 and j == 0:
                                split_second(i)
                                if more:
                                    split_first(i + 1, 0, rg, r0)
                        if first and h == 0:
                            for k in range(2):
                                act.wait_ge(comb_turned, 2 * n + k + 1)
                                act.activation(comb_t[0:E + 1, half(k)], bank[5 + k][0:E + 1, 0:HT], ACT.Copy)\
                                   .then_inc(comb_hi, 1)
                        for j in range(2):
                            if not (first and h == 0 and n == 0):
                                act.wait_ge(hid_made, 4 * (i + rg) + 2 * (h - 1) + j + 1)
                            keep(ring, f"s{j}", share[:, j, :], HT)
                        high_rows(i, h, r0, [(hid_made, 4 * (i + rg) + 2 * h + j + 1) for j in range(2)])
                        if h == 1 and more:
                            keep_selection(i + 1, rg, r0)
                            split_first(i + 1, 1, rg, r0)

                body(0, True, True)
                with act.Fori(1, N - 1) as i:
                    body(i, False, True)
                body(N - 1, False, False)

            def high_rows(i, h, r0, needs):
                for j in range(2):
                    act.wait_ge(*needs[j])
                    act.activation(hids[0][:, h, j, :], hid[:, h, j, :], ACT.Copy).then_inc(hid_hi, 1)

            def plain_attention():
                def keep_part(out, use, rows, width):
                    act.wait_ge(q1_ready, use)
                    act.activation(out, bank[2][0:rows, 0:width], ACT.Copy).then_inc(q1_kept, 1)

                def keep_key(b, side):
                    keep_part(k1[:, side, :, :].rearrange("p c s -> p (c s)"), 3 * b + 1, P, C * S)

                def keep_query(b, side):
                    keep_part(q1[:, side, :, :].rearrange("p c s -> p (c s)"), 3 * b + 2, P, C * S)

                def keep_value(b, side):
                    keep_part(v1[:, side, :], 3 * b + 3, S, D)

                def keep_turned(G, r):
                    act.wait_ge(p1_turned, G + 1)
                    act.activation(pt1[:, r % 2, :], bank[r % 2][0:S, 0:4 * S], ACT.Copy).then_inc(p1_kept, 1)

                def keep_context(b):
                    act.wait_ge(c1_ready, b + 1)
                    act.activation(c1[:, :], bank[3][:, 0:C * S], ACT.Copy).then_inc(c1_kept, 1)

                def batch(b, side, more):
                    first = isinstance(b, int) and b == 0
                    for r in range(4):
                        if more and r == 0:
                            keep_key(b + 1, 1 - side)
                        if more and r == 3:
                            keep_value(b + 1, 1 - side)
                        act.wait_ge(s1_max, 4 * b + r + 1)
                        for c in range(C):
                            ins = act.activation(s1[:, r, c * S:(c + 1) * S], s1[:, r, c * S:(c + 1) * S], ACT.Exp,
                                                 bias=m1[:, r, c:c + 1], scale=1.0, accum_out=z1[:, r, c:c + 1])
                        ins.then_inc(s1_exp, 1)
                        if more and r == 1:
                            keep_query(b + 1, 1 - side)
                        if not (first and r == 0):
                            keep_turned(4 * b + r - 1, (r - 1) % 4)
                        if r == 1 and not first:
                            keep_context(b - 1)

                keep_key(0, 0)
                keep_query(0, 0)
                keep_value(0, 0)
                run_batches(act, batch)
                keep_turned(4 * B - 1, 3)
                keep_context(B - 1)

            def sign_first(i, j):
                act.wait_ge(up_in[j], 16 * (i + 1))
                act.wait_ge(gu_used[j], i + rounds_at["sgn"])
                act.activation(ws_gu[0][:, j, 0:C, :], w_gu[:, j, 0:C, :], ACT.Sign).then_inc(gu_split[j], 1)

            def sign_layer():
                r0, at0, N = rounds_at["sgn"], ring_at["sgn"], SGN_N // 2

                def body(i, more):
                    ring = Ring(SIGN_ROUND, at0, 4, i)
                    act.wait_ge(dn1_in, 16 * (i + 1))
                    act.wait_ge(bank_free[ring.bank("11")], ring.uses_before("11"))
                    act.activation(sup[:, :], w_dn[:, :, D], ACT.Copy).then_inc(sup_kept, 1)
                    act.wait_ge(sup_kept, i + 1)
                    for h in range(HALVES):
                        for j in range(2):
                            act.wait_ge(ring_ready, ring.count(f"{h}{j}"))
                            act.activation(hid[:, h, j, :], bank[ring.bank(f"{h}{j}")][:, 0:HT], ACT.Relu,
                                           scale=sup[:, j:j + 1])\
                               .then_inc(bank_free[ring.bank(f"{h}{j}")], 1)
                            if h == 1 and j == 0:
                                act.wait_ge(dn_used, i + r0)
                                act.activation(ws_dn[0][:, :, :], w_dn[:, :, 0:D], ACT.Sign).then_inc(dn_split, 1)
                                if more:
                                    sign_first(i + 1, 0)
                        high_rows(i, h, r0, [(bank_free[ring.bank(f"{h}{j}")], ring.uses_before(f"{h}{j}") + 1)
                                             for j in range(2)])
                        if h == 1 and more:
                            sign_first(i + 1, 1)

                with act.Fori(0, N - 1) as i:
                    body(i, True)
                body(N - 1, False)

            def nothing():
                pass

            squares(0, lambda: split_query_weights(0))
            latent_attention(0, True)
            squares(1, lambda: first_round(0, "glu0"))
            glu_layer(0, "glu0")
            squares(2, nothing)
            plain_attention()
            squares(3, lambda: (sign_first(0, 0), sign_first(0, 1)))
            sign_layer()
            squares(4, lambda: split_query_weights(HEADS))
            latent_attention(1, False)
            squares(5, nothing)
            squares(6, lambda: split_query_weights(2 * HEADS))
            latent_attention(2, True)
            squares(7, lambda: first_round(1, "glu1"))
            glu_layer(1, "glu1")

        @block.vector
        def _(dve):
            def layer_norm(s):
                layer_input_ready(dve, s)

                def centre(h):
                    dve.wait_ge(ln_mean, HALVES * s + h + 1)
                    for c in range(C):
                        dve.tensor_tensor(xn[:, c, half(h)], x[:, c, half(h)], bank[h][:, 0:HT], ALU.subtract)\
                           .then_inc(ln_centred, 1)

                def add_squares(h):
                    for k, (to, c) in enumerate(((0, 1), (2, 3), (0, 2))):
                        if k < 2:
                            dve.wait_ge(ln_squared, HALVES * C * s + C * h + c + 1)
                        else:
                            dve.wait_ge(ln_summed, 6 * s + 3 * h + k)
                        dve.tensor_tensor(sq[:, to, half(h)], sq[:, to, half(h)], sq[:, c, half(h)], ALU.add)\
                           .then_inc(ln_summed, 1)

                def guard(h):
                    dve.wait_ge(ln_var, HALVES * s + h + 1)
                    bs = slice(h * BH, (h + 1) * BH)
                    dve.tensor_scalar(var[:, bs], bank[2][0:S, bs], EPS, None, ALU.add).then_inc(ln_step[h], 1)

                def deviation(h):
                    n0, done = 6 * s, ln_step[h]
                    bs = slice(h * BH, (h + 1) * BH)
                    dve.wait_ge(ln_pow, HALVES * s + h + 1)
                    dve.tensor_tensor(nwt[:, 1, bs], nwt[:, 0, bs], nwt[:, 0, bs], ALU.mult).then_inc(done, 1)
                    dve.wait_ge(done, n0 + 2)
                    dve.tensor_tensor(nwt[:, 1, bs], nwt[:, 1, bs], var[:, bs], ALU.mult).then_inc(done, 1)
                    dve.wait_ge(done, n0 + 3)
                    dve.tensor_scalar(nwt[:, 2, bs], nwt[:, 1, bs], -0.5, 1.5, ALU.mult, ALU.add).then_inc(done, 1)
                    dve.wait_ge(done, n0 + 4)
                    dve.tensor_tensor(rstd[:, bs], nwt[:, 0, bs], nwt[:, 2, bs], ALU.mult).then_inc(done, 1)
                    dve.wait_ge(done, n0 + 5)
                    dve.tensor_tensor(diag[:, bs, :], ident[0:S, 0:S].unsqueeze(1).broadcast_to([S, BH, S]),
                                      rstd[:, bs].unsqueeze(2).broadcast_to([S, BH, S]), ALU.mult).then_inc(done, 1)

                def scale(h):
                    dve.wait_ge(ln_spread, HALVES * s + h + 1)
                    for c in range(C):
                        dve.tensor_tensor(xn[:, c, half(h)], xn[:, c, half(h)], bank[3 + h][:, 0:HT], ALU.mult)\
                           .then_inc(ln_done, 1)

                def low_part():
                    for c in range(C):
                        dve.wait_ge(x_hi_set, HALVES * C * splits_before[s] + c + 1)
                        dve.tensor_tensor(x_lo[:, c, half(0)], xn[:, c, half(0)], x_hi[:, c, half(0)].bitcast(F32),
                                          ALU.subtract).then_inc(x_split[0], 1)

                centre(0)
                add_squares(0)
                centre(1)
                guard(0)
                add_squares(1)
                deviation(0)
                guard(1)
                scale(0)
                deviation(1)
                if s in splits_before:
                    low_part()
                scale(1)

            def add_to_x(h, c, psum):
                return dve.tensor_tensor(x[:, c, half(h)], x[:, c, half(h)], psum, ALU.add)

            def latent_attention(n, rope):
                def head(ring, slots, p, a, last, more):
                    ga = None if a is None else a + n * HEADS
                    gl = None if last is None else last + n * HEADS

                    def low(name, out, high, width, done, count):
                        k = ring.bank(name)
                        dve.wait_ge(done, count)
                        dve.tensor_tensor(out, bank[k][:, 0:width], high.bitcast(F32), ALU.subtract).then_inc(bank_free[k], 1)

                    def turn_query(name):
                        c, h = "abc".index(name[0]), int(name[1])
                        o = bank[ring.bank(name)]
                        free = bank_free[ring.bank(name)]
                        dve.wait_ge(ring_ready, ring.count(name))

                        def product(out, lo, hi, kind, tlo):
                            t = rope_q[tlo:tlo + hi - lo, kind, c if kind == 0 or c == 2 else 1 - c, :]
                            return dve.tensor_tensor(out.rearrange("p (b s) -> p b s", b=BH),
                                                     o[lo:hi, 0:HT].rearrange("p (b s) -> p b s", b=BH),
                                                     t.unsqueeze(1).broadcast_to([hi - lo, BH, S]), ALU.mult)

                        product(qb[:, c, half(h)], 0, P, 0, 0)
                        before = 6 * (p + ropes_at[n]) + 3 * h
                        if not (isinstance(before, int) and before == 0):
                            dve.wait_ge(rope_added, before)
                        if c < 2:
                            product(turned[:, 1 - c, :], 0, P, 1, 0).then_inc(free, 1)
                        else:
                            product(turned[0:R, 2, :], R, P, 1, 0)
                            product(turned[R:P, 2, :], 0, R, 1, R).then_inc(free, 1)

                    def add_out(name):
                        k, m = ring.bank(name), int(name[1])
                        dve.wait_ge(ring_ready, ring.count(name))
                        add_to_x(m // C, m % C, bank[k][:, 0:HT]).then_inc(bank_free[k], 1)

                    def use(name):
                        if name == "ww" and rope:
                            low("ww", ww[1][:, :, :].rearrange("p c d -> p (c d)"),
                                ww[0][:, :, :].rearrange("p c d -> p (c d)"), QC * DC, ww_hi, p + ropes_at[n] + 1)
                        elif name[0] in "abc":
                            turn_query(name)
                        elif name[0] == "v":
                            k, width = int(name[1]), D // outs_of[n]
                            cols = slice(k * width, (k + 1) * width)
                            low(name, vo[1][:, cols], vo[0][:, cols], width, vo_hi, outs_at[n] + outs_of[n] * a + k + 1)
                        elif name[0] in "ot":
                            add_out(name)

                    def row_max(b):
                        dve.wait_ge(scores_ready, ga * B + b + 1)
                        dve.tensor_reduce(nmax[:, b:b + 1], bank[4 + b % 2][0:S, 0:L], AX_X, ALU.max, negate=True)\
                           .then_inc(max_ready, 1)

                    def normalise(b):
                        G = ga * B + b
                        dve.wait_ge(exp_ready, G + 1)
                        dve.reciprocal(prec[:, b:b + 1], psum_e[:, b:b + 1]).then_inc(rec_ready, 1)
                        dve.wait_ge(rec_ready, G + 1)
                        dve.tensor_scalar(probs[:, b % 2, :], probs[:, b % 2, :], prec[:, b:b + 1], None, ALU.mult)\
                           .then_inc(probs_ready, 1)

                    def low_turned(chunks):
                        for c in chunks:
                            dve.wait_ge(qb_hi, 6 * (p + ropes_at[n]) + 3 + c + 1)
                            dve.tensor_tensor(qbs[1][:, c, half(1)], qb[:, c, half(1)], qbs[0][:, c, half(1)].bitcast(F32),
                                              ALU.subtract).then_inc(qb_split[1], 1)

                    def low_ctx(g, h):
                        dve.wait_ge(ctx_hi, g * HALVES + h + 1)
                        dve.tensor_tensor(ctxs[1][:, half(h)], bank[7][:, 0:HT], ctxs[0][:, half(h)].bitcast(F32),
                                          ALU.subtract).then_inc(ctx_kept, 1)

                    for b, (before, after) in enumerate(slots):
                        if b == 2 and gl is not None:
                            low_ctx(gl, 1)
                        if b == BH + 2 and a is not None:
                            low_ctx(ga, 0)
                        if a is not None:
                            row_max(b)
                        if rope and p is not None and HIGH_AFTER.get(b - 1, (0,))[0] == 1:
                            low_turned(HIGH_AFTER[b - 1][1])
                        for name in before:
                            use(name)
                        if a is not None:
                            normalise(b)
                        for name in after:
                            use(name)
                    if n == 0 and a is None and last is None:
                        context_rest()

                run_latent(dve, table[n], ring_at[f"lat{n}"], head)

            def route(n):
                E = GLU_E[n]
                done = [route_end[0] if n else 0]
                score, v, one1, one2, left = (rt[n][k] for k in range(1, 6))
                first = rt[n][0]
                m, den = rs[n][0], rs[n][1]

                def step(ins):
                    ins.then_inc(route_step, 1)
                    done[0] += 1
                    dve.wait_ge(route_step, done[0])

                def wide(t):
                    return t[:, :].unsqueeze(2).broadcast_to([S, B, E])

                rev = revio[n][:, :].unsqueeze(1).broadcast_to([S, B, E])
                logits = bank[7][0:S, 0:B * E].rearrange("s (b e) -> s b e", b=B)
                if n == 0:
                    dve.wait_ge(logits_ready, 1)
                    step(dve.tensor_reduce(m[:, :], logits, AX_X, ALU.max))
                    step(dve.tensor_tensor(first[:, :, :], logits, wide(m), ALU.subtract))
                    dve.wait_ge(route_act, 1)
                    step(dve.tensor_reduce(den[:, :], first[:, :, :], AX_X, ALU.add))
                    step(dve.reciprocal(rs[n][2][:, :], den[:, :]))
                    step(dve.tensor_tensor(score[:, :, :], first[:, :, :], wide(rs[n][2]), ALU.mult))
                    pick = score
                else:
                    dve.wait_ge(route_act, 2)
                    step(dve.tensor_tensor(first[:, :, :], score[:, :, :],
                                           ebias[:, :].unsqueeze(1).broadcast_to([S, B, E]), ALU.add))
                    pick = first
                for k, hot in enumerate((one1, one2)):
                    step(dve.tensor_reduce(m[:, :], pick[:, :, :], AX_X, ALU.max))
                    step(dve.tensor_tensor(v[:, :, :], pick[:, :, :], wide(m), ALU.is_equal))
                    step(dve.tensor_tensor(v[:, :, :], v[:, :, :], rev, ALU.mult))
                    step(dve.tensor_reduce(den[:, :], v[:, :, :], AX_X, ALU.max))
                    step(dve.tensor_tensor(hot[:, :, :], v[:, :, :], wide(den), ALU.is_equal))
                    if k == 0:
                        step(dve.scalar_tensor_tensor(left[:, :, :], hot[:, :, :], -HUGE, pick[:, :, :], ALU.mult, ALU.add))
                        pick = left
                step(dve.tensor_tensor(one1[:, :, :], one1[:, :, :], one2[:, :, :], ALU.add))
                step(dve.tensor_tensor(one1[:, :, :], one1[:, :, :], score[:, :, :], ALU.mult))
                step(dve.tensor_reduce(m[:, :], one1[:, :, :], AX_X, ALU.add))
                step(dve.tensor_scalar(m[:, :], m[:, :], 1e-20, None, ALU.add))
                step(dve.reciprocal(rs[n][3][:, :], m[:, :]))
                step(dve.tensor_tensor(comb[n][:, :, 0:E], one1[:, :, :], wide(rs[n][3]), ALU.mult))
                return done[0]

            def ternary_scale():
                dve.wait_ge(w2_sum, 1)
                dve.tensor_scalar(w2m[:, 1:2], bank[4][:, 0:1], 1.0 / (D * D), None, ALU.mult).then_inc(w2_step, 1)
                dve.wait_ge(w2_step, 3)
                dve.tensor_scalar(w2m[:, 2:3], w2m[:, 1:2], 1e-10, None, ALU.add).then_inc(w2_step, 1)
                dve.wait_ge(w2_step, 4)
                dve.reciprocal(w2m[:, 3:4], w2m[:, 2:3]).then_inc(w2_step, 1)

            def glu_layer(n, name):
                r0, at0, N, E1 = rounds_at[name], ring_at[name], GLU_N[n] // 2, GLU_E[n] + 1
                dve.tensor_scalar(comb_t[:, :].rearrange("e (a p) -> e a p", p=P),
                                  one[0:2 * LOW, :].unsqueeze(1).broadcast_to([2 * LOW, T // P, P]), 0.0, None, ALU.mult)
                assert route(n) == route_end[n]
                if n == 0:
                    ternary_scale()

                def rows(i, h):
                    ring = Ring(GLU_HALF, at0 + h * len(GLU_HALF), 2 * len(GLU_HALF), i)
                    for j in range(2):
                        k = ring.bank(f"u{j}")
                        dve.wait_ge(ring_ready, ring.count(f"u{j}"))
                        dve.wait_ge(bank_free[ring.bank(f"g{j}")], ring.uses_before(f"g{j}") + 1)
                        dve.tensor_tensor(hid[:, h, j, :], silu[:, j, :], bank[k][:, 0:HT], ALU.mult).then_inc(bank_free[k], 1)

                def body(i, first):
                    rows(i, 0)
                    if first:
                        for k in range(2):
                            dve.wait_ge(comb_hi, 2 * n + k + 1)
                            dve.tensor_tensor(comb_t[LOW:LOW + E1, half(k)], bank[5 + k][0:E1, 0:HT],
                                              comb_t[0:E1, half(k)].bitcast(F32), ALU.subtract).then_inc(comb_kept, 1)
                    if not first:
                        add_down(i - 1, 1, r0)
                    rows(i, 1)
                    add_down(i, 0, r0)

                body(0, True)
                with dve.Fori(1, N) as i:
                    body(i, False)
                add_down(N - 1, 1, r0)

            def add_down(i, h, r0, scale=None):
                for c in range(C):
                    k = C * (2 * (i + r0) + h) + c
                    dve.wait_ge(down_ready, k + 1)
                    if scale is None:
                        ins = add_to_x(h, c, bank[4 + c][:, 0:HT])
                    else:
                        ins = dve.scalar_tensor_tensor(x[:, c, half(h)], bank[4 + c][:, 0:HT], scale[:, c:c + 1],
                                                       x[:, c, half(h)], ALU.mult, ALU.add)
                    ins.then_inc(down_added, 1)

            def plain_attention():
                def add_out(b):
                    dve.wait_ge(o1_ready, b + 1)
                    here = bass.ds(b * S, S)
                    dve.tensor_tensor(x[:, :, here], x[:, :, here],
                                      bank[2][:, 0:C * S].rearrange("p (c s) -> p c s", c=C), ALU.add).then_inc(o1_added, 1)

                def batch(b, side, more):
                    for r in range(4):
                        G = 4 * b + r
                        s4 = s1[:, r, :].rearrange("s (c k) -> s c k", c=4)
                        dve.wait_ge(s1_ready, G + 1)
                        dve.scalar_tensor_tensor(s4, bank[4 + r][0:S, 0:4 * S].rearrange("s (c k) -> s c k", c=4),
                                                 SCALE1, mask[:, :].unsqueeze(1).broadcast_to([S, 4, S]),
                                                 ALU.mult, ALU.add).then_inc(s1_masked, 1)
                        dve.wait_ge(s1_masked, G + 1)
                        dve.tensor_reduce(m1[:, r, :], s4, AX_X, ALU.max, negate=True).then_inc(s1_max, 1)
                        dve.wait_ge(s1_exp, G + 1)
                        dve.reciprocal(z1[:, r, :], z1[:, r, :]).then_inc(s1_rec, 1)
                        if r == 2 and not (isinstance(b, int) and b == 0):
                            add_out(b - 1)

                dve.wait_ge(mask_loaded, 16)
                run_batches(dve, batch)
                add_out(B - 1)

            def ternary():
                dve.wait_ge(w2_step, 5)
                steps = [
                    lambda: dve.tensor_scalar(w2t[:, :, :], w2s[:, :, :], w2m[:, 3:4], MAGIC, ALU.mult, ALU.add),
                    lambda: dve.tensor_scalar(w2t[:, :, :], w2t[:, :, :], -MAGIC, 1.0, ALU.add, ALU.min),
                    lambda: dve.tensor_scalar(w2t[:, :, :], w2t[:, :, :], -1.0, w2m[:, 1:2], ALU.max, ALU.mult),
                    lambda: dve.tensor_tensor(w2t[:, :, :], w2t[:, :, :], w2s[:, :, :], ALU.subtract),
                    lambda: dve.tensor_tensor(w2s[:, :, :], w2s[:, :, :], w2t[:, :, :], ALU.add),
                ]
                for k, step in enumerate(steps):
                    if k:
                        dve.wait_ge(w2_tern, k)
                    step().then_inc(w2_tern, 1)

            def sign_layer():
                r0, N = rounds_at["sgn"], SGN_N // 2
                dve.wait_ge(scales_loaded, 32)
                dve.tensor_scalar(sdo[:, :], sdn[:, :], s_out[:, 0:1], None, ALU.mult).then_inc(sdo_ready, 1)
                dve.wait_ge(sdo_ready, 1)
                ternary()
                add_down(0, 0, r0, sdo)
                with dve.Fori(1, N) as i:
                    add_down(i - 1, 1, r0, sdo)
                    add_down(i, 0, r0, sdo)
                add_down(N - 1, 1, r0, sdo)

            def ternary_layer():
                for h in range(HALVES):
                    for m in range(C):
                        dve.wait_ge(t2_ready, h * C + m + 1)
                        dve.scalar_tensor_tensor(x[:, m, half(h)], bank[h * C + m][:, 0:HT], w2b[:, m:m + 1],
                                                 x[:, m, half(h)], ALU.add, ALU.add).then_inc(t2_added, 1)

            dve.memset(ones[:, :], 1.0 / D).then_inc(consts_set, 1)
            dve.memset(one[:, :], 1.0).then_inc(consts_set, 1)
            dve.memset(comb[0][:, :, :], 1.0)
            dve.memset(comb[1][:, :, :], 1.0)
            dve.wait_ge(consts_loaded, 32)
            layer_norm(0)
            dve.wait_ge(ctx_loaded, 96)
            dve.wait_ge(rope_t_step, 1)
            dve.tensor_tensor(kv_t[:, :, 0:L], kv_t[:, :, 0:L],
                              rope_t[:, 0, :].unsqueeze(1).broadcast_to([P, B, L]), ALU.mult).then_inc(rope_k_step, 1)
            dve.wait_ge(rope_k_step, 1)
            dve.wait_ge(rope_t_step, 2)
            dve.tensor_tensor(kv_t[:, :, 0:L], kv_t[:, :, 0:L], rot_t[:, :, :], ALU.add).then_inc(rope_k_step, 1)
            dve.wait_ge(rope_k_step, 2)

            def context_rest():
                dve.wait_ge(kv_hi, 1)
                dve.tensor_tensor(kvs[1][:, :, :], kv_t[:, :, :], kvs[0][:, :, :].bitcast(F32), ALU.subtract)\
                   .then_inc(kv_split, 1)
                H2 = DC // 2
                for b in range(B):
                    dve.tensor_tensor(rot_r[:, b, :, 0:H2], kv_r[:, b, :, H2:DC], rope_r[:, 1, :, 0:H2], ALU.mult)
                    dve.tensor_tensor(rot_r[:, b, :, H2:DC], kv_r[:, b, :, 0:H2], rope_r[:, 1, :, H2:DC], ALU.mult)\
                       .then_inc(rope_r_step, 1)
                dve.wait_ge(rope_r_step, B)
                dve.tensor_tensor(kv_r[:, :, :, :], kv_r[:, :, :, :],
                                  rope_r[:, 0, :, :].unsqueeze(1).broadcast_to([KP, B, KC, DC]), ALU.mult)\
                   .then_inc(rope_r_step, 1)
                dve.wait_ge(rope_r_step, B + 1)
                dve.tensor_tensor(kv_r[:, :, :, :], kv_r[:, :, :, :], rot_r[:, :, :, :], ALU.add).then_inc(rope_r_step, 1)

            def ternary_sum():
                dve.wait_ge(w2_loaded, 16)
                dve.tensor_reduce(w2p[:, :], w2s[:, :, :].rearrange("p c (a d) -> p (c a) d", a=8), AX_X, ALU.add,
                                  apply_absolute_value=True).then_inc(w2_step, 1)
                dve.wait_ge(w2_step, 1)
                dve.tensor_reduce(w2m[:, 0:1], w2p[:, :], AX_X, ALU.add).then_inc(w2_step, 1)

            latent_attention(0, True)
            layer_norm(1)
            ternary_sum()
            glu_layer(0, "glu0")
            layer_norm(2)
            plain_attention()
            layer_norm(3)
            sign_layer()
            layer_norm(4)
            latent_attention(1, False)
            layer_norm(5)
            ternary_layer()
            layer_norm(6)
            latent_attention(2, True)
            layer_norm(7)
            glu_layer(1, "glu1")

        @block.gpsimd
        def _(gp):
            def power(s):
                for h in range(HALVES):
                    bs = slice(h * BH, (h + 1) * BH)
                    gp.wait_ge(ln_step[h], 6 * s + 1)
                    gp.tensor_tensor(nwt[:, 0, bs], var[:, bs], half_pow[:, bs], ALU.pow).then_inc(ln_pow, 1)

            def low_x(s):
                for c in range(C):
                    gp.wait_ge(x_hi_set, HALVES * C * splits_before[s] + C + c + 1)
                    gp.tensor_tensor(x_lo[:, c, half(1)], xn[:, c, half(1)], x_hi[:, c, half(1)].bitcast(F32),
                                     ALU.subtract).then_inc(x_split[1], 1)

            def low_query_weights(g):
                gp.wait_ge(q_hi, g + 1)
                gp.tensor_tensor(ws_q[1][:, :, :], w_q[:, :, :], ws_q[0][:, :, :].bitcast(F32), ALU.subtract)\
                  .then_inc(q_split, 1)

            def latent_attention(n, rope):
                def head(ring, slots, p, a, last, more):
                    def add_turned(h, name, chunks):
                        k = ring.bank(f"{name}{h}")
                        gp.wait_ge(bank_free[k], ring.uses_before(f"{name}{h}") + 1)
                        for c in chunks:
                            gp.tensor_tensor(qb[:, c, half(h)], qb[:, c, half(h)], turned[:, c, :], ALU.add)\
                              .then_inc(rope_added, 1)

                    def low_turned(h, chunks):
                        for c in chunks:
                            gp.wait_ge(qb_hi, 6 * (p + ropes_at[n]) + 3 * h + c + 1)
                            gp.tensor_tensor(qbs[1][:, c, half(h)], qb[:, c, half(h)], qbs[0][:, c, half(h)].bitcast(F32),
                                             ALU.subtract).then_inc(qb_split[h], 1)

                    def low_query(h):
                        gp.wait_ge(qp_hi, 2 * (p + n * HEADS) + h + 1)
                        gp.tensor_tensor(qps[1][:, half(h)], qp[:, half(h)], qps[0][:, half(h)].bitcast(F32),
                                         ALU.subtract).then_inc(qp_lo, 1)

                    if p is None:
                        return
                    if rope:
                        for h in range(HALVES):
                            gp.wait_ge(bank_free[ring.bank(f"a{h}")], ring.uses_before(f"a{h}") + 1)
                            add_turned(h, "b", (0, 1))
                            add_turned(h, "c", (2,))
                            if h == 0:
                                low_turned(h, (0, 1, 2))
                    if more:
                        low_query_weights(p + n * HEADS + 1)
                    low_query(0)
                    low_query(1)

                run_latent(gp, table[n], ring_at[f"lat{n}"], head)

            def low_first(j, i, rg):
                gp.wait_ge(gu_hi[j], i + rg + 1)
                gp.tensor_tensor(ws_gu[1][:, j, :, :], w_gu[:, j, :, :], ws_gu[0][:, j, :, :].bitcast(F32), ALU.subtract)\
                  .then_inc(gu_split[j], 1)

            def low_rows(i, h, r0):
                for j in range(2):
                    gp.wait_ge(hid_hi, 4 * (i + r0) + 2 * h + j + 1)
                    gp.tensor_tensor(hids[1][:, h, j, :], hid[:, h, j, :], hids[0][:, h, j, :].bitcast(F32),
                                     ALU.subtract).then_inc(hid_ready, 1)

            def glu_layer(n, name):
                at0, N, r0 = ring_at[name], GLU_N[n] // 2, rounds_at[name]
                rg = 0 if n == 0 else GLU_N[0] // 2

                def body(i, more):
                    for h in range(HALVES):
                        ring = Ring(GLU_HALF, at0 + h * len(GLU_HALF), 2 * len(GLU_HALF), i)
                        if h == 1:
                            gp.wait_ge(dn_hi, i + rg + 1)
                            gp.tensor_tensor(ws_dn[1][:, :, :], w_dn[:, :, 0:D], ws_dn[0][:, :, :].bitcast(F32),
                                             ALU.subtract).then_inc(dn_split, 1)
                            if more:
                                low_first(0, i + 1, rg)
                        for j in range(2):
                            for kind in "us":
                                gp.wait_ge(bank_free[ring.bank(f"{kind}{j}")], ring.uses_before(f"{kind}{j}") + 1)
                            gp.tensor_tensor(hid[:, h, j, :], hid[:, h, j, :], share[:, j, :], ALU.mult).then_inc(hid_made, 1)
                        low_rows(i, h, r0)
                    if more:
                        low_first(1, i + 1, rg)

                with gp.Fori(0, N - 1) as i:
                    body(i, True)
                body(N - 1, False)

            def sign_layer():
                with gp.Fori(0, SGN_N // 2) as i:
                    for h in range(HALVES):
                        low_rows(i, h, rounds_at["sgn"])

            def plain_attention():
                def raw_batch(b):
                    gp.tensor_copy(raw_b[:, :], raw_s[:, bass.ds(b, 1), :].rearrange("p a s -> p (a s)")).then_inc(raw_b_ready, 1)

                def batch(b, side, more):
                    for r in range(4):
                        s4 = s1[:, r, :].rearrange("s (c k) -> s c k", c=4)
                        gp.wait_ge(s1_rec, 4 * b + r + 1)
                        gp.tensor_tensor(s4, s4, z1[:, r, :].unsqueeze(2).broadcast_to([S, 4, S]), ALU.mult)\
                          .then_inc(s1_norm, 1)
                        if r == 0 and more:
                            gp.wait_ge(q1_kept, 3 * b + 3)
                            raw_batch(b + 1)

                gp.wait_ge(w1_loaded, 16 * N_W1)
                raw_batch(0)
                run_batches(gp, batch)

            gp.memset(half_pow[:, :], -0.5).then_inc(gp_set, 1)
            for n, e in enumerate(GLU_E):
                gp.iota(revio_i[n][:, :], pattern=[[-1, e]], base=e, channel_multiplier=0).then_inc(gp_set, 1)
            gp.wait_ge(gp_set, 3)
            for n in range(2):
                gp.tensor_copy(revio[n][:, :], revio_i[n][:, :]).then_inc(gp_set, 1)
            gp.memset(kv_t[:, :, L:LE], 0.0).then_inc(rope_t_step, 1)
            power(0)
            low_query_weights(0)
            gp.wait_ge(ctx_loaded, 96)
            gp.tensor_tensor(rot_t[:, :, :], rot_t[:, :, :], rope_t[:, 1, :].unsqueeze(1).broadcast_to([P, B, L]), ALU.mult)\
              .then_inc(rope_t_step, 1)
            low_x(0)
            latent_attention(0, True)
            power(1)
            for j in range(2):
                low_first(j, 0, 0)
            low_x(1)
            glu_layer(0, "glu0")
            power(2)
            plain_attention()
            power(3)
            low_x(3)
            sign_layer()
            power(4)
            low_query_weights(HEADS)
            low_x(4)
            latent_attention(1, False)
            power(5)
            power(6)
            low_query_weights(2 * HEADS)
            low_x(6)
            latent_attention(2, True)
            power(7)
            for j in range(2):
                low_first(j, 0, GLU_N[0] // 2)
            low_x(7)
            glu_layer(1, "glu1")


def kernel(**inputs):
    import numpy as np
    import concourse.bacc as bacc
    from concourse import mybir as mb
    from concourse.bass_utils import run_bass_kernel_spmd as run

    nc = bacc.Bacc("TRN2", target_bir_lowering=False, num_devices=1)
    arrays = {}

    def arg(name, a):
        a = np.ascontiguousarray(a)
        arrays["in_" + name] = a
        return nc.dram_tensor("in_" + name, a.shape, mb.dt.from_np(a.dtype), kind="ExternalInput").ap()

    a = {k: np.asarray(v) for k, v in inputs.items()}

    def rope_tables(length, dim):
        inv = (np.float32(1.0) / np.float32(10000.0) ** (np.arange(0, dim, 2, dtype=np.float32) / np.float32(dim))).astype(np.float32)
        f = np.arange(length, dtype=np.float32)[:, None] * inv[None, :]
        return np.repeat(np.sin(f), 2, axis=-1).astype(np.float32), np.repeat(np.cos(f), 2, axis=-1).astype(np.float32)

    def query_order(w):
        return np.concatenate([w[..., 0:128], w[..., 192:320], w[..., 128:192], w[..., 320:384]], axis=-1)

    sin, cos = rope_tables(S, 384)
    turn = np.concatenate([-sin[:, :192], sin[:, 192:]], axis=1)
    tq = np.stack([query_order(cos), query_order(turn)])
    tabs_q = tq.reshape(2, S, 3, 128).transpose(3, 0, 2, 1)
    sin, cos = rope_tables(L, DC)
    turn = np.concatenate([-sin[:, :64], sin[:, 64:]], axis=1)
    tk = np.stack([cos, turn])
    tabs_k = tk.transpose(2, 0, 1)
    tabs_r = tk.reshape(2, KC, KP, DC).transpose(2, 0, 1, 3)
    mask = np.where(np.tril(np.ones((S, S), bool)), np.float32(0), np.float32(MASKED)).astype(np.float32)

    latent = []
    for n, name in enumerate(("L0", "L2", "L3")):
        w = {k: a[f"{name}_xattn_{k}"] for k in ("Wq", "w_kc_q", "w_kc_kv", "W_qr", "W_kr", "Wo")}
        q_rank = w["W_qr"].transpose(0, 2, 1)
        kc = w["w_kc_q"]
        if name != "L2":
            q_rank, kc = query_order(q_rank), query_order(kc)
            kc = kc.reshape(HEADS, P, QC, P)
        else:
            kc = kc.reshape(HEADS, P, QC, P).transpose(0, 3, 2, 1)
        latent.append({
            "qk": arg(f"{name}_qk", np.concatenate([q_rank, w["W_kr"].transpose(0, 2, 1)], axis=2)),
            "q": arg(f"{name}_q", w["Wq"].reshape(HEADS, P, C, P).transpose(0, 3, 2, 1)),
            "kc": arg(f"{name}_kc", kc),
            "vo": arg(f"{name}_vo", np.concatenate([w["w_kc_kv"], w["Wo"].reshape(D, HEADS, P).transpose(1, 2, 0)], axis=2)),
        })

    def pad(w):
        rows = -w.shape[0] % (2 * P)
        return np.concatenate([w, np.zeros((rows, w.shape[1]), np.float32)], axis=0) if rows else w

    def hidden_first(w):
        return pad(w).reshape(-1, P, C, P).transpose(0, 3, 2, 1)

    def hidden_second(w):
        return pad(w).reshape(-1, 2, P, D).transpose(0, 2, 1, 3)

    def selection(E, F, total):
        n = -(-total // (2 * P)) * 2 * P
        sel = np.zeros((n, 2 * LOW), np.float32)
        owner = np.minimum(np.arange(total) // F, E)
        sel[np.arange(total), owner] = 1.0
        sel[np.arange(total), LOW + owner] = 1.0
        return sel.reshape(-1, 2, P, 2 * LOW).transpose(0, 3, 1, 2)

    def gated(name, wg, wu, wd, E, F):
        gu = np.concatenate([hidden_first(wg), hidden_first(wu)], axis=2)
        return arg(f"{name}_gu", gu), arg(f"{name}_dn", hidden_second(wd)), arg(f"{name}_sel", selection(E, F, wg.shape[0]))

    E0, F0 = a["L0_ffn_w_gate"].shape[:2]
    g0 = gated("L0", np.concatenate([a["L0_ffn_w_gate"].reshape(-1, D), a["L0_ffn_sw_gate"]]),
               np.concatenate([a["L0_ffn_w_up"].reshape(-1, D), a["L0_ffn_sw_up"]]),
               np.concatenate([a["L0_ffn_w_down"].transpose(0, 2, 1).reshape(-1, D), a["L0_ffn_sw_down"].T]), E0, F0)
    eg = a["L3_ffn_experts_gate_up"]
    E3, F3 = eg.shape[0], eg.shape[2] // 2
    g3 = gated("L3", np.concatenate([eg[:, :, :F3].transpose(0, 2, 1).reshape(-1, D), a["L3_ffn_shared_gate_w"].T]),
               np.concatenate([eg[:, :, F3:].transpose(0, 2, 1).reshape(-1, D), a["L3_ffn_shared_up_w"].T]),
               np.concatenate([a["L3_ffn_experts_down"].reshape(-1, D), a["L3_ffn_shared_down_w"]]), E3, F3)

    def in_first(w):
        return w.reshape(w.shape[0], C, P).transpose(2, 1, 0)

    ctx = a["ctx_512"]
    out = nc.dram_tensor("out_x", (P, C, T), mb.dt.float32, kind="ExternalOutput").ap()
    build(nc,
          arg("x", a["x"].reshape(T, C, P).transpose(2, 1, 0)),
          arg("ctx_t", ctx.transpose(2, 0, 1)),
          arg("ctx_r", ctx.reshape(B, KC, KP, DC).transpose(2, 0, 1, 3)),
          arg("tabs_q", tabs_q), arg("tabs_k", tabs_k), arg("tabs_r", tabs_r),
          arg("mask", mask), arg("ident", np.eye(P, dtype=np.float32)),
          latent,
          [arg("gate0", in_first(a["L0_ffn_gate_weight"])), arg("gate3", in_first(a["L3_ffn_gate_w"].T))],
          arg("bias3", a["L3_ffn_expert_bias"]),
          [g0[0], g3[0]], [g0[1], g3[1]], [g0[2], g3[2]],
          arg("w1q", in_first(a["L1_xattn_Wq"])), arg("w1kv", a["L1_xattn_Wkv_expand"].T),
          arg("w1o", in_first(a["L1_xattn_Wout"])),
          arg("up1", hidden_first(a["L1_ffn_up_weight"])), arg("dn1", np.concatenate(
              [hidden_second(a["L1_ffn_down_weight"].T),
               a["L1_ffn_up_scale"].reshape(-1, 2, P).transpose(0, 2, 1)[..., None]], axis=3)),
          arg("dn1s", a["L1_ffn_down_scale"].reshape(C, P).T),
          arg("out1s", a["L1_ffn_output_scale"]),
          arg("w2", in_first(a["L2_ffn_weight"])), arg("b2", a["L2_ffn_bias"].reshape(C, P).T),
          out)
    r = run(nc, [arrays], core_ids=[0])
    return r.results[0]["out_x"].transpose(2, 1, 0).reshape(B, S, D)
```
